# Optimizing a Trainium2 kernel written in Bass

```python
import numpy as np
import jax
import jax.numpy as jnp

def _softmax(x, axis=-1):
    return jax.nn.softmax(x, axis=axis)

def _gelu(x):
    return jax.nn.gelu(x, approximate=True)

def _silu(x):
    return jax.nn.silu(x)

def _sigmoid(x):
    return jax.nn.sigmoid(x)

def _layernorm(x, axis=-1, eps=1e-05):
    m = jnp.mean(x, axis=axis, keepdims=True)
    v = jnp.var(x, axis=axis, keepdims=True)
    return (x - m) / jnp.sqrt(v + eps)

def _scatter_add(tgt, idx, src, axis=0):
    return tgt.at[idx].add(src)

def _segment_sum(src, seg, n):
    return jax.ops.segment_sum(src, seg, n)
kernel_name = 'mk_lm_tower_d1_tok_ids768_r4_f2f275'

def setup_inputs(seed: int=0):
    np.random.seed(seed)
    _w = jnp.asarray

    def _rec_inputs():
        import jax
        import jax.numpy as jnp
        _rk = jax.random.key(seed)
        x = jax.random.randint(jax.random.fold_in(_rk, 1), (16, 512), 0, 8000, jnp.int32)
        return x
    x = _rec_inputs()

    def _L0_tok_setup():
        import jax, jax.numpy as jnp
        import numpy as np
        N_QUBITS = 6
        N_LAYERS = 3
        DIM = 1 << N_QUBITS
        VOCAB = 8000
        EMBED = 192
        B, S = (16, 1024)

        def _cnot_perm(control, target):
            idx = np.arange(DIM)
            cbit = idx >> N_QUBITS - 1 - control & 1
            flipped = idx ^ 1 << N_QUBITS - 1 - target
            return np.where(cbit == 1, flipped, idx)
        _idx = np.arange(DIM)
        Z_SIGNS = np.stack([1.0 - 2.0 * (_idx >> N_QUBITS - 1 - q & 1) for q in range(N_QUBITS)], axis=1).astype(np.float32)

        def _apply_ry(state, theta, q):
            T = state.shape[0]
            left, right = (1 << q, 1 << N_QUBITS - 1 - q)
            s = state.reshape(T, left, 2, right)
            c = jnp.cos(theta * 0.5)[:, None, None]
            sn = jnp.sin(theta * 0.5)[:, None, None]
            a0, a1 = (s[:, :, 0, :], s[:, :, 1, :])
            out = jnp.stack([c * a0 - sn * a1, sn * a0 + c * a1], axis=2)
            return out.reshape(T, DIM)

        def _apply_rz(state, theta, q):
            T = state.shape[0]
            left, right = (1 << q, 1 << N_QUBITS - 1 - q)
            s = state.reshape(T, left, 2, right)
            ph = jnp.exp(1j * (theta * 0.5)).astype(state.dtype)[:, None, None]
            out = jnp.stack([jnp.conj(ph) * s[:, :, 0, :], ph * s[:, :, 1, :]], axis=2)
            return out.reshape(T, DIM)

        def _circuit_expvals(params):
            T = params.shape[0]
            state = jnp.zeros((T, DIM), dtype=jnp.complex64).at[:, 0].set(1.0)
            for layer in range(N_LAYERS):
                for q in range(N_QUBITS):
                    state = _apply_ry(state, params[:, layer, q, 0], q)
                    state = _apply_rz(state, params[:, layer, q, 1], q)
                if layer < N_LAYERS - 1:
                    for q in range(N_QUBITS - 1):
                        state = state[:, _cnot_perm(q, q + 1)]
                    if N_QUBITS > 2:
                        state = state[:, _cnot_perm(N_QUBITS - 1, 0)]
            probs = state.real ** 2 + state.imag ** 2
            return probs @ jnp.asarray(Z_SIGNS)
        key = jax.random.key(seed)
        k1, k2, k3, k4 = jax.random.split(key, 4)
        token_ids = jax.random.randint(k1, (B, S), 0, VOCAB)
        quantum_params = jax.random.normal(k2, (VOCAB, N_LAYERS, N_QUBITS, 2), dtype=jnp.float32) * 0.1
        post_w = jax.random.normal(k3, (EMBED, N_QUBITS), dtype=jnp.float32) / np.sqrt(N_QUBITS)
        post_b = jax.random.normal(k4, (EMBED,), dtype=jnp.float32) * 0.01
        return {'token_ids': token_ids, 'quantum_params': quantum_params, 'post_w': post_w, 'post_b': post_b}
    _L0_tok_all = _L0_tok_setup()
    _L0_tok_in = {k: v for k, v in _L0_tok_all.items() if k in ('quantum_params', 'post_w', 'post_b')}
    del _L0_tok_all

    def _L0_attn_setup():
        import math
        import jax, jax.numpy as jnp
        import numpy as np
        B, S, IN_DIM, EMB, H, MAX_LEN = (4, 128, 192, 192, 12, 128)
        D = EMB // H
        key = jax.random.key(seed)
        ks = jax.random.split(key, 16)

        def lin(k, fan_in, fan_out):
            lim = math.sqrt(6.0 / (fan_in + fan_out))
            W = jax.random.uniform(k, (fan_in, fan_out), minval=-lim, maxval=lim, dtype=jnp.float32)
            return (W, jnp.zeros((fan_out,), jnp.float32))
        Wq, bq = lin(ks[0], IN_DIM, EMB)
        Wk, bk = lin(ks[1], IN_DIM, EMB)
        Wv, bv = lin(ks[2], IN_DIM, EMB)
        Wpk, bpk = lin(ks[3], IN_DIM, EMB)
        Wpq, bpq = lin(ks[4], IN_DIM, EMB)
        Wo, bo = lin(ks[5], EMB, IN_DIM)
        rel_table = jax.random.normal(ks[6], (2 * MAX_LEN - 1, IN_DIM), jnp.float32)
        x = jax.random.normal(ks[7], (B, S, IN_DIM), jnp.float32)
        return {'x': x, 'Wq': Wq, 'bq': bq, 'Wk': Wk, 'bk': bk, 'Wv': Wv, 'bv': bv, 'rel_table': rel_table, 'Wpk': Wpk, 'bpk': bpk, 'Wpq': Wpq, 'bpq': bpq, 'Wo': Wo, 'bo': bo}
    _L0_attn_all = _L0_attn_setup()
    _L0_attn_in = {k: v for k, v in _L0_attn_all.items() if k in ('Wq', 'bq', 'Wk', 'bk', 'Wv', 'bv', 'rel_table', 'Wpk', 'bpk', 'Wpq', 'bpq', 'Wo', 'bo')}
    del _L0_attn_all

    def _L0_ffn_setup():
        import jax, jax.numpy as jnp
        import numpy as np
        EPS = 1e-06

        def l2_normalize(x, axis):
            norm = jnp.sqrt(jnp.square(x).sum(axis=axis, keepdims=True))
            return x * (1.0 / (norm + EPS))
        key = jax.random.key(seed)
        ks = jax.random.split(key, 8)
        b, m, d = (32, 256, 192)
        n, p = (8, 4)
        h = d // 8
        X = jax.random.normal(ks[0], (b, m, d), dtype=jnp.float32)
        std_slot = float(np.sqrt(2.0 / (d + n * p)))
        slot_params = jax.random.normal(ks[1], (d, n, p), dtype=jnp.float32) * std_slot
        scale = jnp.ones((), dtype=jnp.float32)
        W_down = jax.random.normal(ks[2], (n, d, h), dtype=jnp.float32) * float(np.sqrt(1.0 / d))
        b_down = jnp.zeros((n, h), dtype=jnp.float32)
        W_up = jax.random.normal(ks[3], (n, h, d), dtype=jnp.float32) * float(np.sqrt(1.0 / h))
        b_up = jnp.zeros((n, d), dtype=jnp.float32)
        return {'X': X, 'slot_params': slot_params, 'scale': scale, 'W_down': W_down, 'b_down': b_down, 'W_up': W_up, 'b_up': b_up}
    _L0_ffn_all = _L0_ffn_setup()
    _L0_ffn_in = {k: v for k, v in _L0_ffn_all.items() if k in ('slot_params', 'scale', 'W_down', 'b_down', 'W_up', 'b_up')}
    del _L0_ffn_all
    return {'x': x, 'L0_tok_quantum_params': _L0_tok_in['quantum_params'], 'L0_tok_post_w': _L0_tok_in['post_w'], 'L0_tok_post_b': _L0_tok_in['post_b'], 'L0_attn_Wq': _L0_attn_in['Wq'], 'L0_attn_bq': _L0_attn_in['bq'], 'L0_attn_Wk': _L0_attn_in['Wk'], 'L0_attn_bk': _L0_attn_in['bk'], 'L0_attn_Wv': _L0_attn_in['Wv'], 'L0_attn_bv': _L0_attn_in['bv'], 'L0_attn_rel_table': _L0_attn_in['rel_table'], 'L0_attn_Wpk': _L0_attn_in['Wpk'], 'L0_attn_bpk': _L0_attn_in['bpk'], 'L0_attn_Wpq': _L0_attn_in['Wpq'], 'L0_attn_bpq': _L0_attn_in['bpq'], 'L0_attn_Wo': _L0_attn_in['Wo'], 'L0_attn_bo': _L0_attn_in['bo'], 'L0_ffn_slot_params': _L0_ffn_in['slot_params'], 'L0_ffn_scale': _L0_ffn_in['scale'], 'L0_ffn_W_down': _L0_ffn_in['W_down'], 'L0_ffn_b_down': _L0_ffn_in['b_down'], 'L0_ffn_W_up': _L0_ffn_in['W_up'], 'L0_ffn_b_up': _L0_ffn_in['b_up']}

def reference(x, L0_tok_quantum_params, L0_tok_post_w, L0_tok_post_b, L0_attn_Wq, L0_attn_bq, L0_attn_Wk, L0_attn_bk, L0_attn_Wv, L0_attn_bv, L0_attn_rel_table, L0_attn_Wpk, L0_attn_bpk, L0_attn_Wpq, L0_attn_bpq, L0_attn_Wo, L0_attn_bo, L0_ffn_slot_params, L0_ffn_scale, L0_ffn_W_down, L0_ffn_b_down, L0_ffn_W_up, L0_ffn_b_up):
    import jax
    import jax.numpy as jnp

    def _L0_tok_ref(token_ids, quantum_params, post_w, post_b):
        import jax, jax.numpy as jnp
        import numpy as np
        N_QUBITS = 6
        N_LAYERS = 3
        DIM = 1 << N_QUBITS
        VOCAB = 8000
        EMBED = 192
        B, S = (16, 1024)

        def _cnot_perm(control, target):
            idx = np.arange(DIM)
            cbit = idx >> N_QUBITS - 1 - control & 1
            flipped = idx ^ 1 << N_QUBITS - 1 - target
            return np.where(cbit == 1, flipped, idx)
        _idx = np.arange(DIM)
        Z_SIGNS = np.stack([1.0 - 2.0 * (_idx >> N_QUBITS - 1 - q & 1) for q in range(N_QUBITS)], axis=1).astype(np.float32)

        def _apply_ry(state, theta, q):
            T = state.shape[0]
            left, right = (1 << q, 1 << N_QUBITS - 1 - q)
            s = state.reshape(T, left, 2, right)
            c = jnp.cos(theta * 0.5)[:, None, None]
            sn = jnp.sin(theta * 0.5)[:, None, None]
            a0, a1 = (s[:, :, 0, :], s[:, :, 1, :])
            out = jnp.stack([c * a0 - sn * a1, sn * a0 + c * a1], axis=2)
            return out.reshape(T, DIM)

        def _apply_rz(state, theta, q):
            T = state.shape[0]
            left, right = (1 << q, 1 << N_QUBITS - 1 - q)
            s = state.reshape(T, left, 2, right)
            ph = jnp.exp(1j * (theta * 0.5)).astype(state.dtype)[:, None, None]
            out = jnp.stack([jnp.conj(ph) * s[:, :, 0, :], ph * s[:, :, 1, :]], axis=2)
            return out.reshape(T, DIM)

        def _circuit_expvals(params):
            T = params.shape[0]
            state = jnp.zeros((T, DIM), dtype=jnp.complex64).at[:, 0].set(1.0)
            for layer in range(N_LAYERS):
                for q in range(N_QUBITS):
                    state = _apply_ry(state, params[:, layer, q, 0], q)
                    state = _apply_rz(state, params[:, layer, q, 1], q)
                if layer < N_LAYERS - 1:
                    for q in range(N_QUBITS - 1):
                        state = state[:, _cnot_perm(q, q + 1)]
                    if N_QUBITS > 2:
                        state = state[:, _cnot_perm(N_QUBITS - 1, 0)]
            probs = state.real ** 2 + state.imag ** 2
            return probs @ jnp.asarray(Z_SIGNS)
        b, s = token_ids.shape
        params = quantum_params[token_ids.reshape(-1)]
        ev = _circuit_expvals(params)
        emb = ev @ post_w.T + post_b
        return emb.reshape(b, s, -1)

    def _L0_attn_ref(x, Wq, bq, Wk, bk, Wv, bv, rel_table, Wpk, bpk, Wpq, bpq, Wo, bo):
        import math
        import jax, jax.numpy as jnp
        import numpy as np
        B, S, IN_DIM, EMB, H, MAX_LEN = (4, 128, 192, 192, 12, 128)
        D = EMB // H
        Bx, Sx, _ = x.shape

        def shape_heads(t):
            return t.reshape(Bx, Sx, H, D).transpose(0, 2, 1, 3)
        q = shape_heads(x @ Wq + bq)
        k = shape_heads(x @ Wk + bk)
        v = shape_heads(x @ Wv + bv)
        pos = jnp.arange(Sx)
        ids = jnp.clip(pos[:, None] - pos[None, :], -(MAX_LEN - 1), MAX_LEN - 1) + (MAX_LEN - 1)
        pos_k = (rel_table @ Wpk + bpk)[ids].reshape(Sx, Sx, H, D)
        pos_q = (rel_table @ Wpq + bpq)[ids].reshape(Sx, Sx, H, D)
        scores = jnp.einsum('bhid,bhjd->bhij', q, k)
        scores = scores + jnp.einsum('bhid,ijhd->bhij', q, pos_k)
        scores = scores + jnp.einsum('ijhd,bhjd->bhij', pos_q, k)
        scores = scores / math.sqrt(D * 3.0)
        attn = jax.nn.softmax(scores, axis=-1)
        out = jnp.einsum('bhij,bhjd->bhid', attn, v)
        out = out.transpose(0, 2, 1, 3).reshape(Bx, Sx, EMB)
        return out @ Wo + bo

    def _L0_ffn_ref(X, slot_params, scale, W_down, b_down, W_up, b_up):
        import jax, jax.numpy as jnp
        import numpy as np
        EPS = 1e-06

        def l2_normalize(x, axis):
            norm = jnp.sqrt(jnp.square(x).sum(axis=axis, keepdims=True))
            return x * (1.0 / (norm + EPS))
        b, m, d = X.shape
        _, n, p = slot_params.shape
        Xn = l2_normalize(X, axis=-1)
        sp = l2_normalize(slot_params, axis=1) * scale
        logits = jnp.einsum('bmd,dnp->bmnp', Xn, sp)
        D = jax.nn.softmax(logits, axis=1)
        C = jax.nn.softmax(logits.reshape(b, m, n * p), axis=2).reshape(b, m, n, p)
        X_tilde = jnp.einsum('bmd,bmnp->bnpd', Xn, D)
        H = jax.nn.gelu(jnp.einsum('bnpd,ndh->bnph', X_tilde, W_down) + b_down[None, :, None, :], approximate=False)
        Y_tilde = jnp.einsum('bnph,nhd->bnpd', H, W_up) + b_up[None, :, None, :]
        Y = jnp.einsum('bnpd,bmnp->bmd', Y_tilde, C)
        return Y
    h = _L0_tok_ref(x, L0_tok_quantum_params, L0_tok_post_w, L0_tok_post_b)
    h = h + _L0_attn_ref(_layernorm(h, axis=-1), L0_attn_Wq, L0_attn_bq, L0_attn_Wk, L0_attn_bk, L0_attn_Wv, L0_attn_bv, L0_attn_rel_table, L0_attn_Wpk, L0_attn_bpk, L0_attn_Wpq, L0_attn_bpq, L0_attn_Wo, L0_attn_bo)
    h = h + _L0_ffn_ref(_layernorm(h, axis=-1), L0_ffn_slot_params, L0_ffn_scale, L0_ffn_W_down, L0_ffn_b_down, L0_ffn_W_up, L0_ffn_b_up)
    return h

_drawn_inputs = setup_inputs


def setup_inputs(seed=0):
    import zlib

    import numpy as np

    out = dict(_drawn_inputs(seed))
    spreads = {'L0_attn_bq': (0.0, 0.8),
     'L0_attn_bk': (0.0, 0.8),
     'L0_attn_bv': (0.0, 0.1),
     'L0_attn_bpk': (0.0, 0.8),
     'L0_attn_bpq': (0.0, 0.8),
     'L0_attn_bo': (0.0, 0.1),
     'L0_ffn_b_down': (0.0, 0.549),
     'L0_ffn_b_up': (0.0, 0.298)}
    factors = {'L0_tok_quantum_params': 3.802,
     'L0_tok_post_b': 5.806,
     'L0_attn_Wq': 8.0,
     'L0_attn_Wk': 8.0,
     'L0_attn_rel_table': 8.0,
     'L0_attn_Wpk': 8.0,
     'L0_attn_Wpq': 8.0,
     'L0_ffn_slot_params': 8.0,
     'L0_ffn_W_down': 6.095,
     'L0_ffn_W_up': 3.181}
    for name, (base, spread) in spreads.items():
        noise = np.random.default_rng([zlib.crc32(name.encode()), seed]).standard_normal(out[name].shape)
        drawn = base * np.exp(spread * noise) if base else spread * noise
        out[name] = jnp.asarray(drawn.astype(out[name].dtype))
    for name, factor in factors.items():
        out[name] = (out[name] * factor).astype(out[name].dtype)
    return out
```

```python
import math
from contextlib import ExitStack

import numpy as np
import concourse.bass as bass
from concourse import mybir

ALU = mybir.AluOpType
ACT = mybir.ActivationFunctionType
AX = mybir.AxisListType
F32 = mybir.dt.float32
BF16 = mybir.dt.bfloat16
I32 = mybir.dt.int32

B, S, D = 16, 512, 192
H, DH = 12, 16
P = 128
IB = S // P
NT = B * IB
T = B * S
KC = D // 96
HC = H // KC
NQ, NA = 6, 36
NF = 8
REL = 127
NR = 2 * REL + 1
NPR = 6
KF = 2 * NPR * NF
TAB = 516
SCALE = 1.0 / math.sqrt(3.0 * DH)
EXP, SLOT = 8, 4
NS = EXP * SLOT
HF = D // 8
EPS_LN, EPS_L2 = 1e-5, 1e-6
HI, MID, LO = range(3)

TABLE_PARTS = (0, 0, 0, 1, 1, 2)
TOKEN_PARTS = (0, 1, 2, 0, 1, 0)

XQ_PITCH = 5 * P
XQ_LEN = 2 * P + B * XQ_PITCH


def beside(ib):
    return [jb for jb in (ib - 1, ib, ib + 1) if 0 <= jb < IB]


def circuit_plan(n=NQ):
    steps, memo = [], {}

    def emit(op, a, b):
        key = (op, min(a, b), max(a, b)) if op != "subtract" else (op, a, b)
        if key not in memo:
            memo[key] = len(steps)
            steps.append((op, a, b))
        return ("t", memo[key])

    def times(a, b):
        if a is None or b is None:
            return b if a is None else a
        return emit("mult", a, b)

    def total(terms):
        plus = [t for s, t in terms if s > 0]
        minus = [t for s, t in terms if s < 0]
        sign = 1
        if not plus:
            plus, minus, sign = minus, plus, -1
        while len(plus) > 1:
            plus = plus[2:] + [emit("add", plus[0], plus[1])]
        while len(minus) > 1:
            minus = minus[2:] + [emit("add", minus[0], minus[1])]
        return (sign, emit("subtract", plus[0], minus[0]) if minus else plus[0])

    def site(ops):
        x = z = k = 0
        for a in ops:
            if a == "X":
                k += 2 * z
                x ^= 1
            else:
                z ^= 1
        return x, z, (k - (x & z)) % 4

    def chain(sites, menu):
        last, out = max(sites), []
        for wrap in (0, 1) if last == n - 1 else (0,):
            for z0 in (0, 1) if 0 in sites else (0,):
                cur = {(par, 0): (0, 1, None) for par in (0, 1)}
                for j in range(n):
                    new = {}
                    for (pold, xo), (ko, so, no) in cur.items():
                        opts = [(0, 0, None, 1, 0)]
                        if j in sites:
                            opts = [(x, z, *v) for (x, z), v in menu.items() if j > 0 or z == z0]
                        for x, z, c, s, k in opts:
                            if j == n - 1 and last == n - 1 and x != wrap:
                                continue
                            par = pold ^ z if j > 0 else pold
                            ops = ["X"] * (j == 1 and xo) + ["Z"] * (j >= 1 and z0) + ["X"] * (j > 1 and xo)
                            ops += ["X"] * x + ["Z"] * (z and j > 0) + ["Z"] * par + ["X"] * (wrap and j <= 1)
                            lx, lz, ph = site(ops)
                            letter = {(0, 0): None, (1, 0): "x", (0, 1): "z", (1, 1): "y"}[lx, lz]
                            tot = (ph + k + ko + (so < 0) * 2 + (s < 0) * 2) % 4
                            new.setdefault((par, x, c), []).append((tot, no, letter))
                    merged = {}
                    for (par, x, c), found in new.items():
                        kap = found[0][0] % 2
                        terms = [(1 if tot == kap else -1, times(no, ("b", lt, j) if lt else None))
                                 for tot, no, lt in found]
                        s1, node = terms[0] if len(terms) == 1 else total(terms)
                        node = times(node, ("w", c, j) if c else None)
                        merged.setdefault((par, x), []).append((kap, s1, node))
                    cur = {}
                    for key, found in merged.items():
                        s1, node = found[0][1:] if len(found) == 1 else total([f[1:] for f in found])
                        cur[key] = (found[0][0], s1, node)
                    if j >= last:
                        cur = {k: v for k, v in cur.items() if k[0] == 0}
                out += [(s1, node) for _, s1, node in cur.values()]
        return total(out)

    zs = {(0, 1): ("c", 1, 0), (1, 0): ("s", -1, 0)}
    xs = {(1, 0): ("al", 1, 0), (0, 1): ("be", 1, 0), (1, 1): ("ga", -1, 1)}
    ez = [chain(range(1, n), zs)] + [chain(range(q + 1), zs) for q in range(1, n)]
    ex = [chain((q, q + 1), xs) for q in range(n - 1)] + [chain((0, 1, n - 1), xs)]
    level = []
    for _, a, b in steps:
        level.append(1 + max([level[x[1]] for x in (a, b) if x[0] == "t"], default=-1))
    levels = [[i for i in range(len(steps)) if level[i] == v] for v in range(max(level) + 1)]
    ends = {e[1][1] for e in ez + ex}
    until = list(level)
    for i, (_, a, b) in enumerate(steps):
        for x in (a, b):
            if x[0] == "t":
                until[x[1]] = max(until[x[1]], level[i])
    for e in ends:
        until[e] = len(levels) + 1
    place, free, width = {}, [], 0
    for v, ids in enumerate(levels):
        free += sorted(place[i] for i in place if until[i] == v - 1 and i not in ends)
        for i in ids:
            if free:
                place[i] = free.pop(0)
            else:
                place[i], width = width, width + 1
    return steps, levels, place, width, ez, ex


def embed_block(nc, dram, keep):
    steps, levels, place, width, ez, ex = circuit_plan()
    with ExitStack() as ctx:
        def sb(name, shape, dt=F32):
            return ctx.enter_context(nc.sbuf_tensor(name, shape, dt))

        def ps(name, shape, dt=F32):
            return ctx.enter_context(nc.psum_tensor(name, shape, dt))

        def sem(name):
            return ctx.enter_context(nc.semaphore(name))

        ident, FX, GS = keep["ident"], keep["FX"], keep["GS"]
        ids = sb("ids", [P, NT], I32)
        angle = sb("angle", [P, NT, NA])
        turns = sb("turns", [P, NT, NA])
        sine = sb("sine", [P, NT, NA])
        cosine = sb("cosine", [P, NT, NA])
        bloch = sb("bloch", [P, 2, NQ, NT])
        tilt = sb("tilt", [P, 2, NQ, NT])
        work = sb("work", [P, width, NT])
        edge = sb("edge", [P, 3, NQ, NT])
        E = sb("E", [P, NT, NF])
        EU = sb("EU", [P, NT, NF])
        var = sb("var", [P, 6, NT])
        Ft = sb("Ft", [P, NT, NF])
        Fr = sb("Fr", [P, 2, NT, NF])
        Fp = sb("Fp", [P, 3, NT, NF], BF16)
        parity = sb("parity", [P, 2])
        FW = sb("FW", [P, NT, 2, NPR, NF], BF16)
        identb = sb("identb", [P, P], BF16)
        ET = sb("ET", [NF, 2, S])
        GM = sb("GM", [NF, NF])
        Wq, Wk, Wv, Wpk, Wpq = (sb(f"W{k}", [96, KC, D]) for k in ("q", "k", "v", "pk", "pq"))
        cen = sb("cen", [96, KC, D])
        post = sb("post", [96, KC, NF])
        relr = sb("relr", [96, KC, NR])
        relf = sb("relf", [96, KC, NR])
        rows = sb("rows", [1, 5, D])
        ones = sb("ones", [1, 256])
        e7 = sb("e7", [1, NF])
        hmask = sb("hmask", [96, HC])
        CT = sb("CT", [96, KC, NF])
        WT = sb("WT", [96, 2, KC, NF])
        RT = sb("RT", [96, 2, KC, NR])
        WB = sb("WB", [96, 2, KC, HC, NF])
        K3 = sb("K3", [96, KC, 3, NF])
        KB = sb("KB", [96, KC, HC, 3, NF])
        LQ = sb("LQ", [96, KC, 2, NF])
        TB = sb("TB", [48, KC, 2, TAB])
        TR = sb("TR", [48, 2, KC, 2, TAB])
        TP_ = sb("TP", [48, 3, KC, 2, TAB], BF16)
        GW = sb("GW", [NF, 480])
        GR = sb("GR", [NF, 2, 480])
        GP = sb("GP", [NF, 3, 480], BF16)
        pbank = ps("pbank", [P, 8, 512])

        s_ids, s_par, s_w = sem("ids_loaded"), sem("angles_gathered"), sem("weights_loaded")
        s_red, s_sin, s_lvl = sem("angles_reduced"), sem("sines_ready"), sem("circuit_steps")
        s_cir = sem("circuit_done")
        s_tab, s_tv = sem("tables_on_pe"), sem("tables_on_dve")
        s_et, s_ete = sem("evT_ready"), sem("evT_copied")
        s_etd = [sem("evT_stored_even"), sem("evT_stored_odd")]
        s_vg, s_v, s_sq = sem("gram_ready"), sem("variance_steps"), sem("root_ready")
        s_fw, s_fx = sem("features_split"), sem("featuresT_ready")
        s_fe = [sem("featuresT_copied_by_scalar"), sem("featuresT_copied_by_vector")]
        s_gs, s_td = sem("g_weights_stacked"), sem("tables_stored")

        block = ctx.enter_context(nc.Block())
        NW = 14

        @block.gpsimd
        def _(pool):
            pool.wait_ge(s_ids, 16)
            for t in range(NT):
                pool.indirect_dma_start(
                    out=angle[:, t, :], out_offset=None, in_=dram["qparams"],
                    in_offset=bass.IndirectOffsetOnAxis(ap=ids[:, t:t + 1], axis=0)).then_inc(s_par, 16)

        flat = "p t a -> p (t a)"
        ang, trn, sn, cs = (x[:].rearrange(flat) for x in (angle, turns, sine, cosine))
        TWO_PI = 2 * np.pi
        C1 = 6.28125
        C2 = float(TWO_PI - C1)
        MAGIC = 1.5 * 2.0 ** 23
        EDGE = 3.1415925

        def gate(arr, layer, kind):
            return arr[:].rearrange("p t (l q g) -> p l g q t", l=3, q=NQ)[:, layer, kind]

        def operand(x):
            if x[0] == "t":
                return work[:, place[x[1]], :]
            kind, name, q = x
            if kind == "b":
                return gate(cosine, 0, 0)[:, q] if name == "z" else bloch[:, "xy".index(name), q, :]
            if name in ("al", "be"):
                return tilt[:, ("al", "be").index(name), q, :]
            return {"c": gate(cosine, 1, 0), "s": gate(sine, 1, 0), "ga": gate(sine, 1, 1)}[name][:, q]

        TV = {}

        @block.vector
        def _(dve):
            done = [0]

            def step(ins, name=None):
                ins.then_inc(s_tv, 1)
                done[0] += 1
                if name:
                    TV[name] = done[0]
                dve.wait_ge(s_tv, done[0])

            dve.wait_ge(s_w, 16 * NW)
            step(dve.memset(ones[:], 1.0), "ones")
            step(dve.tensor_copy(identb[:], ident[:]), "identb")
            dve.wait_ge(s_tab, 1)
            step(dve.tensor_copy(CT[:], pbank[0:96, 0, 0:KC * NF].rearrange("p (c f) -> p c f", c=KC)), "CT")
            dve.wait_ge(s_tab, 2)
            step(dve.tensor_scalar(GM[:], pbank[0:NF, 1, 480:488], 1.0 / D, None, ALU.mult), "GM")
            step(dve.tensor_copy(WT[:], pbank[0:96, 2, 0:2 * KC * NF].rearrange(
                "p (k c f) -> p k c f", k=2, c=KC)))
            for k in range(2):
                for m in range(KC):
                    step(dve.tensor_copy(RT[:, k, m, :], pbank[0:96, 3 + 2 * k + m, 0:NR]))
            for k in range(2):
                for m in range(KC):
                    step(dve.tensor_tensor(
                        WB[:, k, m], WT[:, k, m, None, :].to_broadcast([96, HC, NF]),
                        hmask[:, :, None].to_broadcast([96, HC, NF]), ALU.mult))
            for m in range(KC):
                for t in range(3):
                    step(dve.tensor_copy(K3[:, m, t, :], WT[:, 1, m, :]))
                for t, r in ((HI, 0), (LO, NR - 1)):
                    step(dve.tensor_tensor(K3[:, m, t, 7:8], K3[:, m, t, 7:8], RT[:, 0, m, r:r + 1], ALU.add))
                for t in range(3):
                    step(dve.tensor_tensor(
                        KB[:, m, :, t, :], K3[:, m, t, None, :].to_broadcast([96, HC, NF]),
                        hmask[:, :, None].to_broadcast([96, HC, NF]), ALU.mult))
                step(dve.memset(LQ[:, m], 0.0))
                for i, r in ((0, NR - 1), (1, 0)):
                    step(dve.tensor_copy(LQ[:, m, i, 7:8], RT[:, 1, m, r:r + 1]))
            TV["blocks"] = done[0]
            dve.wait_ge(s_tab, 3)
            for k in range(2):
                for m in range(KC):
                    src = pbank[0:48, 3 + 2 * k + m, 0:NR]
                    step(dve.tensor_copy(TB[:, m, k, 130:130 + NR], src))
                    step(dve.tensor_copy(TB[:, m, k, 0:130], src[:, 0:1].to_broadcast([48, 130])))
                    step(dve.tensor_copy(TB[:, m, k, 385:TAB], src[:, NR - 1:NR].to_broadcast([48, TAB - 385])))
            step(dve.tensor_copy(GW[:, 0:288], pbank[0:NF, 0, 0:288]))
            step(dve.tensor_copy(GW[:, 288:480], pbank[0:NF, 1, 0:D]))
            for src, rest, parts, name in ((TB[:], TR, TP_, "tables"), (GW[:], GR, GP, "gparts")):
                step(dve.tensor_copy(parts[:, 0], src))
                step(dve.tensor_tensor(rest[:, 0], src, parts[:, 0], ALU.subtract))
                step(dve.tensor_copy(parts[:, 1], rest[:, 0]))
                step(dve.tensor_tensor(rest[:, 1], rest[:, 0], parts[:, 1], ALU.subtract))
                step(dve.tensor_copy(parts[:, 2], rest[:, 1]), name)

            dve.wait_ge(s_par, 16 * NT)
            n = [0]

            def red(ins):
                ins.then_inc(s_red, 1)
                n[0] += 1
                dve.wait_ge(s_red, n[0])

            red(dve.tensor_scalar(trn, ang, float(1 / TWO_PI), MAGIC, ALU.mult, ALU.add))
            red(dve.tensor_scalar(trn, trn, MAGIC, None, ALU.subtract))
            red(dve.scalar_tensor_tensor(out=ang, in0=trn, scalar=-C1, in1=ang, op0=ALU.mult, op1=ALU.add))
            red(dve.scalar_tensor_tensor(out=ang, in0=trn, scalar=-C2, in1=ang, op0=ALU.mult, op1=ALU.add))
            red(dve.tensor_scalar(ang, ang, EDGE, -EDGE, ALU.min, ALU.max))
            red(dve.tensor_scalar(trn, ang, float(np.pi / 2), float(-TWO_PI), ALU.is_gt, ALU.mult))
            red(dve.scalar_tensor_tensor(out=trn, in0=ang, scalar=float(np.pi / 2), in1=trn,
                                         op0=ALU.add, op1=ALU.add))
            red(dve.tensor_scalar(trn, trn, EDGE, -EDGE, ALU.min, ALU.max))
            dve.wait_ge(s_sin, 2)
            pre = [0]

            def lvl(ins):
                ins.then_inc(s_lvl, 1)
                pre[0] += 1

            lvl(dve.tensor_tensor(bloch[:, 0], gate(sine, 0, 0), gate(cosine, 0, 1), ALU.mult))
            lvl(dve.tensor_tensor(bloch[:, 1], gate(sine, 0, 0), gate(sine, 0, 1), ALU.mult))
            lvl(dve.tensor_tensor(tilt[:, 0], gate(cosine, 1, 1), gate(cosine, 1, 0), ALU.mult))
            lvl(dve.tensor_tensor(tilt[:, 1], gate(cosine, 1, 1), gate(sine, 1, 0), ALU.mult))
            for ids_ in levels:
                dve.wait_ge(s_lvl, pre[0])
                for i in ids_:
                    op, a, b = steps[i]
                    lvl(dve.tensor_tensor(work[:, place[i], :], operand(a), operand(b),
                                          {"mult": ALU.mult, "add": ALU.add, "subtract": ALU.subtract}[op]))
            dve.wait_ge(s_lvl, pre[0])
            for q in range(NQ):
                lvl(dve.tensor_tensor(edge[:, 0, q], gate(cosine, 2, 0)[:, q], operand(ez[q][1]), ALU.mult))
                lvl(dve.tensor_tensor(edge[:, 1, q], gate(sine, 2, 0)[:, q], operand(ex[q][1]), ALU.mult))
            lvl(dve.memset(E[:], 1.0))
            dve.wait_ge(s_lvl, pre[0])
            for q in range(NQ):
                assert ez[q][0] == 1 and ex[q][0] == 1
                ins = dve.tensor_tensor(E[:, :, q], edge[:, 0, q], edge[:, 1, q], ALU.subtract)
            ins.then_inc(s_cir, 1)

            dve.wait_ge(s_cir, 1)
            dve.wait_ge(s_vg, B)
            vn = [0]

            def vs(ins):
                ins.then_inc(s_v, 1)
                vn[0] += 1
                dve.wait_ge(s_v, vn[0])

            vs(dve.tensor_tensor(EU[:], pbank[:, 7, :].rearrange("p (t f) -> p t f", f=NF), E[:], ALU.mult))
            vs(dve.tensor_reduce(var[:, 0], EU[:], AX.X, ALU.add))
            vs(dve.tensor_scalar(var[:, 1], var[:, 0], 0.0, EPS_LN, ALU.max, ALU.add))
            dve.wait_ge(s_sq, 1)
            vs(dve.reciprocal(var[:, 3], var[:, 2]))
            vs(dve.tensor_tensor(var[:, 4], var[:, 3], var[:, 3], ALU.mult))
            vs(dve.tensor_tensor(var[:, 4], var[:, 4], var[:, 1], ALU.mult))
            vs(dve.tensor_scalar(var[:, 4], var[:, 4], -0.5, 1.5, ALU.mult, ALU.add))
            vs(dve.tensor_tensor(var[:, 5], var[:, 3], var[:, 4], ALU.mult))
            vs(dve.memset(Ft[:, :, 7:8], 1.0))
            vs(dve.tensor_tensor(Ft[:, :, 0:7], E[:, :, 0:7],
                                 var[:, 5, :, None].to_broadcast([P, NT, 7]), ALU.mult))
            vs(dve.tensor_copy(Fp[:, 0], Ft[:]))
            vs(dve.tensor_tensor(Fr[:, 0], Ft[:], Fp[:, 0], ALU.subtract))
            vs(dve.tensor_copy(Fp[:, 1], Fr[:, 0]))
            vs(dve.tensor_tensor(Fr[:, 1], Fr[:, 0], Fp[:, 1], ALU.subtract))
            vs(dve.tensor_copy(Fp[:, 2], Fr[:, 1]))
            for u in range(2):
                for k, part in enumerate(TOKEN_PARTS):
                    ins = dve.tensor_scalar(FW[:, :, u, k, :], Fp[:, part], parity[:, u:u + 1], None, ALU.mult)
            ins.then_inc(s_fw, 1)
            for c in range(1, NT // 8, 2):
                dve.wait_ge(s_fx, c + 1)
                dve.tensor_copy(FX[:, c * 1024:(c + 1) * 1024],
                                pbank[0:KF, 2 + c % 2, :].bitcast(BF16)).then_inc(s_fe[1], 1)

        @block.sync
        def _(sp):
            sp.dma_start(ids[:], dram["ids"]).then_inc(s_ids, 16)
            for t, name in ((Wq, "Wq"), (Wk, "Wk"), (Wv, "Wv"), (Wpk, "Wpk"), (Wpq, "Wpq")):
                sp.dma_start(t[:], dram[name].rearrange("(c k) n -> k c n", c=KC)).then_inc(s_w, 16)
            sp.dma_start(cen[:], dram["centre"].rearrange("(c k) n -> k c n", c=KC)).then_inc(s_w, 16)
            sp.dma_start(post[:], dram["post"].rearrange("(c k) n -> k c n", c=KC)).then_inc(s_w, 16)
            sp.dma_start(relr[:], dram["rel_back"].rearrange("(c k) n -> k c n", c=KC)).then_inc(s_w, 16)
            sp.dma_start(relf[:], dram["rel_fore"].rearrange("(c k) n -> k c n", c=KC)).then_inc(s_w, 16)
            sp.dma_start(rows[:], dram["rows"]).then_inc(s_w, 16)
            sp.dma_start(ident[:], dram["ident"]).then_inc(s_w, 16)
            sp.dma_start(parity[:], dram["parity"]).then_inc(s_w, 16)
            sp.dma_start(hmask[:], dram["hmask"]).then_inc(s_w, 16)
            sp.dma_start(e7[:], dram["e7"]).then_inc(s_w, 16)
            sp.wait_ge(s_tv, TV["tables"])
            for m in range(KC):
                sp.dma_start(dram["tabD"][m * 48:(m + 1) * 48], TP_[:, :, m]).then_inc(s_td, 16)
            sp.dma_start(dram["tabD"][96:104], TP_[40:48, :, KC - 1]).then_inc(s_td, 16)
            sp.wait_ge(s_tv, TV["gparts"])
            for u in range(2):
                for k, part in enumerate(TABLE_PARTS):
                    r0 = (u * NPR + k) * NF
                    sp.dma_start(GS[r0:r0 + NF, :], GP[:, part, :]).then_inc(s_gs, 16)
            for b in range(B):
                sp.wait_ge(s_ete, b + 1)
                sp.dma_start(dram["evT"][:, b * S:(b + 1) * S], ET[:, b % 2, :]).then_inc(s_etd[b % 2], 16)
            for k in range(2):
                sp.wait_ge(s_etd[k], 16 * B // 2)
            sp.wait_ge(s_td, 16 * (KC + 1))
            sp.wait_ge(s_gs, 16 * 2 * NPR)

        @block.scalar
        def _(act):
            act.wait_ge(s_red, 8)
            act.activation(sn, ang, ACT.Sin).then_inc(s_sin, 1)
            act.activation(cs, trn, ACT.Sin).then_inc(s_sin, 1)
            for b in range(B):
                act.wait_ge(s_et, b + 1)
                if b >= 2:
                    act.wait_ge(s_etd[b % 2], 16 * (b // 2))
                    act.wait_ge(s_vg, b - 1)
                act.activation(ET[:, b % 2, :], pbank[0:NF, 4 + b % 2, :], ACT.Copy).then_inc(s_ete, 1)
            act.wait_ge(s_v, 3)
            act.activation(var[:, 2], var[:, 1], ACT.Sqrt).then_inc(s_sq, 1)
            for c in range(0, NT // 8, 2):
                act.wait_ge(s_fx, c + 1)
                act.activation(FX[:, c * 1024:(c + 1) * 1024],
                               pbank[0:KF, 2 + c % 2, :].bitcast(BF16), ACT.Copy).then_inc(s_fe[0], 1)

        @block.tensor
        def _(pe):
            pe.wait_ge(s_tv, TV["ones"])
            for m in range(KC):
                for c in range(KC):
                    mm = pe.matmul(pbank[0:96, 0, m * NF:(m + 1) * NF], cen[:, c, m * 96:(m + 1) * 96],
                                   post[:, c, :], start=(c == 0), stop=(c == KC - 1), skip_group_check=True)
            mm.then_inc(s_tab, 1)
            pe.wait_ge(s_tv, TV["CT"])
            for c in range(KC):
                pe.matmul(pbank[0:NF, 1, 480:488], CT[:, c, :], CT[:, c, :], start=(c == 0),
                          stop=(c == KC - 1), skip_group_check=True)
            for k, w in enumerate((Wq, Wk)):
                for m in range(KC):
                    out = pbank[0:96, 2, (k * KC + m) * NF:(k * KC + m + 1) * NF]
                    for c in range(KC):
                        pe.matmul(out, w[:, c, m * 96:(m + 1) * 96], CT[:, c, :], start=(c == 0),
                                  stop=False, skip_group_check=True)
                    pe.matmul(out, rows[0:1, k, m * 96:(m + 1) * 96], e7[0:1, :], start=False, stop=True,
                              skip_group_check=True)
            for k, (w, rel) in enumerate(((Wpk, relr), (Wpq, relf))):
                for m in range(KC):
                    out = pbank[0:96, 3 + 2 * k + m, 0:NR]
                    for c in range(KC):
                        pe.matmul(out, w[:, c, m * 96:(m + 1) * 96], rel[:, c, :], start=(c == 0),
                                  stop=False, skip_group_check=True)
                    mm = pe.matmul(out, rows[0:1, 3 + k, m * 96:(m + 1) * 96], ones[0:1, 0:NR], start=False,
                                   stop=True, skip_group_check=True)
            mm.then_inc(s_tab, 1)
            pe.wait_ge(s_tv, TV["blocks"])
            for k in range(2):
                for m in range(KC):
                    pe.matmul(pbank[0:48, 3 + 2 * k + m, 0:NR], WB[:, k, m].rearrange("p h f -> p (h f)"),
                              RT[:, k, m, :], start=True, stop=True, skip_group_check=True)
            for m in range(KC):
                for t in range(3):
                    out = pbank[0:NF, 0, 0:288].rearrange("p (h t f) -> p h t f", h=H, t=3)[
                        :, m * HC:(m + 1) * HC, t, :]
                    pe.matmul(out, WT[:, 0, m, :], KB[:, m, :, t, :], start=True, stop=(t == MID),
                              skip_group_check=True)
                    if t != MID:
                        pe.matmul(out, LQ[:, m, 0 if t == HI else 1, :], WB[:, 1, m], start=False, stop=True,
                                  skip_group_check=True)
            for c in range(KC):
                pe.matmul(pbank[0:NF, 1, 0:D], CT[:, c, :], Wv[:, c, :], start=(c == 0), stop=False,
                          skip_group_check=True)
            pe.matmul(pbank[0:NF, 1, 0:D], e7[0:1, :], rows[0:1, 2, :], start=False, stop=True,
                      skip_group_check=True).then_inc(s_tab, 1)

            pe.wait_ge(s_cir, 1)
            pe.wait_ge(s_tv, TV["gparts"])
            for b in range(B + 1):
                if b < B:
                    if b >= 2:
                        pe.wait_ge(s_ete, b - 1)
                    for k in range(IB):
                        mm = pe.transpose(pbank[0:NF, 4 + b % 2, k * P:(k + 1) * P], E[:, b * IB + k, :], ident[:])
                    mm.then_inc(s_et, 1)
                if b >= 1:
                    pe.wait_ge(s_ete, b)
                    for k in range(IB):
                        t = (b - 1) * IB + k
                        mm = pe.matmul(pbank[:, 7, t * NF:(t + 1) * NF], ET[:, (b - 1) % 2, k * P:(k + 1) * P],
                                       GM[:], start=True, stop=True, skip_group_check=True)
                    mm.then_inc(s_vg, 1)
            pe.wait_ge(s_fw, 1)
            for c in range(NT // 8):
                if c >= 2:
                    pe.wait_ge(s_fe[c % 2], c // 2)
                for k in range(8):
                    mm = pe.transpose(pbank[0:KF, 2 + c % 2, :].bitcast(BF16)[:, k * P:(k + 1) * P],
                                      FW[:, c * 8 + k].rearrange("p u k f -> p (u k f)"), identb[:])
                mm.then_inc(s_fx, 1)


def key_tables_block(nc, dram, keep):
    with ExitStack() as ctx:
        gps = ctx.enter_context(nc.psum_tensor("gps", [96, 2, S], F32))
        parts = ctx.enter_context(nc.sbuf_tensor("gparts", [96, 2, 3, S], BF16))
        rest = ctx.enter_context(nc.sbuf_tensor("grest", [96, 2, S], F32))
        FX, GS = keep["FX"], keep["GS"]
        s_mm, s_hi, s_rest, s_mid, s_low, *s_st = (ctx.enter_context(nc.semaphore(n)) for n in (
            "g_ready", "g_high", "g_rest", "g_middle", "g_low", "g_stored_even", "g_stored_odd"))
        block = ctx.enter_context(nc.Block())
        NG = 3

        @block.tensor
        def _(pe):
            with pe.Fori(0, NG) as q:
                with pe.Fori(0, B // 2) as bp:
                    for k in range(2):
                        pe.wait_ge(s_rest, q * B + bp * 2 + (k + 1))
                        pe.matmul(gps[:, k, :], GS[0:KF, bass.ds(q * 96, 96)],
                                  FX[0:KF, bass.ds(bp * (2 * S) + k * S, S)], start=True, stop=True).then_inc(s_mm, 1)

        @block.scalar
        def _(act):
            with act.Fori(0, NG) as q:
                with act.Fori(0, B // 2) as bp:
                    for k in range(2):
                        act.wait_ge(s_mm, q * B + bp * 2 + (k + 1))
                        act.wait_ge(s_st[k], (q * (B // 2) + bp + 1) * 48)
                        act.activation(parts[:, k, 0], gps[:, k, :], ACT.Copy).then_inc(s_hi, 1)
                        act.wait_ge(s_rest, q * B + bp * 2 + (k + 3))
                        act.activation(parts[:, k, 1], rest[:, k], ACT.Copy).then_inc(s_mid, 1)

        @block.vector
        def _(dve):
            dve.sem_inc(s_rest, 2)
            with dve.Fori(0, NG) as q:
                with dve.Fori(0, B // 2) as bp:
                    for k in range(2):
                        dve.wait_ge(s_hi, q * B + bp * 2 + (k + 1))
                        dve.wait_ge(s_low, q * B + bp * 2 + (k + 1))
                        dve.tensor_tensor(rest[:, k], gps[:, k, :], parts[:, k, 0], ALU.subtract).then_inc(s_rest, 1)

        @block.gpsimd
        def _(pool):
            pool.sem_inc(s_low, 2)
            with pool.Fori(0, NG) as q:
                with pool.Fori(0, B // 2) as bp:
                    for k in range(2):
                        pool.wait_ge(s_mid, q * B + bp * 2 + (k + 1))
                        pool.tensor_tensor(parts[:, k, 2], rest[:, k], parts[:, k, 1], ALU.subtract).then_inc(s_low, 1)

        @block.sync
        def _(sp):
            for k in range(2):
                sp.sem_inc(s_st[k], 48)
            gv = dram["gD"].rearrange("(q r) s i b p -> q b r s i p", q=NG)
            with sp.Fori(0, NG) as q:
                with sp.Fori(0, B // 2) as bp:
                    for k in range(2):
                        sp.wait_ge(s_low, q * B + bp * 2 + (k + 3))
                        for part in range(3):
                            sp.dma_start(gv[q, bp * 2 + k, :, part],
                                         parts[:, k, part].rearrange("r (i p) -> r i p", i=IB)).then_inc(s_st[k], 16)
            for k in range(2):
                sp.wait_ge(s_st[k], 48 + 48 * NG * B // 2)


def attention_block(nc, dram, keep):
    UB = B
    UH = IB * UB
    SB, XR, TB_, PR, OB = 2, 4, 2, 8, 2
    CH = [4 * len(beside(ib)) for ib in range(IB)]
    CHH = 1 + sum(CH)
    AHEAD = CH[0]
    with ExitStack() as ctx:
        def sb(name, shape, dt=F32):
            return ctx.enter_context(nc.sbuf_tensor(name, shape, dt))

        ident, FX = keep["ident"], keep["FX"]
        WV = keep["GS"][0:KF, 288:480]
        TT = sb("TT", [KF, 2, 512], BF16)
        gB = sb("gB", [KF, 2, 3, B * P], BF16)
        XP = sb("XP", [P, 2, 3, B, P])
        XQ = sb("XQ", [P, 2, XQ_LEN])
        Vh = sb("Vh", [P, NT, 2 * DH])
        X = sb("X", [P, XR, S])
        mx = sb("mx", [P, XR])
        PT = sb("PT", [P, PR, S])
        OT = sb("OT", [P, OB, P])
        SC = ctx.enter_context(nc.psum_tensor("SC", [P, SB, S], F32))
        TU = ctx.enter_context(nc.psum_tensor("TU", [P, TB_, S], F32))
        BI = ctx.enter_context(nc.psum_tensor("BI", [P, 2, S], F32))
        OV = ctx.enter_context(nc.psum_tensor("OV", [P, OB, S], F32))

        def sem(name):
            return ctx.enter_context(nc.semaphore(name))

        s_tt, s_z = sem("tables_loaded"), sem("zeros_ready")
        s_g = [sem("g_loaded_even"), sem("g_loaded_odd")]
        s_bias = [sem("key_bias_ready"), sem("query_bias_ready")]
        s_biased = [sem("key_bias_copied"), sem("query_bias_copied")]
        s_sc = sem("scores_ready")
        s_sum = sem("scores_summed")
        s_sh = sem("scores_shifted")
        s_tu = sem("scores_turned")
        s_ex = sem("exps_ready")
        s_pv = sem("values_summed")
        s_ov = sem("outputs_copied")
        s_go = sem("sums_begun")
        s_od = [sem(f"outputs_stored{i}") for i in range(OB)]

        block = ctx.enter_context(nc.Block())

        def chunks(ib):
            return [(jb - ib + 1, jb, jq) for jb in beside(ib) for jq in range(4)]

        def chunk_base(ib):
            return 1 + sum(CH[1:ib]) if ib else 1 + sum(CH[1:])

        TURN, OUT = 3, 9
        STEPS = UH + OUT + 4

        def chunk_at(s):
            if s >= UH:
                return None
            ib = s // UB
            nxt = (ib + 1) % IB
            c = s % UB
            if c >= CH[nxt]:
                return None
            return nxt, c, chunk_base(nxt) + c

        @block.sync
        def _(sp):
            def load_tables(h):
                for u in range(2):
                    for part, k0, n in ((0, 0, 3), (1, 3, 2), (2, 5, 1)):
                        for k in range(k0, k0 + n):
                            r0 = (u * NPR + k) * NF
                            sp.dma_start(TT[r0:r0 + NF], dram["tabD"][bass.ds(h * NF, NF), part, :, 1 - u:513 - u]
                                         ).then_inc(s_tt, 16)

            def load_g(h, ib):
                for u in range(2):
                    for part, k0, n in ((0, 0, 3), (1, 3, 2), (2, 5, 1)):
                        for k in range(k0, k0 + n):
                            r0 = (u * NPR + k) * NF
                            src = dram["gD"].rearrange("(h t c) s i b p -> h c t s i (b p)", h=H, t=3)
                            sp.dma_start(gB[r0:r0 + NF, ib % 2], src[h, :, :, part, ib]).then_inc(s_g[ib % 2], 16)

            def store(h, q):
                sp.wait_ge(s_ov, h * (UH // 4) + (q + 1 + OB))
                ib, b0 = q // 4, 4 * (q % 4)
                sp.dma_start(dram["otD"][h, b0:b0 + 4, :, ib * P:(ib + 1) * P],
                             OT[:, q % OB, :]).then_inc(s_od[q % OB], 16)

            def head(h, last):
                for ib in range(IB):
                    if ib == 2:
                        for k in range(2):
                            sp.wait_ge(s_bias[k], h * CHH + (AHEAD + chunk_base(3) + CH[3]))
                        load_tables(h + 1)
                    for q in range(4 * ib, 4 * ib + 4):
                        store(h, q)
                    if ib < 2 or not last:
                        sp.wait_ge(s_sc, h * UH + (ib + 1) * UB)
                        load_g(h + (ib + 2) // IB, (ib + 2) % IB)

            for i in range(OB):
                sp.sem_inc(s_od[i], 16)
            load_tables(0)
            load_g(0, 0)
            load_g(0, 1)
            with sp.Fori(0, H - 1) as h:
                head(h, False)
            head(H - 1, True)
            for i in range(OB):
                sp.wait_ge(s_od[i], 16 * (1 + H * UH // 4 // OB))

        @block.gpsimd
        def _(pool):
            pool.memset(XQ[:], 0.0).then_inc(s_z, 1)
            pool.memset(Vh[:, :, DH:], 1.0).then_inc(s_z, 1)
            with pool.Fori(0, H) as h:
                for s in range(UH):
                    pool.wait_ge(s_sum, h * UH + (s + 1 + SB))
                    pool.tensor_tensor(X[:, s % XR, :], X[:, s % XR, :],
                                       mx[:, s % XR:s % XR + 1].to_broadcast([P, S]),
                                       ALU.subtract).then_inc(s_sh, 1)

        def bias_out(kind, ib, c):
            rel, jb, jq = chunks(ib)[c]
            if kind == 0:
                return XP[:, ib % 2, rel, :, jq * 32:(jq + 1) * 32]
            o = 2 * P + rel * P + jq * 32
            return XQ[:, ib % 2, 2 * P:].rearrange("p (b n) -> p b n", b=B)[:, :, o - 2 * P:o - 2 * P + 32]

        @block.scalar
        def _(act):
            act.sem_inc(s_biased[0], 1)
            act.sem_inc(s_ex, TB_)
            act.sem_inc(s_ov, OB)

            def copy_bias(count, ib, c):
                act.wait_ge(s_bias[0], count + 1)
                act.activation(bias_out(0, ib, c), BI[:, 0, :].rearrange("p (b n) -> p b n", b=B),
                               ACT.Copy).then_inc(s_biased[0], 1)

            for c in range(AHEAD):
                copy_bias(c, 0, c)
            with act.Fori(0, H) as h:
                act.wait_ge(s_bias[0], h * CHH + (AHEAD + 1))
                act.activation(Vh[:, 0:NT // 2, 0:DH], BI[:, 0, :].rearrange("p (t d) -> p t d", d=DH),
                               ACT.Copy).then_inc(s_biased[0], 1)
                for s in range(STEPS):
                    if chunk_at(s):
                        ib, c, n = chunk_at(s)
                        copy_bias(h * CHH + (AHEAD + n), ib, c)
                    u = s - TURN
                    if 0 <= u < UH:
                        act.wait_ge(s_tu, h * UH + (u + 1 + XR))
                        act.wait_ge(s_pv, h * (UH // 4) + (u // 4 + 1))
                        act.activation(PT[:, u % PR, :], TU[:, u % TB_, :], ACT.Exp, scale=SCALE).then_inc(s_ex, 1)
                    if s >= OUT and (s - OUT) % 4 == 0 and (s - OUT) // 4 < UH // 4:
                        q = (s - OUT) // 4
                        act.wait_ge(s_pv, h * (UH // 4) + (q + 1 + PR // 4))
                        act.wait_ge(s_od[q % OB], (h * (UH // 4 // OB) + (q // OB + 1)) * 16)
                        act.activation(OT[:, q % OB, :], OV[:, q % OB, 0:P], ACT.Copy).then_inc(s_ov, 1)

        @block.vector
        def _(dve):
            dve.sem_inc(s_biased[1], 1)
            dve.sem_inc(s_sum, SB)
            dve.wait_ge(s_z, 2)

            def copy_bias(count, ib, c):
                dve.wait_ge(s_bias[1], count + 1)
                dve.tensor_copy(bias_out(1, ib, c),
                                BI[:, 1, :].rearrange("p (b n) -> p b n", b=B)).then_inc(s_biased[1], 1)

            for c in range(AHEAD):
                copy_bias(c, 0, c)
            with dve.Fori(0, H) as h:
                dve.wait_ge(s_bias[1], h * CHH + (AHEAD + 1))
                dve.tensor_copy(Vh[:, NT // 2:, 0:DH],
                                BI[:, 1, :].rearrange("p (t d) -> p t d", d=DH)).then_inc(s_biased[1], 1)
                for s in range(UH):
                    ib, b = s // UB, s % UB
                    if b == 0:
                        n = 0 if ib == 0 else chunk_base(ib) + CH[ib]
                        dve.wait_ge(s_biased[1], h * CHH + (AHEAD + n + 1))
                        dve.wait_ge(s_sum, h * UH + (s + SB))
                    if chunk_at(s):
                        nib, c, n = chunk_at(s)
                        copy_bias(h * CHH + (AHEAD + n), nib, c)
                    dve.wait_ge(s_sc, h * UH + (s + 1))
                    dve.wait_ge(s_tu, h * UH + (s + 1))
                    dve.sem_inc(s_go, 1)
                    o = XQ_PITCH * b + 3 * P - P * ib
                    dve.tensor_tensor_reduce(X[:, s % XR, :], SC[:, s % SB, :], XQ[:, ib % 2, o:o + S],
                                             1.0, -3.0e38, ALU.add, ALU.max,
                                             mx[:, s % XR:s % XR + 1]).then_inc(s_sum, 1)

        @block.tensor
        def _(pe):
            pe.sem_inc(s_tu, XR)
            pe.sem_inc(s_pv, PR // 4)

            def bias(kind, count, ib, c):
                rel, jb, jq = chunks(ib)[c]
                pe.wait_ge(s_biased[kind], count + 1)
                out = BI[:, kind, :].rearrange("p (b n) -> p b n", b=B)
                own, other = (jb, ib) if kind == 0 else (ib, jb)
                for g in range(16):
                    at = other * P + jq * 32 + 2 * g
                    w = 256 - (at - own * P)
                    mm = pe.matmul(out[:, :, 2 * g:2 * g + 2], TT[:, kind, w:w + P],
                                   FX[0:KF, :].rearrange("k (b n) -> k b n", b=B)[:, :, at:at + 2],
                                   start=(g == 0), stop=(g == 15), skip_group_check=True)
                mm.then_inc(s_bias[kind], 1)

            def values(h):
                for half in range(2):
                    pe.wait_ge(s_biased[half], h * CHH + (AHEAD + 1))
                    for t in range(NT // 2):
                        tile = half * NT // 2 + t
                        mm = pe.matmul(BI[:, half, t * DH:(t + 1) * DH], FX[0:KF, tile * P:(tile + 1) * P],
                                       WV[:, bass.ds(h * DH, DH)], start=(t == 0), stop=(t == NT // 2 - 1),
                                       skip_group_check=True)
                    mm.then_inc(s_bias[half], 1)

            def score(h, s):
                ib, b = s // UB, s % UB
                if b == 0:
                    n = 0 if ib == 0 else chunk_base(ib) + CH[ib]
                    pe.wait_ge(s_biased[0], h * CHH + (AHEAD + n + 1))
                    pe.wait_ge(s_g[ib % 2], (h * (IB // 2) + (ib // 2 + 1)) * (16 * 2 * NPR))
                pe.wait_ge(s_sum, h * UH + (s + 1))
                near = beside(ib)
                for i, jb in enumerate(near):
                    pe.matmul(SC[:, s % SB, jb * P:(jb + 1) * P], XP[:, ib % 2, jb - ib + 1, b, :], ident[:],
                              start=(i == 0), stop=False, is_transpose=True, skip_group_check=True)
                runs = [(HI, 0, near[0]), (LO, near[-1] + 1, IB), (MID, near[0], near[-1] + 1)]
                for t, j0, j1 in runs:
                    if j0 < j1:
                        mm = pe.matmul(SC[:, s % SB, j0 * P:j1 * P], gB[:, ib % 2, t, b * P:(b + 1) * P],
                                       FX[0:KF, b * S + j0 * P:b * S + j1 * P], start=False, stop=(t == MID),
                                       skip_group_check=True)
                mm.then_inc(s_sc, 1)

            def turn(h, u):
                pe.wait_ge(s_sh, h * UH + (u + 1))
                pe.wait_ge(s_ex, h * UH + (u + 1))
                for jb in range(IB):
                    mm = pe.transpose(TU[:, u % TB_, jb * P:(jb + 1) * P], X[:, u % XR, jb * P:(jb + 1) * P],
                                      ident[:])
                mm.then_inc(s_tu, 1)

            def sum_values(h, q):
                if q == 0:
                    for half in range(2):
                        pe.wait_ge(s_biased[half], h * CHH + (AHEAD + 2))
                pe.wait_ge(s_ex, h * UH + (4 * q + 4 + TB_))
                pe.wait_ge(s_ov, h * (UH // 4) + (q + 1))
                for jb in range(IB):
                    for k in range(4):
                        u = 4 * q + k
                        mm = pe.matmul(OV[32 * k:32 * (k + 1), q % OB, 0:P], Vh[:, (u % UB) * IB + jb, :],
                                       PT[:, u % PR, jb * P:(jb + 1) * P], start=(jb == 0), stop=(jb == IB - 1),
                                       skip_group_check=True)
                mm.then_inc(s_pv, 1)

            pe.wait_ge(s_tt, 16 * 2 * NPR)
            for c in range(AHEAD):
                for kind in range(2):
                    bias(kind, c, 0, c)
            with pe.Fori(0, H) as h:
                values(h)
                for s in range(STEPS):
                    if s < UH:
                        score(h, s)
                    if s == 3 * UB:
                        pe.wait_ge(s_tt, (h + 2) * (16 * 2 * NPR))
                    if chunk_at(s):
                        ib, c, n = chunk_at(s)
                        bias(0, h * CHH + (AHEAD + n), ib, c)
                    if TURN <= s < UH + TURN:
                        turn(h, s - TURN)
                    if chunk_at(s):
                        bias(1, h * CHH + (AHEAD + n), ib, c)
                    q = (s - OUT + 1) // 4
                    if (s - OUT + 1) % 4 == 0 and 0 <= q < UH // 4:
                        sum_values(h, q)


def sums_block(nc, dram):
    with ExitStack() as ctx:
        sums = ctx.enter_context(nc.sbuf_tensor("sums", [96, 2, S], F32))
        over = ctx.enter_context(nc.sbuf_tensor("over", [96, 2, S], F32))
        s_ld, s_ov, s_st = (ctx.enter_context(nc.semaphore(n)) for n in ("sums_loaded", "sums_inverted", "over_stored"))
        block = ctx.enter_context(nc.Block())

        @block.sync
        def _(sp):
            sp.dma_start(sums[:], dram["otD"].rearrange("h b r n -> (h b) r n")[:, DH, :].rearrange(
                "(p c) n -> p c n", c=2)).then_inc(s_ld, 16)
            sp.wait_ge(s_ov, 1)
            sp.dma_start(dram["overD"].rearrange("(p c) n -> p c n", c=2), over[:]).then_inc(s_st, 16)
            sp.wait_ge(s_st, 16)

        @block.vector
        def _(dve):
            dve.wait_ge(s_ld, 16)
            dve.reciprocal(over[:], sums[:]).then_inc(s_ov, 1)


def residual_block(nc, dram, keep):
    H1, stats = keep["H1"], keep["stats"]
    with ExitStack() as ctx:
        def sb(name, shape, dt=F32):
            return ctx.enter_context(nc.sbuf_tensor(name, shape, dt))

        def sem(name):
            return ctx.enter_context(nc.semaphore(name))

        Wo, PB = sb("Wo", [96, KC, D]), sb("PB", [NF, D])
        O, R, ON = sb("O", [96, 2, KC, S]), sb("R", [96, 2, KC, S]), sb("ON", [96, 2, KC, S])
        ET = sb("ETb", [NF, 2, S])
        bn, agg = sb("bn", [P, 2, IB, 6]), sb("agg", [P, 2, IB, 2])
        ph = ctx.enter_context(nc.psum_tensor("ph", [P, 2, IB, 512], F32))
        s_w, s_on, s_h = sem("out_weights"), sem("heads_scaled"), sem("h1_ready")
        s_in = [sem("heads_loaded_even"), sem("heads_loaded_odd")]
        s_hc, s_bn, s_ag, s_st = sem("h1_copied"), sem("bn_ready"), sem("bn_done"), sem("stats_kept")
        s_go = sem("aggregates_begun")
        block = ctx.enter_context(nc.Block())
        NL = 16 * (2 * KC + 1)

        @block.sync
        def _(sp):
            sp.dma_start(Wo[:], dram["Wo"].rearrange("(c k) n -> k c n", c=KC)).then_inc(s_w, 16)
            sp.dma_start(PB[:], dram["post_rows"]).then_inc(s_w, 16)
            with sp.Fori(0, B // 2) as bp:
                for k in range(2):
                    b = bp * 2 + k
                    sp.wait_ge(s_h, bp * 2 + (k + 1))
                    for c in range(KC):
                        sp.dma_start(O[:, k, c], dram["otD"].rearrange("h b r n -> b h r n")[
                            b, c * HC:(c + 1) * HC, 0:DH, :]).then_inc(s_in[k], 16)
                        sp.dma_start(R[:, k, c], dram["overD"].rearrange("(h b) n -> b h n", h=H)[
                            b, c * HC:(c + 1) * HC, None, :].to_broadcast([HC, DH, S])).then_inc(s_in[k], 16)
                    sp.dma_start(ET[:, k], dram["evT"][:, bass.ds(bp * (2 * S) + k * S, S)]).then_inc(s_in[k], 16)

        @block.vector
        def _(dve):
            dve.sem_inc(s_st, 2)
            with dve.Fori(0, B // 2) as bp:
                for k in range(2):
                    dve.wait_ge(s_in[k], (bp + 1) * NL)
                    dve.wait_ge(s_h, bp * 2 + (k + 1))
                    dve.tensor_tensor(ON[:, k], O[:, k], R[:, k], ALU.mult).then_inc(s_on, 1)
                    dve.wait_ge(s_hc, bp * 2 + (k + 3))
                    dve.wait_ge(s_st, bp * 2 + (k + 1))
                    for i in range(IB):
                        dve.bn_stats(bn[:, k, i], H1[:, bass.ds(bp * (2 * IB) + (k * IB + i), 1), :].rearrange(
                            "p a n -> p (a n)")).then_inc(s_bn, 1)
                    dve.wait_ge(s_bn, (bp * 2 + (k + 1)) * IB)
                    dve.sem_inc(s_go, 1)
                    for i in range(IB):
                        dve.bn_aggr(agg[:, k, i], bn[:, k, i]).then_inc(s_ag, 1)
                    dve.wait_ge(s_ag, (bp * 2 + (k + 1)) * IB)
                    dve.tensor_copy(stats[:, bass.ds(bp * (2 * IB) + k * IB, IB), :], agg[:, k]).then_inc(s_st, 1)

        @block.scalar
        def _(act):
            act.sem_inc(s_hc, 2)
            with act.Fori(0, B // 2) as bp:
                for k in range(2):
                    act.wait_ge(s_h, bp * 2 + (k + 3))
                    act.activation(H1[:, bass.ds(bp * (2 * IB) + k * IB, IB), :], ph[:, k, :, 0:D],
                                   ACT.Copy).then_inc(s_hc, 1)

        @block.tensor
        def _(pe):
            pe.sem_inc(s_h, 2)
            pe.wait_ge(s_w, 32)
            with pe.Fori(0, B // 2) as bp:
                for k in range(2):
                    pe.wait_ge(s_on, bp * 2 + (k + 1))
                    pe.wait_ge(s_hc, bp * 2 + (k + 1))
                    for i in range(IB):
                        for c in range(KC):
                            pe.matmul(ph[:, k, i, 0:D], ON[:, k, c, i * P:(i + 1) * P], Wo[:, c, :],
                                      start=(c == 0), stop=False)
                        mm = pe.matmul(ph[:, k, i, 0:D], ET[:, k, i * P:(i + 1) * P], PB[:], start=False, stop=True)
                    mm.then_inc(s_h, 1)


def experts_block(nc, dram, keep):
    H1, stats, CTA, ident, XTL = keep["H1"], keep["stats"], keep["CTA"], keep["ident"], keep["XTL"]
    with ExitStack() as ctx:
        def sb(name, shape, dt=F32):
            return ctx.enter_context(nc.sbuf_tensor(name, shape, dt))

        def ps(name, shape):
            return ctx.enter_context(nc.psum_tensor(name, shape, F32))

        def sem(name):
            return ctx.enter_context(nc.semaphore(name))

        slot, sq, SP = sb("slot", [96, KC, NS]), sb("sq", [96, KC, NS]), sb("SP", [96, KC, NS])
        scale, nrm = sb("scale", [96, 1]), sb("nrm", [96, 5, KC, SLOT])
        tok = sb("tok", [P, 6, NT])
        XN = sb("XN", [P, 2, IB, D])
        XT = sb("XT", [96, 2, KC, S])
        DT, DN = sb("DT", [NS, 2, S]), sb("DN", [NS, 2, S])
        dm = sb("dm", [NS, 2, 4])
        DK = sb("DK", [P, 2, IB, NS])
        C0, C1, C2 = (sb(f"C{i}", [P, 2, IB, NS]) for i in range(3))
        cm = sb("cm", [P, 2, 3, IB])
        pX = ps("pX", [96, KC, S])
        pL = ps("pL", [NS, S])
        pC = ps("pC", [P, IB, NS])
        pD = ps("pD", [P, IB, NS])
        pT = ps("pT", [NS, S])
        pS = ps("pS", [96, KC, NS])
        s_w, s_sp, s_rt = sem("slots_loaded"), sem("slot_steps"), sem("roots")
        s_tk, s_xn, s_xt, s_xc = sem("token_steps"), sem("x_normed"), sem("x_turned"), sem("x_copied")
        s_lg, s_dm, s_de, s_dn = sem("logits"), sem("dispatch_steps"), sem("dispatch_exp"), sem("dispatch_scaled")
        s_dt, s_dk = sem("dispatch_turned"), sem("dispatch_copied")
        s_cm, s_ce, s_cr, s_cn = (sem(n) for n in (
            "combine_steps", "combine_exp", "combine_inverted", "combine_scaled"))
        s_ct, s_cc = sem("combine_turned"), sem("combine_copied")
        s_go = sem("turns_begun")
        s_s, s_sc = sem("slots_summed"), sem("slots_copied")
        block = ctx.enter_context(nc.Block())

        @block.sync
        def _(sp):
            sp.dma_start(slot[:], dram["slots"].rearrange("(c k) n -> k c n", c=KC)).then_inc(s_w, 16)
            sp.dma_start(scale[:], dram["scale"].to_broadcast([96, 1])).then_inc(s_w, 16)

        TVN = {}

        @block.vector
        def _(dve):
            n = [0]

            def st(ins):
                ins.then_inc(s_sp, 1)
                n[0] += 1
                dve.wait_ge(s_sp, n[0])

            dve.wait_ge(s_w, 32)
            st(dve.tensor_tensor(sq[:], slot[:], slot[:], ALU.mult))
            st(dve.tensor_reduce(nrm[:, 0], sq[:].rearrange("k c (e s) -> k c s e", e=EXP), AX.X, ALU.add))
            TVN["sq"] = n[0]
            st(dve.tensor_scalar(tok[:, 0], stats[:, :, 1], float(D), None, ALU.mult))
            st(dve.tensor_scalar(tok[:, 1], stats[:, :, 1], EPS_LN, None, ALU.add))
            TVN["var"] = n[0]
            dve.wait_ge(s_rt, 3)
            st(dve.tensor_scalar(tok[:, 4], tok[:, 3], EPS_L2, None, ALU.mult))
            st(dve.tensor_tensor(tok[:, 4], tok[:, 4], tok[:, 2], ALU.add))
            st(dve.reciprocal(tok[:, 5], tok[:, 4]))
            st(dve.tensor_scalar(nrm[:, 2], nrm[:, 1], EPS_L2, None, ALU.add))
            st(dve.reciprocal(nrm[:, 3], nrm[:, 2]))
            st(dve.tensor_scalar(nrm[:, 4], nrm[:, 3], scale[:, 0:1], None, ALU.mult))
            for c in range(KC):
                st(dve.tensor_tensor(SP[:, c].rearrange("k (e s) -> k e s", e=EXP),
                                     slot[:, c].rearrange("k (e s) -> k e s", e=EXP),
                                     nrm[:, 4, c, None, :].to_broadcast([96, EXP, SLOT]), ALU.mult))
            TVN["SP"] = n[0]
            dve.sem_inc(s_dk, 1)
            with dve.Fori(0, B // 2) as bp:
                for k in range(2):
                    at = bp * 2 + (k + 1)
                    dve.wait_ge(s_s, at)
                    for i in range(IB):
                        t = bass.ds(bp * (2 * IB) + (k * IB + i), 1)
                        dve.tensor_scalar(XN[:, k, i], H1[:, t, :].rearrange("p a n -> p (a n)"),
                                          stats[:, t, 0:1].rearrange("p a n -> p (a n)"),
                                          tok[:, 5, t], ALU.subtract, ALU.mult).then_inc(s_xn, 1)
                    dve.wait_ge(s_xt, at)
                    dve.tensor_copy(XT[:, k], pX[:]).then_inc(s_xc, 1)
                    dve.wait_ge(s_lg, at)
                    dve.tensor_reduce(dm[:, k, 0:1], pL[:], AX.X, ALU.max).then_inc(s_dm, 1)
                    dve.tensor_reduce(cm[:, k, 0], pC[:], AX.X, ALU.max).then_inc(s_cm, 1)
                    dve.wait_ge(s_dm, bp * 6 + (3 * k + 1))
                    dve.tensor_scalar(dm[:, k, 1:2], dm[:, k, 0:1], -1.0, None, ALU.mult).then_inc(s_dm, 1)
                    dve.wait_ge(s_cm, bp * 6 + (3 * k + 1))
                    dve.tensor_tensor(C0[:, k], pC[:], cm[:, k, 0, :, None].to_broadcast([P, IB, NS]),
                                      ALU.subtract).then_inc(s_cm, 1)
                    dve.wait_ge(s_de, at)
                    dve.reciprocal(dm[:, k, 3:4], dm[:, k, 2:3]).then_inc(s_dm, 1)
                    dve.wait_ge(s_dm, bp * 6 + (3 * k + 3))
                    dve.tensor_scalar(DN[:, k], DT[:, k], dm[:, k, 3:4], None, ALU.mult).then_inc(s_dn, 1)
                    dve.wait_ge(s_ce, at)
                    dve.tensor_reduce(cm[:, k, 1], C1[:, k], AX.X, ALU.add).then_inc(s_cm, 1)
                    dve.wait_ge(s_cm, bp * 6 + (3 * k + 3))
                    dve.reciprocal(cm[:, k, 2], cm[:, k, 1]).then_inc(s_cr, 1)
                    dve.wait_ge(s_cr, at)
                    dve.tensor_tensor(C2[:, k], C1[:, k], cm[:, k, 2, :, None].to_broadcast([P, IB, NS]),
                                      ALU.mult).then_inc(s_cn, 1)
                    dve.wait_ge(s_dt, at)
                    dve.tensor_copy(DK[:, k], pD[:]).then_inc(s_dk, 1)

        @block.scalar
        def _(act):
            act.wait_ge(s_sp, TVN["sq"])
            act.activation(nrm[:, 1], nrm[:, 0], ACT.Sqrt).then_inc(s_rt, 1)
            act.wait_ge(s_sp, TVN["var"])
            act.activation(tok[:, 2], tok[:, 0], ACT.Sqrt).then_inc(s_rt, 1)
            act.activation(tok[:, 3], tok[:, 1], ACT.Sqrt).then_inc(s_rt, 1)
            with act.Fori(0, B // 2) as bp:
                for k in range(2):
                    at = bp * 2 + (k + 1)
                    act.wait_ge(s_dm, bp * 6 + (3 * k + 2))
                    act.activation(DT[:, k], pL[:], ACT.Exp, bias=dm[:, k, 1:2],
                                   accum_out=dm[:, k, 2:3]).then_inc(s_de, 1)
                    act.wait_ge(s_cm, bp * 6 + (3 * k + 2))
                    act.activation(C1[:, k], C0[:, k], ACT.Exp).then_inc(s_ce, 1)
                    act.wait_ge(s_ct, at)
                    act.activation(CTA[:, bass.ds(bp * (2 * S) + k * S, S)], pT[:], ACT.Copy).then_inc(s_cc, 1)
                    act.wait_ge(s_s, bp * 2 + (k + 3))
                    act.activation(XTL[:, :, bass.ds(bp * 2 + k, 1), :],
                                   pS[:].rearrange("p c (a n) -> p c a n", a=1), ACT.Copy).then_inc(s_sc, 1)

        @block.tensor
        def _(pe):
            pe.sem_inc(s_s, 2)
            pe.wait_ge(s_sp, TVN["SP"])
            with pe.Fori(0, B // 2) as bp:
                for k in range(2):
                    at = bp * 2 + (k + 1)
                    pe.wait_ge(s_xn, (bp * 2 + (k + 1)) * IB)
                    for c in range(KC):
                        for i in range(IB):
                            mm = pe.transpose(pX[:, c, i * P:(i + 1) * P], XN[:, k, i, c * 96:(c + 1) * 96], ident[:])
                    mm.then_inc(s_xt, 1)
                    pe.wait_ge(s_xc, at)
                    for c in range(KC):
                        pe.matmul(pL[:], SP[:, c, :], XT[:, k, c, :], start=(c == 0), stop=(c == KC - 1))
                    for i in range(IB):
                        for c in range(KC):
                            mm = pe.matmul(pC[:, i, :], XT[:, k, c, i * P:(i + 1) * P], SP[:, c, :],
                                           start=(c == 0), stop=(c == KC - 1), skip_group_check=True)
                    mm.then_inc(s_lg, 1)
                    pe.wait_ge(s_dn, at)
                    pe.wait_ge(s_dk, at)
                    pe.sem_inc(s_go, 1)
                    for i in range(IB):
                        mm = pe.transpose(pD[:, i, :], DN[:, k, i * P:(i + 1) * P], ident[0:NS, 0:NS])
                    mm.then_inc(s_dt, 1)
                    pe.wait_ge(s_cn, at)
                    for i in range(IB):
                        mm = pe.transpose(pT[:, i * P:(i + 1) * P], C2[:, k, i, :], ident[:])
                    mm.then_inc(s_ct, 1)
                    pe.wait_ge(s_dk, bp * 2 + (k + 2))
                    for c in range(KC):
                        for i in range(IB):
                            mm = pe.matmul(pS[:, c, :], XN[:, k, i, c * 96:(c + 1) * 96], DK[:, k, i, :],
                                           start=(i == 0), stop=(i == IB - 1), skip_group_check=True)
                    mm.then_inc(s_s, 1)
                    pe.wait_ge(s_cc, at)
                    pe.wait_ge(s_sc, at)


def mix_block(nc, dram, keep):
    H1, CTA, XTL = keep["H1"], keep["CTA"], keep["XTL"]
    with ExitStack() as ctx:
        def sb(name, shape, dt=F32):
            return ctx.enter_context(nc.sbuf_tensor(name, shape, dt))

        def sem(name):
            return ctx.enter_context(nc.semaphore(name))

        Wd, Wu = sb("Wd", [96, KC, EXP, HF]), sb("Wu", [HF, EXP, D])
        bd, bu, ones = sb("bd", [HF, EXP]), sb("bu", [1, EXP, D]), sb("onesr", [1, B * SLOT])
        HG = sb("HG", [HF, EXP, B * SLOT])
        YS = sb("YS", [B * SLOT, EXP, D])
        YB = sb("YB", [NS, B, D])
        CR = sb("CR", [NS, 2, S])
        OUT = sb("OUT", [P, 2, IB, D])
        pH = ctx.enter_context(nc.psum_tensor("pH", [P, 8, 512], F32))
        s_w, s_on, s_h, s_g, s_y, s_yc, s_yd, s_yb = (sem(n) for n in (
            "expert_weights", "ones_set", "hidden_ready", "gelu_done", "slot_out", "slot_out_copied",
            "slot_out_stored", "slot_out_loaded"))
        s_cr, s_m, s_o = sem("combine_placed"), sem("mixed"), sem("outputs_ready")
        s_od = [sem("outputs_written_even"), sem("outputs_written_odd")]
        block = ctx.enter_context(nc.Block())

        @block.sync
        def _(sp):
            for c in range(KC):
                sp.dma_start(Wd[:, c], dram["Wd"].rearrange("e (c k) h -> c k e h", c=KC)[c]).then_inc(s_w, 16)
            sp.dma_start(Wu[:], dram["Wu"].rearrange("e h d -> h e d")).then_inc(s_w, 16)
            with nc.allow_non_contiguous_dma(reason="192 biases"):
                sp.dma_start(bd[:], dram["bd"].rearrange("e h -> h e")).then_inc(s_w, 16)
            sp.dma_start(bu[:], dram["bu"].rearrange("(a e) d -> a e d", a=1)).then_inc(s_w, 16)
            sp.wait_ge(s_yc, EXP // 2)
            sp.dma_start(dram["yD"].rearrange("b p e d -> (b p) e d"), YS[:]).then_inc(s_yd, 16)
            sp.wait_ge(s_yd, 16)
            for e in range(EXP):
                sp.dma_start(YB[e * SLOT:(e + 1) * SLOT], dram["yD"].rearrange("b p e d -> e p b d")[e]
                             ).then_inc(s_yb, 16)
            for k in range(2):
                sp.sem_inc(s_od[k], 16)
            with sp.Fori(0, B // 2) as bp:
                for k in range(2):
                    sp.wait_ge(s_o, bp * 2 + (k + 3))
                    sp.dma_start(dram["out"].rearrange("b (i p) d -> b p i d", p=P)[bp * 2 + k],
                                 OUT[:, k]).then_inc(s_od[k], 16)
            for k in range(2):
                sp.wait_ge(s_od[k], 16 + 16 * B // 2)

        @block.scalar
        def _(act):
            act.wait_ge(s_h, 1)
            act.wait_ge(s_w, 80)
            for e in range(EXP):
                ins = act.activation(HG[:, e, :], pH[0:HF, 0, e * 64:(e + 1) * 64], ACT.Gelu, bias=bd[:, e:e + 1])
            ins.then_inc(s_g, 1)
            with act.Fori(0, B // 2) as bp:
                for k in range(2):
                    act.wait_ge(s_m, bp * 2 + (k + 1))
                    act.activation(CR[:, k], CTA[:, bass.ds(bp * (2 * S) + k * S, S)], ACT.Copy).then_inc(s_cr, 1)

        @block.vector
        def _(dve):
            dve.memset(ones[:], 1.0).then_inc(s_on, 1)
            for e in range(0, EXP, 2):
                dve.wait_ge(s_y, e // 2 + 1)
                dve.tensor_copy(YS[:, e:e + 2, :], pH[0:B * SLOT, 1 + e // 2, 0:2 * D].rearrange(
                    "p (e d) -> p e d", e=2)).then_inc(s_yc, 1)
            dve.sem_inc(s_o, 2)
            with dve.Fori(0, B // 2) as bp:
                for k in range(2):
                    dve.wait_ge(s_m, bp * 2 + (k + 3))
                    dve.wait_ge(s_od[k], (bp + 1) * 16)
                    dve.tensor_tensor(OUT[:, k], pH[:, 4 * k:4 * k + 4, 0:D],
                                      H1[:, bass.ds(bp * (2 * IB) + k * IB, IB), :], ALU.add).then_inc(s_o, 1)

        @block.tensor
        def _(pe):
            pe.sem_inc(s_m, 2)
            pe.wait_ge(s_w, 80)
            pe.wait_ge(s_on, 1)
            for e in range(EXP):
                for c in range(KC):
                    mm = pe.matmul(pH[0:HF, 0, e * 64:(e + 1) * 64], Wd[:, c, e, :],
                                   XTL[:, c, :, e * SLOT:(e + 1) * SLOT], start=(c == 0), stop=(c == KC - 1),
                                   skip_group_check=True)
            mm.then_inc(s_h, 1)
            pe.wait_ge(s_g, 1)
            for e in range(EXP):
                out = pH[0:B * SLOT, 1 + e // 2, (e % 2) * D:(e % 2 + 1) * D]
                pe.matmul(out, HG[:, e, :], Wu[:, e, :], start=True, stop=False, skip_group_check=True)
                mm = pe.matmul(out, ones[0:1, :], bu[0:1, e, :], start=False, stop=True, skip_group_check=True)
                if e % 2:
                    mm.then_inc(s_y, 1)
            pe.wait_ge(s_yb, 16 * EXP)
            with pe.Fori(0, B // 2) as bp:
                for k in range(2):
                    pe.wait_ge(s_cr, bp * 2 + (k + 1))
                    pe.wait_ge(s_o, bp * 2 + (k + 1))
                    for i in range(IB):
                        mm = pe.matmul(pH[:, 4 * k + i, 0:D], CR[:, k, i * P:(i + 1) * P],
                                       YB[:, bass.ds(bp * 2 + k, 1), :].rearrange("p a n -> p (a n)"),
                                       start=True, stop=True)
                    mm.then_inc(s_m, 1)


def build(nc, dram):
    with ExitStack() as outer:
        def sb(name, shape, dt=F32):
            return outer.enter_context(nc.sbuf_tensor(name, shape, dt))

        keep = {"ident": sb("ident", [P, P])}
        with ExitStack() as ctx:
            keep["FX"] = ctx.enter_context(nc.sbuf_tensor("FX", [KF, T], BF16))
            keep["GS"] = ctx.enter_context(nc.sbuf_tensor("GS", [KF, 480], BF16))
            embed_block(nc, dram, keep)
            key_tables_block(nc, dram, keep)
            attention_block(nc, dram, keep)
        sums_block(nc, dram)
        keep["H1"] = sb("H1", [P, NT, D])
        keep["stats"] = sb("stats", [P, NT, 2])
        residual_block(nc, dram, keep)
        keep["CTA"] = sb("CTA", [NS, T])
        keep["XTL"] = sb("XTL", [96, KC, B, NS])
        experts_block(nc, dram, keep)
        mix_block(nc, dram, keep)


def kernel(x, L0_tok_quantum_params, L0_tok_post_w, L0_tok_post_b, L0_attn_Wq, L0_attn_bq, L0_attn_Wk,
           L0_attn_bk, L0_attn_Wv, L0_attn_bv, L0_attn_rel_table, L0_attn_Wpk, L0_attn_bpk, L0_attn_Wpq,
           L0_attn_bpq, L0_attn_Wo, L0_attn_bo, L0_ffn_slot_params, L0_ffn_scale, L0_ffn_W_down,
           L0_ffn_b_down, L0_ffn_W_up, L0_ffn_b_up):
    import concourse.bacc as bacc
    from concourse.bass_utils import run_bass_kernel_spmd

    f4 = np.float32
    one = np.ones((1, 1), f4)
    rel = np.asarray(L0_attn_rel_table).T
    post_w, post_b = np.asarray(L0_tok_post_w), np.asarray(L0_tok_post_b)
    arrays = {
        "ids": np.asarray(x).reshape(NT, P).T,
        "qparams": np.asarray(L0_tok_quantum_params).reshape(-1, NA),
        "Wq": L0_attn_Wq, "Wk": L0_attn_Wk, "Wv": L0_attn_Wv, "Wpk": L0_attn_Wpk, "Wpq": L0_attn_Wpq,
        "Wo": L0_attn_Wo,
        "post": np.concatenate([post_w, post_b[:, None], np.zeros((D, 1), f4)], axis=1),
        "post_rows": np.concatenate([post_w.T, post_b[None], np.asarray(L0_attn_bo)[None]]),
        "rel_back": rel[:, ::-1], "rel_fore": rel,
        "rows": np.stack([np.asarray(a) for a in (L0_attn_bq, L0_attn_bk, L0_attn_bv, L0_attn_bpk,
                                                  L0_attn_bpq)])[None],
        "slots": np.asarray(L0_ffn_slot_params).reshape(D, NS),
        "scale": np.asarray(L0_ffn_scale).reshape(1, 1),
        "Wd": L0_ffn_W_down, "bd": L0_ffn_b_down, "Wu": L0_ffn_W_up, "bu": L0_ffn_b_up,
        "ident": np.eye(P, dtype=f4),
        "centre": np.eye(D, dtype=f4) - f4(1 / D),
        "parity": (np.arange(P)[:, None] % 2 == np.arange(2)[None]).astype(f4),
        "hmask": (np.arange(96)[:, None] // DH == np.arange(HC)[None]).astype(f4),
        "e7": np.eye(NF, dtype=f4)[7:8],
    }
    arrays = {k: np.ascontiguousarray(v) for k, v in arrays.items()}
    nc = bacc.Bacc("TRN2", target_bir_lowering=False, num_devices=1)
    dram = {k: nc.dram_tensor(f"{k}_in", a.shape, mybir.dt.from_np(a.dtype), kind="ExternalInput").ap()
            for k, a in arrays.items()}
    dram["out"] = nc.dram_tensor("out_dram", (B, S, D), F32, kind="ExternalOutput").ap()
    scratch = {
        "tabD": ((H + 1) * NF, 3, 2, TAB, BF16),
        "evT": (NF, T, F32),
        "gD": (H * 3 * NF, 3, IB, B, P, BF16),
        "otD": (H, B, 2 * DH, S, F32),
        "overD": (H * B, S, F32),
        "yD": (B, SLOT, EXP, D, F32),
    }
    for k, (*shape, dt) in scratch.items():
        dram[k] = nc.dram_tensor(f"{k}_scratch", tuple(shape), dt).ap()
    build(nc, dram)
    r = run_bass_kernel_spmd(nc, [{f"{k}_in": a for k, a in arrays.items()}], core_ids=[0])
    return r.results[0]["out_dram"]
```

```python
import math
from contextlib import ExitStack

import numpy as np
import concourse.bass as bass
from concourse import mybir

ALU = mybir.AluOpType
ACT = mybir.ActivationFunctionType
AX = mybir.AxisListType
F32 = mybir.dt.float32
BF16 = mybir.dt.bfloat16
I32 = mybir.dt.int32

B, S, D = 16, 512, 192
H, DH = 12, 16
P = 128
IB = S // P
NT = B * IB
T = B * S
KC = D // 96
HC = H // KC
NQ, NA = 6, 36
NF = 8
REL = 127
NR = 2 * REL + 1
NPR = 6
KF = 2 * NPR * NF
TAB = 516
SCALE = 1.0 / math.sqrt(3.0 * DH)
EXP, SLOT = 8, 4
NS = EXP * SLOT
HF = D // 8
GN = 2 * H * 2 * NF + D
EPS_LN, EPS_L2 = 1e-5, 1e-6
HI, MID, LO = range(3)

TABLE_PARTS = (0, 0, 0, 1, 1, 2)
TOKEN_PARTS = (0, 1, 2, 0, 1, 0)

XQ_PITCH = 5 * P
XQ_LEN = 2 * P + B * XQ_PITCH


def beside(ib):
    return [jb for jb in (ib - 1, ib, ib + 1) if 0 <= jb < IB]


def circuit_plan(n=NQ):
    steps, memo = [], {}

    def emit(op, a, b):
        key = (op, min(a, b), max(a, b)) if op != "subtract" else (op, a, b)
        if key not in memo:
            memo[key] = len(steps)
            steps.append((op, a, b))
        return ("t", memo[key])

    def times(a, b):
        if a is None or b is None:
            return b if a is None else a
        return emit("mult", a, b)

    def total(terms):
        plus = [t for s, t in terms if s > 0]
        minus = [t for s, t in terms if s < 0]
        sign = 1
        if not plus:
            plus, minus, sign = minus, plus, -1
        while len(plus) > 1:
            plus = plus[2:] + [emit("add", plus[0], plus[1])]
        while len(minus) > 1:
            minus = minus[2:] + [emit("add", minus[0], minus[1])]
        return (sign, emit("subtract", plus[0], minus[0]) if minus else plus[0])

    def site(ops):
        x = z = k = 0
        for a in ops:
            if a == "X":
                k += 2 * z
                x ^= 1
            else:
                z ^= 1
        return x, z, (k - (x & z)) % 4

    def chain(sites, menu):
        last, out = max(sites), []
        for wrap in (0, 1) if last == n - 1 else (0,):
            for z0 in (0, 1) if 0 in sites else (0,):
                cur = {(par, 0): (0, 1, None) for par in (0, 1)}
                for j in range(n):
                    new = {}
                    for (pold, xo), (ko, so, no) in cur.items():
                        opts = [(0, 0, None, 1, 0)]
                        if j in sites:
                            opts = [(x, z, *v) for (x, z), v in menu.items() if j > 0 or z == z0]
                        for x, z, c, s, k in opts:
                            if j == n - 1 and last == n - 1 and x != wrap:
                                continue
                            par = pold ^ z if j > 0 else pold
                            ops = ["X"] * (j == 1 and xo) + ["Z"] * (j >= 1 and z0) + ["X"] * (j > 1 and xo)
                            ops += ["X"] * x + ["Z"] * (z and j > 0) + ["Z"] * par + ["X"] * (wrap and j <= 1)
                            lx, lz, ph = site(ops)
                            letter = {(0, 0): None, (1, 0): "x", (0, 1): "z", (1, 1): "y"}[lx, lz]
                            tot = (ph + k + ko + (so < 0) * 2 + (s < 0) * 2) % 4
                            new.setdefault((par, x, c), []).append((tot, no, letter))
                    merged = {}
                    for (par, x, c), found in new.items():
                        kap = found[0][0] % 2
                        terms = [(1 if tot == kap else -1, times(no, ("b", lt, j) if lt else None))
                                 for tot, no, lt in found]
                        s1, node = terms[0] if len(terms) == 1 else total(terms)
                        node = times(node, ("w", c, j) if c else None)
                        merged.setdefault((par, x), []).append((kap, s1, node))
                    cur = {}
                    for key, found in merged.items():
                        s1, node = found[0][1:] if len(found) == 1 else total([f[1:] for f in found])
                        cur[key] = (found[0][0], s1, node)
                    if j >= last:
                        cur = {k: v for k, v in cur.items() if k[0] == 0}
                out += [(s1, node) for _, s1, node in cur.values()]
        return total(out)

    zs = {(0, 1): ("c", 1, 0), (1, 0): ("s", -1, 0)}
    xs = {(1, 0): ("al", 1, 0), (0, 1): ("be", 1, 0), (1, 1): ("ga", -1, 1)}
    ez = [chain(range(1, n), zs)] + [chain(range(q + 1), zs) for q in range(1, n)]
    ex = [chain((q, q + 1), xs) for q in range(n - 1)] + [chain((0, 1, n - 1), xs)]
    level = []
    for _, a, b in steps:
        level.append(1 + max([level[x[1]] for x in (a, b) if x[0] == "t"], default=-1))
    levels = [[i for i in range(len(steps)) if level[i] == v] for v in range(max(level) + 1)]
    ends = {e[1][1] for e in ez + ex}
    until = list(level)
    for i, (_, a, b) in enumerate(steps):
        for x in (a, b):
            if x[0] == "t":
                until[x[1]] = max(until[x[1]], level[i])
    for e in ends:
        until[e] = len(levels) + 1
    place, free, width = {}, [], 0
    for v, ids in enumerate(levels):
        free += sorted(place[i] for i in place if until[i] == v - 1 and i not in ends)
        for i in ids:
            if free:
                place[i] = free.pop(0)
            else:
                place[i], width = width, width + 1
    return steps, levels, place, width, ez, ex


def embed_block(nc, dram, keep):
    steps, levels, place, width, ez, ex = circuit_plan()
    EB, EQ = 4, 2
    with ExitStack() as ctx:
        def sb(name, shape, dt=F32):
            return ctx.enter_context(nc.sbuf_tensor(name, shape, dt))

        def ps(name, shape, dt=F32):
            return ctx.enter_context(nc.psum_tensor(name, shape, dt))

        def sem(name):
            return ctx.enter_context(nc.semaphore(name))

        ident, FX, GS = keep["ident"], keep["FX"], keep["GS"]
        ids = sb("ids", [P, NT], I32)
        angle = sb("angle", [P, NT, NA])
        turns = sb("turns", [P, NT, NA])
        sine = sb("sine", [P, NT, NA])
        cosine = sb("cosine", [P, NT, NA])
        bloch = sb("bloch", [P, 2, NQ, NT])
        tilt = sb("tilt", [P, 2, NQ, NT])
        work = sb("work", [P, width, NT])
        edge = sb("edge", [P, 3, NQ, NT])
        E = sb("E", [P, NT, NF])
        EU = sb("EU", [P, 2, NT, NQ + 1])
        var = sb("var", [P, 6, NT])
        Ft = sb("Ft", [P, NT, NF])
        Fr = sb("Fr", [P, 2, NT, NF])
        Fp = sb("Fp", [P, 3, NT, NF], BF16)
        parity = sb("parity", [P, 2])
        FW = sb("FW", [P, NT, 2, NPR, NF], BF16)
        identb = sb("identb", [P, P], BF16)
        ET = sb("ET", [NF, EB, S])
        GM = sb("GM", [NF, NF])
        GMB = sb("GMB", [P, NF, NF])
        Wq, Wk, Wv, Wpk, Wpq = (sb(f"W{k}", [96, KC, D]) for k in ("q", "k", "v", "pk", "pq"))
        cen = sb("cen", [96, KC, D])
        post = sb("post", [96, KC, NF])
        relr = sb("relr", [96, KC, NR])
        relf = sb("relf", [96, KC, NR])
        rows = sb("rows", [1, 5, D])
        ones = sb("ones", [1, 256])
        e7 = sb("e7", [1, NF])
        hmask = sb("hmask", [96, HC])
        CT = sb("CT", [96, KC, NF])
        WT = sb("WT", [96, 2, KC, NF])
        RT = sb("RT", [96, 2, KC, NR])
        WB = sb("WB", [96, 2, KC, HC, NF])
        K3 = sb("K3", [96, KC, 3, NF])
        KB = sb("KB", [96, KC, HC, 3, NF])
        LQ = sb("LQ", [96, KC, 2, NF])
        TB = sb("TB", [48, KC, 2, TAB])
        TR = sb("TR", [48, 2, KC, 2, TAB])
        TP_ = sb("TP", [48, 3, KC, 2, TAB], BF16)
        GW = sb("GW", [NF, GN])
        GR = sb("GR", [NF, 2, GN])
        GP = sb("GP", [NF, 3, GN], BF16)
        pbank = ps("pbank", [P, 8, 512])

        s_ids, s_par, s_w = sem("ids_loaded"), sem("angles_gathered"), sem("weights_loaded")
        s_red, s_sin, s_lvl = sem("angles_reduced"), sem("sines_ready"), sem("circuit_steps")
        s_cir = sem("circuit_done")
        s_tab, s_tv = sem("tables_on_pe"), sem("tables_on_dve")
        s_et, s_ete = sem("evT_ready"), sem("evT_copied")
        s_etd = [sem(f"evT_stored{k}") for k in range(EB // EQ)]
        s_gm, s_v, s_sq = sem("gram_moved"), sem("variance_steps"), sem("root_ready")
        s_fw, s_fx = sem("features_split"), sem("featuresT_ready")
        s_fe = [sem("featuresT_copied_by_scalar"), sem("featuresT_copied_by_vector")]
        s_gs, s_td = sem("g_weights_stacked"), sem("tables_stored")

        block = ctx.enter_context(nc.Block())
        NW = 14

        @block.gpsimd
        def _(pool):
            pool.wait_ge(s_ids, 16)
            for t in range(NT):
                pool.indirect_dma_start(
                    out=angle[:, t, :], out_offset=None, in_=dram["qparams"],
                    in_offset=bass.IndirectOffsetOnAxis(ap=ids[:, t:t + 1], axis=0)).then_inc(s_par, 16)

        flat = "p t a -> p (t a)"
        ang, trn, sn, cs = (x[:].rearrange(flat) for x in (angle, turns, sine, cosine))
        TWO_PI = 2 * np.pi
        C1 = 6.28125
        C2 = float(TWO_PI - C1)
        MAGIC = 1.5 * 2.0 ** 23
        EDGE = 3.1415925

        def gate(arr, layer, kind):
            return arr[:].rearrange("p t (l q g) -> p l g q t", l=3, q=NQ)[:, layer, kind]

        def operand(x):
            if x[0] == "t":
                return work[:, place[x[1]], :]
            kind, name, q = x
            if kind == "b":
                return gate(cosine, 0, 0)[:, q] if name == "z" else bloch[:, "xy".index(name), q, :]
            if name in ("al", "be"):
                return tilt[:, ("al", "be").index(name), q, :]
            return {"c": gate(cosine, 1, 0), "s": gate(sine, 1, 0), "ga": gate(sine, 1, 1)}[name][:, q]

        TV = {}

        @block.vector
        def _(dve):
            done = [0]

            def step(ins, name=None):
                ins.then_inc(s_tv, 1)
                done[0] += 1
                if name:
                    TV[name] = done[0]
                dve.wait_ge(s_tv, done[0])

            dve.wait_ge(s_w, 16 * NW)
            step(dve.memset(ones[:], 1.0), "ones")
            step(dve.tensor_copy(identb[:], ident[:]), "identb")
            dve.wait_ge(s_tab, 1)
            step(dve.tensor_copy(CT[:], pbank[0:96, 0, 0:KC * NF].rearrange("p (c f) -> p c f", c=KC)), "CT")
            dve.wait_ge(s_tab, 2)
            step(dve.tensor_scalar(GM[:], pbank[0:NF, 1, 480:488], 1.0 / D, None, ALU.mult), "GM")
            step(dve.tensor_copy(WT[:], pbank[0:96, 2, 0:2 * KC * NF].rearrange(
                "p (k c f) -> p k c f", k=2, c=KC)))
            for k in range(2):
                for m in range(KC):
                    step(dve.tensor_copy(RT[:, k, m, :], pbank[0:96, 3 + 2 * k + m, 0:NR]))
            for k in range(2):
                for m in range(KC):
                    step(dve.tensor_tensor(
                        WB[:, k, m], WT[:, k, m, None, :].to_broadcast([96, HC, NF]),
                        hmask[:, :, None].to_broadcast([96, HC, NF]), ALU.mult))
            for m in range(KC):
                for t in range(3):
                    step(dve.tensor_copy(K3[:, m, t, :], WT[:, 1, m, :]))
                for t, r in ((HI, 0), (LO, NR - 1)):
                    step(dve.tensor_tensor(K3[:, m, t, 7:8], K3[:, m, t, 7:8], RT[:, 0, m, r:r + 1], ALU.add))
                for t in range(3):
                    step(dve.tensor_tensor(
                        KB[:, m, :, t, :], K3[:, m, t, None, :].to_broadcast([96, HC, NF]),
                        hmask[:, :, None].to_broadcast([96, HC, NF]), ALU.mult))
                step(dve.memset(LQ[:, m], 0.0))
                for i, r in ((0, NR - 1), (1, 0)):
                    step(dve.tensor_copy(LQ[:, m, i, 7:8], RT[:, 1, m, r:r + 1]))
            TV["blocks"] = done[0]
            dve.wait_ge(s_tab, 3)
            for k in range(2):
                for m in range(KC):
                    src = pbank[0:48, 3 + 2 * k + m, 0:NR]
                    step(dve.tensor_copy(TB[:, m, k, 130:130 + NR], src))
                    step(dve.tensor_copy(TB[:, m, k, 0:130], src[:, 0:1].to_broadcast([48, 130])))
                    step(dve.tensor_copy(TB[:, m, k, 385:TAB], src[:, NR - 1:NR].to_broadcast([48, TAB - 385])))
            for k, t0 in enumerate((MID, HI)):
                step(dve.tensor_copy(GW[:, k * 192:(k + 1) * 192].rearrange("p (h f t) -> p h f t", h=H, f=NF),
                                     pbank[0:NF, 0, 0:288].rearrange("p (h t f) -> p h f t", h=H, t=3)[
                                         :, :, :, t0:t0 + 2]))
            step(dve.tensor_copy(GW[:, 384:576], pbank[0:NF, 1, 0:D]))
            for src, rest, parts, name in ((TB[:], TR, TP_, "tables"), (GW[:], GR, GP, "gparts")):
                step(dve.tensor_copy(parts[:, 0], src))
                step(dve.tensor_tensor(rest[:, 0], src, parts[:, 0], ALU.subtract))
                step(dve.tensor_copy(parts[:, 1], rest[:, 0]))
                step(dve.tensor_tensor(rest[:, 1], rest[:, 0], parts[:, 1], ALU.subtract))
                step(dve.tensor_copy(parts[:, 2], rest[:, 1]), name)

            dve.wait_ge(s_par, 16 * NT)
            n = [0]

            def red(ins):
                ins.then_inc(s_red, 1)
                n[0] += 1
                dve.wait_ge(s_red, n[0])

            red(dve.tensor_scalar(trn, ang, float(1 / TWO_PI), MAGIC, ALU.mult, ALU.add))
            red(dve.tensor_scalar(trn, trn, MAGIC, None, ALU.subtract))
            red(dve.scalar_tensor_tensor(out=ang, in0=trn, scalar=-C1, in1=ang, op0=ALU.mult, op1=ALU.add))
            red(dve.scalar_tensor_tensor(out=ang, in0=trn, scalar=-C2, in1=ang, op0=ALU.mult, op1=ALU.add))
            red(dve.tensor_scalar(ang, ang, EDGE, -EDGE, ALU.min, ALU.max))
            red(dve.tensor_scalar(trn, ang, float(np.pi / 2), float(-TWO_PI), ALU.is_gt, ALU.mult))
            red(dve.scalar_tensor_tensor(out=trn, in0=ang, scalar=float(np.pi / 2), in1=trn,
                                         op0=ALU.add, op1=ALU.add))
            red(dve.tensor_scalar(trn, trn, EDGE, -EDGE, ALU.min, ALU.max))
            dve.wait_ge(s_sin, 2)
            pre = [0]

            def lvl(ins):
                ins.then_inc(s_lvl, 1)
                pre[0] += 1

            lvl(dve.tensor_tensor(bloch[:, 0], gate(sine, 0, 0), gate(cosine, 0, 1), ALU.mult))
            lvl(dve.tensor_tensor(bloch[:, 1], gate(sine, 0, 0), gate(sine, 0, 1), ALU.mult))
            lvl(dve.tensor_tensor(tilt[:, 0], gate(cosine, 1, 1), gate(cosine, 1, 0), ALU.mult))
            lvl(dve.tensor_tensor(tilt[:, 1], gate(cosine, 1, 1), gate(sine, 1, 0), ALU.mult))
            for ids_ in levels:
                dve.wait_ge(s_lvl, pre[0])
                for i in ids_:
                    op, a, b = steps[i]
                    lvl(dve.tensor_tensor(work[:, place[i], :], operand(a), operand(b),
                                          {"mult": ALU.mult, "add": ALU.add, "subtract": ALU.subtract}[op]))
            dve.wait_ge(s_lvl, pre[0])
            for q in range(NQ):
                lvl(dve.tensor_tensor(edge[:, 0, q], gate(cosine, 2, 0)[:, q], operand(ez[q][1]), ALU.mult))
                lvl(dve.tensor_tensor(edge[:, 1, q], gate(sine, 2, 0)[:, q], operand(ex[q][1]), ALU.mult))
            lvl(dve.memset(E[:], 1.0))
            dve.wait_ge(s_lvl, pre[0])
            for q in range(NQ):
                assert ez[q][0] == 1 and ex[q][0] == 1
                ins = dve.tensor_tensor(E[:, :, q], edge[:, 0, q], edge[:, 1, q], ALU.subtract)
            ins.then_inc(s_cir, 1)

            dve.wait_ge(s_cir, 1)
            dve.wait_ge(s_gm, 32)
            vn = [0]

            def vs(ins):
                ins.then_inc(s_v, 1)
                vn[0] += 1
                dve.wait_ge(s_v, vn[0])

            F1 = NQ + 1
            for g in range(F1):
                vs(dve.tensor_tensor(EU[:, min(g, 1)], E[:, :, g:g + 1].to_broadcast([P, NT, F1]),
                                     GMB[:, g, None, 0:F1].to_broadcast([P, NT, F1]), ALU.mult))
                if g:
                    vs(dve.tensor_tensor(EU[:, 0], EU[:, 0], EU[:, 1], ALU.add))
            vs(dve.tensor_tensor(EU[:, 0], EU[:, 0], E[:, :, 0:F1], ALU.mult))
            vs(dve.tensor_reduce(var[:, 0], EU[:, 0], AX.X, ALU.add))
            vs(dve.tensor_scalar(var[:, 1], var[:, 0], 0.0, EPS_LN, ALU.max, ALU.add))
            assert vn[0] == 2 * NQ + 4
            dve.wait_ge(s_sq, 1)
            vs(dve.reciprocal(var[:, 3], var[:, 2]))
            vs(dve.tensor_tensor(var[:, 4], var[:, 3], var[:, 3], ALU.mult))
            vs(dve.tensor_tensor(var[:, 4], var[:, 4], var[:, 1], ALU.mult))
            vs(dve.tensor_scalar(var[:, 4], var[:, 4], -0.5, 1.5, ALU.mult, ALU.add))
            vs(dve.tensor_tensor(var[:, 5], var[:, 3], var[:, 4], ALU.mult))
            vs(dve.memset(Ft[:, :, 7:8], 1.0))
            vs(dve.tensor_tensor(Ft[:, :, 0:7], E[:, :, 0:7],
                                 var[:, 5, :, None].to_broadcast([P, NT, 7]), ALU.mult))
            vs(dve.tensor_copy(Fp[:, 0], Ft[:]))
            vs(dve.tensor_tensor(Fr[:, 0], Ft[:], Fp[:, 0], ALU.subtract))
            vs(dve.tensor_copy(Fp[:, 1], Fr[:, 0]))
            vs(dve.tensor_tensor(Fr[:, 1], Fr[:, 0], Fp[:, 1], ALU.subtract))
            vs(dve.tensor_copy(Fp[:, 2], Fr[:, 1]))
            for u in range(2):
                for k, part in enumerate(TOKEN_PARTS):
                    ins = dve.tensor_scalar(FW[:, :, u, k, :], Fp[:, part], parity[:, u:u + 1], None, ALU.mult)
            ins.then_inc(s_fw, 1)
            for c in range(1, NT // 8, 2):
                dve.wait_ge(s_fx, c + 1)
                dve.tensor_copy(FX[:, c * 1024:(c + 1) * 1024],
                                pbank[0:KF, 2 + c % 2, :].bitcast(BF16)).then_inc(s_fe[1], 1)

        @block.sync
        def _(sp):
            sp.dma_start(ids[:], dram["ids"]).then_inc(s_ids, 16)
            for t, name in ((Wq, "Wq"), (Wk, "Wk"), (Wv, "Wv"), (Wpk, "Wpk"), (Wpq, "Wpq")):
                sp.dma_start(t[:], dram[name].rearrange("(c k) n -> k c n", c=KC)).then_inc(s_w, 16)
            sp.dma_start(cen[:], dram["centre"].rearrange("(c k) n -> k c n", c=KC)).then_inc(s_w, 16)
            sp.dma_start(post[:], dram["post"].rearrange("(c k) n -> k c n", c=KC)).then_inc(s_w, 16)
            sp.dma_start(relr[:], dram["rel_back"].rearrange("(c k) n -> k c n", c=KC)).then_inc(s_w, 16)
            sp.dma_start(relf[:], dram["rel_fore"].rearrange("(c k) n -> k c n", c=KC)).then_inc(s_w, 16)
            sp.dma_start(rows[:], dram["rows"]).then_inc(s_w, 16)
            sp.dma_start(ident[:], dram["ident"]).then_inc(s_w, 16)
            sp.dma_start(parity[:], dram["parity"]).then_inc(s_w, 16)
            sp.dma_start(hmask[:], dram["hmask"]).then_inc(s_w, 16)
            sp.dma_start(e7[:], dram["e7"]).then_inc(s_w, 16)
            sp.wait_ge(s_tv, TV["GM"])
            sp.dma_start(dram["gmD"], GM[:]).then_inc(s_gm, 16)
            sp.wait_ge(s_gm, 16)
            sp.dma_start(GMB[:].rearrange("p f g -> p (f g)"), dram["gmD"].rearrange("(a f) g -> a (f g)", a=1
                         ).to_broadcast([P, NF * NF])).then_inc(s_gm, 16)
            sp.wait_ge(s_tv, TV["tables"])
            for m in range(KC):
                sp.dma_start(dram["tabD"][m * 48:(m + 1) * 48], TP_[:, :, m]).then_inc(s_td, 16)
            sp.dma_start(dram["tabD"][96:104], TP_[40:48, :, KC - 1]).then_inc(s_td, 16)
            sp.wait_ge(s_tv, TV["gparts"])
            for u in range(2):
                for k, part in enumerate(TABLE_PARTS):
                    r0 = (u * NPR + k) * NF
                    sp.dma_start(GS[r0:r0 + NF, :], GP[:, part, :]).then_inc(s_gs, 16)
            for n in range(B // EQ):
                sp.wait_ge(s_ete, (n + 1) * EQ)
                q = n % (EB // EQ)
                sp.dma_start(dram["evT"][:, n * EQ * S:(n + 1) * EQ * S],
                             ET[:, q * EQ:(q + 1) * EQ].rearrange("f b n -> f (b n)")).then_inc(s_etd[q], 16)
            for q in range(EB // EQ):
                sp.wait_ge(s_etd[q], 16 * B // EB)
            sp.wait_ge(s_td, 16 * (KC + 1))
            sp.wait_ge(s_gs, 16 * 2 * NPR)

        @block.scalar
        def _(act):
            act.wait_ge(s_red, 8)
            act.activation(sn, ang, ACT.Sin).then_inc(s_sin, 1)
            act.activation(cs, trn, ACT.Sin).then_inc(s_sin, 1)
            for b in range(B):
                if b == 7:
                    act.wait_ge(s_v, 2 * NQ + 4)
                    act.activation(var[:, 2], var[:, 1], ACT.Sqrt).then_inc(s_sq, 1)
                act.wait_ge(s_et, b + 1)
                if b >= EB and b % EQ == 0:
                    act.wait_ge(s_etd[b % EB // EQ], 16 * (b // EB))
                act.activation(ET[:, b % EB, :], pbank[0:NF, 4 + b % 2, :], ACT.Copy).then_inc(s_ete, 1)
            for c in range(0, NT // 8, 2):
                act.wait_ge(s_fx, c + 1)
                act.activation(FX[:, c * 1024:(c + 1) * 1024],
                               pbank[0:KF, 2 + c % 2, :].bitcast(BF16), ACT.Copy).then_inc(s_fe[0], 1)

        @block.tensor
        def _(pe):
            pe.wait_ge(s_tv, TV["ones"])
            for m in range(KC):
                for c in range(KC):
                    mm = pe.matmul(pbank[0:96, 0, m * NF:(m + 1) * NF], cen[:, c, m * 96:(m + 1) * 96],
                                   post[:, c, :], start=(c == 0), stop=(c == KC - 1), skip_group_check=True)
            mm.then_inc(s_tab, 1)
            pe.wait_ge(s_tv, TV["CT"])
            for c in range(KC):
                pe.matmul(pbank[0:NF, 1, 480:488], CT[:, c, :], CT[:, c, :], start=(c == 0),
                          stop=(c == KC - 1), skip_group_check=True)
            for k, w in enumerate((Wq, Wk)):
                for m in range(KC):
                    out = pbank[0:96, 2, (k * KC + m) * NF:(k * KC + m + 1) * NF]
                    for c in range(KC):
                        pe.matmul(out, w[:, c, m * 96:(m + 1) * 96], CT[:, c, :], start=(c == 0),
                                  stop=False, skip_group_check=True)
                    pe.matmul(out, rows[0:1, k, m * 96:(m + 1) * 96], e7[0:1, :], start=False, stop=True,
                              skip_group_check=True)
            for k, (w, rel) in enumerate(((Wpk, relr), (Wpq, relf))):
                for m in range(KC):
                    out = pbank[0:96, 3 + 2 * k + m, 0:NR]
                    for c in range(KC):
                        pe.matmul(out, w[:, c, m * 96:(m + 1) * 96], rel[:, c, :], start=(c == 0),
                                  stop=False, skip_group_check=True)
                    mm = pe.matmul(out, rows[0:1, 3 + k, m * 96:(m + 1) * 96], ones[0:1, 0:NR], start=False,
                                   stop=True, skip_group_check=True)
            mm.then_inc(s_tab, 1)
            pe.wait_ge(s_tv, TV["blocks"])
            for k in range(2):
                for m in range(KC):
                    pe.matmul(pbank[0:48, 3 + 2 * k + m, 0:NR], WB[:, k, m].rearrange("p h f -> p (h f)"),
                              RT[:, k, m, :], start=True, stop=True, skip_group_check=True)
            for m in range(KC):
                for t in range(3):
                    out = pbank[0:NF, 0, 0:288].rearrange("p (h t f) -> p h t f", h=H, t=3)[
                        :, m * HC:(m + 1) * HC, t, :]
                    pe.matmul(out, WT[:, 0, m, :], KB[:, m, :, t, :], start=True, stop=(t == MID),
                              skip_group_check=True)
                    if t != MID:
                        pe.matmul(out, LQ[:, m, 0 if t == HI else 1, :], WB[:, 1, m], start=False, stop=True,
                                  skip_group_check=True)
            for c in range(KC):
                pe.matmul(pbank[0:NF, 1, 0:D], CT[:, c, :], Wv[:, c, :], start=(c == 0), stop=False,
                          skip_group_check=True)
            pe.matmul(pbank[0:NF, 1, 0:D], e7[0:1, :], rows[0:1, 2, :], start=False, stop=True,
                      skip_group_check=True).then_inc(s_tab, 1)

            pe.wait_ge(s_cir, 1)
            pe.wait_ge(s_tv, TV["gparts"])
            for b in range(B):
                if b >= 2:
                    pe.wait_ge(s_ete, b - 1)
                for k in range(IB):
                    mm = pe.transpose(pbank[0:NF, 4 + b % 2, k * P:(k + 1) * P], E[:, b * IB + k, :], ident[:])
                mm.then_inc(s_et, 1)
            pe.wait_ge(s_fw, 1)
            for c in range(NT // 8):
                if c >= 2:
                    pe.wait_ge(s_fe[c % 2], c // 2)
                for k in range(8):
                    mm = pe.transpose(pbank[0:KF, 2 + c % 2, :].bitcast(BF16)[:, k * P:(k + 1) * P],
                                      FW[:, c * 8 + k].rearrange("p u k f -> p (u k f)"), identb[:])
                mm.then_inc(s_fx, 1)


def batches(engine, unroll, stages, count=B):
    lag = max(lag for lag, _ in stages)
    lead = -(-lag // unroll) * unroll

    def rounds(first, last, base):
        for r in range(first, last):
            for late, stage in stages:
                c = r - late
                if base is None and not 0 <= c < count:
                    continue
                if base is None:
                    stage(c, c % unroll, c // unroll)
                else:
                    stage(base * unroll + c, c % unroll, base + c // unroll)

    rounds(0, lead, None)
    with engine.Fori(0, (count - lead) // unroll) as base:
        rounds(lead, lead + unroll, base)
    rounds(count, count + lag, None)


def key_tables_block(nc, dram, keep):
    GB = 4
    UNITS = 2 * B // GB
    with ExitStack() as ctx:
        gps = ctx.enter_context(nc.psum_tensor("gps", [96, 2, IB, GB * P], F32))
        parts = ctx.enter_context(nc.sbuf_tensor("gparts", [96, 2, 3, IB, GB * P], BF16))
        rest = ctx.enter_context(nc.sbuf_tensor("grest", [96, 2, IB, GB * P], F32))
        FX, GS = keep["FX"], keep["GS"]
        s_mm, s_hi, s_rest, s_mid = (ctx.enter_context(nc.semaphore(n)) for n in (
            "g_ready", "g_high", "g_rest", "g_middle"))
        s_low = [ctx.enter_context(nc.semaphore(n)) for n in ("g_low_by_vector", "g_low_by_gpsimd")]
        s_st = [ctx.enter_context(nc.semaphore(f"g_stored{k}")) for k in range(2)]
        s_go = ctx.enter_context(nc.semaphore("stores_begun"))
        block = ctx.enter_context(nc.Block())
        FOR_POOL = IB // 2

        @block.tensor
        def _(pe):
            def product(u, k, g):
                pe.wait_ge(s_rest, u + 1)
                for i in range(IB):
                    at = (0 if i < IB // 2 else 192) + 96 * k
                    mm = pe.matmul(gps[:, k, i], GS[0:KF, at:at + 96],
                                   FX[0:KF, :].rearrange("k (b i p) -> k b i p", b=B, i=IB)[
                                       :, bass.ds(g * GB, GB), i, :], start=True, stop=True)
                mm.then_inc(s_mm, 1)

            batches(pe, 2, [(0, product)], UNITS)

        @block.scalar
        def _(act):
            def high(u, k, g):
                act.wait_ge(s_mm, u + 1)
                act.wait_ge(s_st[k], g * 48 + 48)
                act.activation(parts[:, k, 0], gps[:, k], ACT.Copy).then_inc(s_hi, 1)

            def middle(u, k, g):
                act.wait_ge(s_rest, u + 3)
                act.activation(parts[:, k, 1], rest[:, k], ACT.Copy).then_inc(s_mid, 1)

            batches(act, 2, [(0, high), (1, middle)], UNITS)

        @block.vector
        def _(dve):
            def subtract_high(u, k, g):
                dve.wait_ge(s_hi, u + 1)
                dve.wait_ge(s_low[1], u + 1)
                dve.tensor_tensor(rest[:, k], gps[:, k], parts[:, k, 0], ALU.subtract).then_inc(s_rest, 1)

            def low(u, k, g):
                dve.wait_ge(s_mid, u + 1)
                dve.tensor_tensor(parts[:, k, 2, FOR_POOL:], rest[:, k, FOR_POOL:], parts[:, k, 1, FOR_POOL:],
                                  ALU.subtract).then_inc(s_low[0], 1)

            dve.sem_inc(s_rest, 2)
            batches(dve, 2, [(0, subtract_high), (1, low)], UNITS)

        @block.gpsimd
        def _(pool):
            def low(u, k, g):
                pool.wait_ge(s_mid, u + 1)
                pool.tensor_tensor(parts[:, k, 2, 0:FOR_POOL], rest[:, k, 0:FOR_POOL], parts[:, k, 1, 0:FOR_POOL],
                                   ALU.subtract).then_inc(s_low[1], 1)

            pool.sem_inc(s_low[1], 2)
            batches(pool, 2, [(0, low)], UNITS)

        @block.sync
        def _(sp):
            def store(u, k, g):
                rows = dram["gD"].rearrange("s i h c t b p -> (h c t) s i (b p)")[k * 96:(k + 1) * 96]
                for part in range(3):
                    if part < 2:
                        sp.wait_ge((s_hi, s_mid)[part], u + 1)
                    else:
                        sp.wait_ge(s_low[0], u + 1)
                        sp.sem_inc(s_go, 1)
                        sp.wait_ge(s_low[1], u + 3)
                    sp.sem_inc(s_go, 1)
                    sp.dma_start(rows[:, part, :, bass.ds(g * (GB * P), GB * P)],
                                 parts[:, k, part]).then_inc(s_st[k], 16)

            for k in range(2):
                sp.sem_inc(s_st[k], 48)
            batches(sp, 2, [(0, store)], UNITS)
            for k in range(2):
                sp.wait_ge(s_st[k], 48 + 48 * UNITS // 2)


def attention_block(nc, dram, keep):
    UB = B
    UH = IB * UB
    SB, XR, TB_, PR, OB = 3, 4, 2, 8, 2
    CH = [4 * len(beside(ib)) for ib in range(IB)]
    CHH = 1 + sum(CH)
    AHEAD = CH[0]
    VALUES = 5
    with ExitStack() as ctx:
        def sb(name, shape, dt=F32):
            return ctx.enter_context(nc.sbuf_tensor(name, shape, dt))

        ident, FX = keep["ident"], keep["FX"]
        WV = keep["GS"][0:KF, 384:576]
        TT = sb("TT", [KF, 2, 512], BF16)
        gB = sb("gB", [KF, 2, 2, B * P], BF16)
        XP = sb("XP", [P, 2, 3, B, P])
        XQ = sb("XQ", [P, 2, XQ_LEN])
        Vh = sb("Vh", [P, NT, 2 * DH])
        X = sb("X", [P, XR, S])
        mx = sb("mx", [P, XR])
        PT = sb("PT", [P, PR, S])
        OT = sb("OT", [P, OB, P])
        SC = ctx.enter_context(nc.psum_tensor("SC", [P, SB, S], F32))
        TU = ctx.enter_context(nc.psum_tensor("TU", [P, TB_, S], F32))
        BI = ctx.enter_context(nc.psum_tensor("BI", [P, 2, S], F32))
        OV = ctx.enter_context(nc.psum_tensor("OV", [P, S], F32))

        def sem(name):
            return ctx.enter_context(nc.semaphore(name))

        s_tt, s_z = sem("tables_loaded"), sem("zeros_ready")
        s_g = [sem("g_loaded_even"), sem("g_loaded_odd")]
        s_bias = [sem("key_bias_ready"), sem("query_bias_ready")]
        s_biased = [sem("key_bias_copied"), sem("query_bias_copied")]
        s_sc = sem("scores_ready")
        s_sum = sem("scores_summed")
        s_sh = sem("scores_shifted")
        s_tu = sem("scores_turned")
        s_ex = sem("exps_ready")
        s_pv = sem("values_summed")
        s_ov = sem("outputs_copied")
        s_go = sem("sums_begun")
        s_od = [sem(f"outputs_stored{i}") for i in range(OB)]

        block = ctx.enter_context(nc.Block())

        def chunks(ib):
            return [(jb - ib + 1, jb, jq) for jb in beside(ib) for jq in range(4)]

        def chunk_base(ib):
            return 1 + sum(CH[1:ib]) if ib else 1 + sum(CH[1:])

        TURN, OUT = 3, 9
        LEAD = OUT + 4
        STEPS = UH + LEAD

        def heads(engine, step):
            for s in range(LEAD):
                step([(0, s)])
            with engine.Fori(0, H - 1) as h:
                for s in range(LEAD, STEPS):
                    step([(h, s)] if s < UH else [(h, s), (h + 1, s - UH)])
            for s in range(LEAD, STEPS):
                step([(H - 1, s)])

        def chunk_at(s):
            if s >= UH:
                return None
            ib = s // UB
            nxt = (ib + 1) % IB
            c = s % UB
            if c >= CH[nxt]:
                return None
            return nxt, c, chunk_base(nxt) + c - (1 if nxt == 1 and c < VALUES else 0)

        @block.sync
        def _(sp):
            def load_tables(h):
                for u in range(2):
                    for part, k0, n in ((0, 0, 3), (1, 3, 2), (2, 5, 1)):
                        for k in range(k0, k0 + n):
                            r0 = (u * NPR + k) * NF
                            sp.dma_start(TT[r0:r0 + NF], dram["tabD"][bass.ds(h * NF, NF), part, :, 1 - u:513 - u]
                                         ).then_inc(s_tt, 16)

            def load_g(h, ib):
                for u in range(2):
                    for part, k0, n in ((0, 0, 3), (1, 3, 2), (2, 5, 1)):
                        for k in range(k0, k0 + n):
                            r0 = (u * NPR + k) * NF
                            sp.dma_start(gB[r0:r0 + NF, ib % 2],
                                         dram["gD"][part, ib, h].rearrange("c t b p -> c t (b p)")
                                         ).then_inc(s_g[ib % 2], 16)

            def store(h, q):
                sp.wait_ge(s_ov, h * (UH // 4) + (q + 1 + OB))
                ib, b0 = q // 4, 4 * (q % 4)
                sp.dma_start(dram["otD"].rearrange("h r b n -> h b r n")[h, b0:b0 + 4, :, ib * P:(ib + 1) * P],
                             OT[:, q % OB, :]).then_inc(s_od[q % OB], 16)

            def head(h, last):
                for ib in range(IB):
                    if ib == 2:
                        for k in range(2):
                            sp.wait_ge(s_bias[k], h * CHH + (AHEAD + chunk_base(3) + CH[3]))
                        load_tables(h + 1)
                    for q in range(4 * ib, 4 * ib + 4):
                        store(h, q)
                    if ib < 2 or not last:
                        sp.wait_ge(s_sc, h * UH + (ib + 1) * UB)
                        load_g(h + (ib + 2) // IB, (ib + 2) % IB)

            for i in range(OB):
                sp.sem_inc(s_od[i], 16)
            load_tables(0)
            load_g(0, 0)
            load_g(0, 1)
            with sp.Fori(0, H - 1) as h:
                head(h, False)
            head(H - 1, True)
            for i in range(OB):
                sp.wait_ge(s_od[i], 16 * (1 + H * UH // 4 // OB))

        @block.gpsimd
        def _(pool):
            for k in range(2):
                pool.memset(XQ[:, k, 0:2 * P], 0.0).then_inc(s_z, 1)
                pool.memset(XQ[:, k, 2 * P:].rearrange("p (b n) -> p b n", b=B)[:, :, 3 * P:], 0.0).then_inc(s_z, 1)
            pool.memset(Vh[:, :, DH:], 1.0).then_inc(s_z, 1)
            with pool.Fori(0, H) as h:
                for s in range(UH):
                    pool.wait_ge(s_sum, h * UH + (s + 1 + SB))
                    pool.tensor_tensor(X[:, s % XR, :], X[:, s % XR, :],
                                       mx[:, s % XR:s % XR + 1].to_broadcast([P, S]),
                                       ALU.subtract).then_inc(s_sh, 1)

        def bias_out(kind, ib, c):
            rel, jb, jq = chunks(ib)[c]
            if kind == 0:
                return XP[:, ib % 2, rel, :, jq * 32:(jq + 1) * 32]
            o = 2 * P + rel * P + jq * 32
            return XQ[:, ib % 2, 2 * P:].rearrange("p (b n) -> p b n", b=B)[:, :, o - 2 * P:o - 2 * P + 32]

        @block.scalar
        def _(act):
            act.sem_inc(s_biased[0], 1)
            act.sem_inc(s_ex, TB_)
            act.sem_inc(s_ov, OB)

            def copy_bias(count, ib, c):
                act.wait_ge(s_bias[0], count + 1)
                act.activation(bias_out(0, ib, c), BI[:, 0, :].rearrange("p (b n) -> p b n", b=B),
                               ACT.Copy).then_inc(s_biased[0], 1)

            def step(at):
                for h, s in at:
                    if s == VALUES:
                        act.wait_ge(s_bias[0], h * CHH + (AHEAD + VALUES + 1))
                        act.wait_ge(s_pv, h * (UH // 4) + PR // 4)
                        act.activation(Vh[:, 0:NT // 2, 0:DH], BI[:, 0, :].rearrange("p (t d) -> p t d", d=DH),
                                       ACT.Copy).then_inc(s_biased[0], 1)
                    if chunk_at(s):
                        ib, c, n = chunk_at(s)
                        copy_bias(h * CHH + (AHEAD + n), ib, c)
                for h, s in at:
                    u = s - TURN
                    if 0 <= u < UH:
                        act.wait_ge(s_tu, h * UH + (u + 1 + XR))
                        act.wait_ge(s_pv, h * (UH // 4) + (u // 4 + 1))
                        act.activation(PT[:, u % PR, :], TU[:, u % TB_, :], ACT.Exp, scale=SCALE).then_inc(s_ex, 1)
                    if s >= OUT and (s - OUT) % 4 == 0 and (s - OUT) // 4 < UH // 4:
                        q = (s - OUT) // 4
                        act.wait_ge(s_pv, h * (UH // 4) + (q + 1 + PR // 4))
                        act.wait_ge(s_od[q % OB], (h * (UH // 4 // OB) + (q // OB + 1)) * 16)
                        act.activation(OT[:, q % OB, :], OV[:, 0:P], ACT.Copy).then_inc(s_ov, 1)

            for c in range(AHEAD):
                copy_bias(c, 0, c)
            heads(act, step)

        @block.vector
        def _(dve):
            dve.sem_inc(s_biased[1], 1)
            dve.sem_inc(s_sum, SB)
            dve.wait_ge(s_z, 5)

            def copy_bias(count, ib, c):
                dve.wait_ge(s_bias[1], count + 1)
                dve.tensor_copy(bias_out(1, ib, c),
                                BI[:, 1, :].rearrange("p (b n) -> p b n", b=B)).then_inc(s_biased[1], 1)

            for c in range(AHEAD):
                copy_bias(c, 0, c)
            def step(at):
                for h, s in at:
                    if s == VALUES:
                        dve.wait_ge(s_bias[1], h * CHH + (AHEAD + VALUES + 1))
                        dve.wait_ge(s_pv, h * (UH // 4) + PR // 4)
                        dve.tensor_copy(Vh[:, NT // 2:, 0:DH],
                                        BI[:, 1, :].rearrange("p (t d) -> p t d", d=DH)).then_inc(s_biased[1], 1)
                    if s >= UH:
                        continue
                    ib, b = s // UB, s % UB
                    if b == 0:
                        n = 0 if ib == 0 else chunk_base(ib) + CH[ib]
                        dve.wait_ge(s_biased[1], h * CHH + (AHEAD + n + 1))
                        dve.wait_ge(s_sum, h * UH + (s + SB))
                    dve.wait_ge(s_sc, h * UH + (s + 1))
                    dve.wait_ge(s_tu, h * UH + (s + 1))
                    dve.sem_inc(s_go, 1)
                    o = XQ_PITCH * b + 3 * P - P * ib
                    dve.tensor_tensor_reduce(X[:, s % XR, :], SC[:, s % SB, :], XQ[:, ib % 2, o:o + S],
                                             1.0, -3.0e38, ALU.add, ALU.max,
                                             mx[:, s % XR:s % XR + 1]).then_inc(s_sum, 1)
                    if chunk_at(s):
                        nib, c, n = chunk_at(s)
                        copy_bias(h * CHH + (AHEAD + n), nib, c)

            heads(dve, step)

        @block.tensor
        def _(pe):
            pe.sem_inc(s_tu, XR)
            pe.sem_inc(s_pv, PR // 4)

            def bias(kind, count, ib, c):
                rel, jb, jq = chunks(ib)[c]
                pe.wait_ge(s_biased[kind], count + 1)
                out = BI[:, kind, :].rearrange("p (b n) -> p b n", b=B)
                own, other = (jb, ib) if kind == 0 else (ib, jb)
                for g in range(16):
                    at = other * P + jq * 32 + 2 * g
                    w = 256 - (at - own * P)
                    mm = pe.matmul(out[:, :, 2 * g:2 * g + 2], TT[:, kind, w:w + P],
                                   FX[0:KF, :].rearrange("k (b n) -> k b n", b=B)[:, :, at:at + 2],
                                   start=(g == 0), stop=(g == 15), skip_group_check=True)
                mm.then_inc(s_bias[kind], 1)

            def values(h):
                for half in range(2):
                    pe.wait_ge(s_biased[half], h * CHH + (AHEAD + VALUES + 1))
                    for t in range(NT // 2):
                        tile = half * NT // 2 + t
                        mm = pe.matmul(BI[:, half, t * DH:(t + 1) * DH], FX[0:KF, tile * P:(tile + 1) * P],
                                       WV[:, bass.ds(h * DH, DH)], start=(t == 0), stop=(t == NT // 2 - 1),
                                       skip_group_check=True)
                    mm.then_inc(s_bias[half], 1)

            def score(h, s):
                ib, b = s // UB, s % UB
                if b == 0:
                    n = 0 if ib == 0 else chunk_base(ib) + CH[ib]
                    pe.wait_ge(s_biased[0], h * CHH + (AHEAD + n + 1))
                    pe.wait_ge(s_g[ib % 2], (h * (IB // 2) + (ib // 2 + 1)) * (16 * 2 * NPR))
                pe.wait_ge(s_sum, h * UH + (s + 1 if s else SB))
                near = beside(ib)
                for i, jb in enumerate(near):
                    pe.matmul(SC[:, s % SB, jb * P:(jb + 1) * P], XP[:, ib % 2, jb - ib + 1, b, :], ident[:],
                              start=(i == 0), stop=False, is_transpose=True, skip_group_check=True)
                runs = [(HI, 0, near[0]), (LO, near[-1] + 1, IB), (MID, near[0], near[-1] + 1)]
                for t, j0, j1 in runs:
                    if j0 < j1:
                        slot = t - (MID if ib < IB // 2 else HI)
                        mm = pe.matmul(SC[:, s % SB, j0 * P:j1 * P], gB[:, ib % 2, slot, b * P:(b + 1) * P],
                                       FX[0:KF, b * S + j0 * P:b * S + j1 * P], start=False, stop=(t == MID),
                                       skip_group_check=True)
                mm.then_inc(s_sc, 1)

            def turn(h, u):
                pe.wait_ge(s_sh, h * UH + (u + 1))
                pe.wait_ge(s_ex, h * UH + (u + 1))
                for jb in range(IB):
                    mm = pe.transpose(TU[:, u % TB_, jb * P:(jb + 1) * P], X[:, u % XR, jb * P:(jb + 1) * P],
                                      ident[:])
                mm.then_inc(s_tu, 1)

            def sum_values(h, q):
                if q == 0:
                    for half in range(2):
                        pe.wait_ge(s_biased[half], h * CHH + (AHEAD + VALUES + 2))
                pe.wait_ge(s_ex, h * UH + (4 * q + 4 + TB_))
                pe.wait_ge(s_ov, h * (UH // 4) + (q + OB))
                for jb in range(IB):
                    for k in range(4):
                        u = 4 * q + k
                        mm = pe.matmul(OV[32 * k:32 * (k + 1), 0:P], Vh[:, (u % UB) * IB + jb, :],
                                       PT[:, u % PR, jb * P:(jb + 1) * P], start=(jb == 0), stop=(jb == IB - 1),
                                       skip_group_check=True)
                mm.then_inc(s_pv, 1)

            pe.wait_ge(s_tt, 16 * 2 * NPR)
            for c in range(AHEAD):
                for kind in range(2):
                    bias(kind, c, 0, c)
            def step(at):
                for h, s in at:
                    if s < UH:
                        score(h, s)
                    if s == 3 * UB:
                        pe.wait_ge(s_tt, (h + 2) * (16 * 2 * NPR))
                    if s == VALUES:
                        values(h)
                    if chunk_at(s):
                        ib, c, n = chunk_at(s)
                        bias(0, h * CHH + (AHEAD + n), ib, c)
                for h, s in at:
                    if TURN <= s < UH + TURN:
                        turn(h, s - TURN)
                for h, s in at:
                    if chunk_at(s):
                        ib, c, n = chunk_at(s)
                        bias(1, h * CHH + (AHEAD + n), ib, c)
                for h, s in at:
                    q = (s - OUT + 1) // 4
                    if (s - OUT + 1) % 4 == 0 and 0 <= q < UH // 4:
                        sum_values(h, q)

            heads(pe, step)


def sums_block(nc, dram):
    with ExitStack() as ctx:
        sums = ctx.enter_context(nc.sbuf_tensor("sums", [96, 2, S], F32))
        over = ctx.enter_context(nc.sbuf_tensor("over", [96, 2, S], F32))
        s_ld, s_ov, s_st = (ctx.enter_context(nc.semaphore(n)) for n in ("sums_loaded", "sums_inverted", "over_stored"))
        block = ctx.enter_context(nc.Block())

        @block.sync
        def _(sp):
            sp.dma_start(sums[:], dram["otD"][:, DH].rearrange("h (p c) n -> h p c n", c=2)).then_inc(s_ld, 16)
            sp.wait_ge(s_ov, 1)
            sp.dma_start(dram["overD"].rearrange("(p c) n -> p c n", c=2), over[:]).then_inc(s_st, 16)
            sp.wait_ge(s_st, 16)

        @block.vector
        def _(dve):
            dve.wait_ge(s_ld, 16)
            dve.reciprocal(over[:], sums[:]).then_inc(s_ov, 1)


def residual_block(nc, dram, keep):
    H1, stats = keep["H1"], keep["stats"]
    U = 4
    with ExitStack() as ctx:
        def sb(name, shape, dt=F32):
            return ctx.enter_context(nc.sbuf_tensor(name, shape, dt))

        def sem(name):
            return ctx.enter_context(nc.semaphore(name))

        Wo = sb("Wo", [96 + NF, KC, D])
        O, R = sb("O", [96, KC, U, S]), sb("R", [96, KC, U, S])
        ON = sb("ON", [96 + NF, KC, U, S])
        bn, agg = sb("bn", [P, U, IB, 6]), sb("agg", [P, U, IB, 2])
        ph = ctx.enter_context(nc.psum_tensor("ph", [P, 2, 2, 512], F32))
        s_w, s_h = sem("out_weights"), sem("h1_ready")
        s_on = [sem("heads_scaled_by_vector"), sem("heads_scaled_by_gpsimd")]
        s_in = [sem(f"heads_loaded{k}") for k in range(U // 2)]
        s_hc, s_bn, s_ag, s_st = sem("h1_copied"), sem("bn_ready"), sem("bn_done"), sem("stats_kept")
        s_go = sem("aggregates_begun")
        block = ctx.enter_context(nc.Block())
        NL = 16 * (2 * KC + 1)

        @block.sync
        def _(sp):
            sp.dma_start(Wo[0:96], dram["Wo"].rearrange("(c k) n -> k c n", c=KC)).then_inc(s_w, 16)
            sp.dma_start(Wo[96:96 + NF, 1, :], dram["post_rows"]).then_inc(s_w, 16)

            def load(b, k, g):
                if k % 2:
                    return
                sp.wait_ge(s_h, b + 2)
                for c in range(KC):
                    sp.dma_start(O[:, c, k:k + 2], dram["otD"][c * HC:(c + 1) * HC, 0:DH, bass.ds(b, 2), :]
                                 ).then_inc(s_in[k // 2], 16)
                    sp.dma_start(R[:, c, k:k + 2], dram["overD"].rearrange("(h b) n -> h b n", h=H)[
                        c * HC:(c + 1) * HC, None, bass.ds(b, 2), :].to_broadcast([HC, DH, 2, S])
                                 ).then_inc(s_in[k // 2], 16)
                sp.dma_start(ON[96:96 + NF, 1, k:k + 2], dram["evT"].rearrange("f (b n) -> f b n", b=B)[
                    :, bass.ds(b, 2)]).then_inc(s_in[k // 2], 16)

            batches(sp, U, [(0, load)])

        @block.gpsimd
        def _(pool):
            def scale(b, k, g):
                pool.wait_ge(s_in[k // 2], g * NL + NL)
                pool.wait_ge(s_h, b + 1)
                pool.tensor_tensor(ON[0:96, 0, k], O[:, 0, k], R[:, 0, k], ALU.mult).then_inc(s_on[1], 1)

            batches(pool, U, [(0, scale)])

        @block.vector
        def _(dve):
            def scale(b, k, g):
                dve.wait_ge(s_in[k // 2], g * NL + NL)
                dve.wait_ge(s_h, b + 1)
                dve.tensor_tensor(ON[0:96, 1, k], O[:, 1, k], R[:, 1, k], ALU.mult).then_inc(s_on[0], 1)

            def spread(b, k, g):
                dve.wait_ge(s_hc, b + 3)
                dve.wait_ge(s_ag, b * IB + IB)
                for i in range(IB):
                    dve.bn_stats(bn[:, k, i], H1[:, bass.ds(b * IB + i, 1), :].rearrange("p a n -> p (a n)")
                                 ).then_inc(s_bn, 1)

            def aggregate(b, k, g):
                dve.wait_ge(s_bn, b * IB + IB)
                dve.wait_ge(s_st, b + 1)
                dve.sem_inc(s_go, 1)
                for i in range(IB):
                    dve.bn_aggr(agg[:, k, i], bn[:, k, i]).then_inc(s_ag, 1)

            def store(b, k, g):
                dve.wait_ge(s_ag, b * IB + (U + 1) * IB)
                dve.tensor_copy(stats[:, bass.ds(b * IB, IB), :], agg[:, k]).then_inc(s_st, 1)

            dve.sem_inc(s_st, U)
            dve.sem_inc(s_ag, U * IB)
            batches(dve, U, [(0, scale), (3, store), (2, aggregate), (1, spread)])

        @block.scalar
        def _(act):
            def copy(b, k, g):
                act.wait_ge(s_h, b + (U + 1))
                act.activation(H1[:, bass.ds(b * IB, IB), :].rearrange("p (a i) n -> p a i n", a=2),
                               ph[:, k % 2, :, 0:2 * D].rearrange("p a (i n) -> p a i n", i=2),
                               ACT.Copy).then_inc(s_hc, 1)

            act.sem_inc(s_hc, 2)
            batches(act, U, [(0, copy)])

        @block.tensor
        def _(pe):
            def project(b, k, g):
                for half in range(2):
                    pe.wait_ge(s_on[half], b + 1)
                pe.wait_ge(s_hc, b + 1)
                for i in range(IB):
                    out = ph[:, k % 2, i // 2, (i % 2) * D:(i % 2 + 1) * D]
                    pe.matmul(out, ON[0:96, 0, k, i * P:(i + 1) * P], Wo[0:96, 0, :], start=True, stop=False,
                              skip_group_check=True)
                    mm = pe.matmul(out, ON[:, 1, k, i * P:(i + 1) * P], Wo[:, 1, :], start=False, stop=True,
                                   skip_group_check=True)
                mm.then_inc(s_h, 1)

            pe.sem_inc(s_h, U)
            pe.wait_ge(s_w, 32)
            batches(pe, U, [(0, project)])


def experts_block(nc, dram, keep):
    H1, stats, CTA, ident, XTL = keep["H1"], keep["stats"], keep["CTA"], keep["ident"], keep["XTL"]
    U = 4
    with ExitStack() as ctx:
        def sb(name, shape, dt=F32):
            return ctx.enter_context(nc.sbuf_tensor(name, shape, dt))

        def ps(name, shape):
            return ctx.enter_context(nc.psum_tensor(name, shape, F32))

        def sem(name):
            return ctx.enter_context(nc.semaphore(name))

        slot, sq, SP = sb("slot", [96, KC, NS]), sb("sq", [96, KC, NS]), sb("SP", [96, KC, NS])
        scale, nrm = sb("scale", [96, 1]), sb("nrm", [96, 5, KC, SLOT])
        tok = sb("tok", [P, 6, NT])
        XN = sb("XN", [P, U, IB, D])
        XT = sb("XT", [96, 2, KC, S])
        DT, DN = sb("DT", [NS, 2, S]), sb("DN", [NS, 2, S])
        dm = sb("dm", [NS, U, 4])
        DK = sb("DK", [P, 2, IB, NS])
        C0, C1, C2 = (sb(f"C{i}", [P, 2, IB, NS]) for i in range(3))
        cm = sb("cm", [P, U, 3, IB])
        pX = ps("pX", [96, KC, S])
        pL = ps("pL", [NS, 2, S])
        pC = ps("pC", [P, IB, NS])
        LS = sb("LS", [NS, 2, S])
        pD = ps("pD", [P, IB, NS])
        pT = ps("pT", [P, P])
        pS = ps("pS", [96, KC, NS])
        Wd, Wu, bd, bu = (keep[k] for k in ("Wd", "Wu", "bd", "bu"))
        s_ew = sem("expert_weights")
        s_w, s_sp, s_rt = sem("slots_loaded"), sem("slot_steps"), sem("roots")
        s_xn, s_xt = sem("x_normed"), sem("x_turned")
        s_xc = [sem("x_copied_by_scalar"), sem("x_copied_by_vector")]
        s_ls, s_lt = sem("logits_copied"), sem("logits_turned")
        s_lg, s_dm, s_cm = sem("logits"), sem("dispatch_steps"), sem("combine_steps")
        s_de, s_ce = sem("dispatch_exp"), sem("combine_exp")
        s_dn, s_cn = sem("dispatch_scaled"), sem("combine_scaled")
        s_tn, s_dk, s_cc = sem("both_turned"), sem("dispatch_copied"), sem("combine_copied")
        s_go = sem("turns_begun")
        s_s, s_sc = sem("slots_summed"), sem("slots_copied")
        block = ctx.enter_context(nc.Block())

        @block.sync
        def _(sp):
            sp.dma_start(slot[:], dram["slots"].rearrange("(c k) n -> k c n", c=KC)).then_inc(s_w, 16)
            sp.dma_start(scale[:], dram["scale"].to_broadcast([96, 1])).then_inc(s_w, 16)
            for c in range(KC):
                sp.dma_start(Wd[:, c], dram["Wd"].rearrange("e (c k) h -> c k e h", c=KC)[c]).then_inc(s_ew, 16)
            sp.dma_start(Wu[:], dram["Wu"].rearrange("e h d -> h e d")).then_inc(s_ew, 16)
            with nc.allow_non_contiguous_dma(reason="192 biases"):
                sp.dma_start(bd[:], dram["bd"].rearrange("e h -> h e")).then_inc(s_ew, 16)
            sp.dma_start(bu[:], dram["bu"].rearrange("(a e) d -> a e d", a=1)).then_inc(s_ew, 16)
            sp.wait_ge(s_ew, 16 * (KC + 3))

        TVN = {}

        @block.vector
        def _(dve):
            n = [0]

            def st(ins):
                ins.then_inc(s_sp, 1)
                n[0] += 1
                dve.wait_ge(s_sp, n[0])

            st(dve.tensor_scalar(tok[:, 0], stats[:, :, 1], float(D), None, ALU.mult))
            st(dve.tensor_scalar(tok[:, 1], stats[:, :, 1], EPS_LN, None, ALU.add))
            TVN["var"] = n[0]
            dve.wait_ge(s_w, 32)
            st(dve.tensor_tensor(sq[:], slot[:], slot[:], ALU.mult))
            st(dve.tensor_reduce(nrm[:, 0], sq[:].rearrange("k c (e s) -> k c s e", e=EXP), AX.X, ALU.add))
            TVN["sq"] = n[0]
            dve.wait_ge(s_rt, 2)
            st(dve.tensor_scalar(tok[:, 4], tok[:, 3], EPS_L2, None, ALU.mult))
            st(dve.tensor_tensor(tok[:, 4], tok[:, 4], tok[:, 2], ALU.add))
            st(dve.reciprocal(tok[:, 5], tok[:, 4]))
            TVN["tok"] = n[0]
            dve.wait_ge(s_rt, 3)
            st(dve.tensor_scalar(nrm[:, 2], nrm[:, 1], EPS_L2, None, ALU.add))
            st(dve.reciprocal(nrm[:, 3], nrm[:, 2]))
            st(dve.tensor_scalar(nrm[:, 4], nrm[:, 3], scale[:, 0:1], None, ALU.mult))
            for c in range(KC):
                st(dve.tensor_tensor(SP[:, c].rearrange("k (e s) -> k e s", e=EXP),
                                     slot[:, c].rearrange("k (e s) -> k e s", e=EXP),
                                     nrm[:, 4, c, None, :].to_broadcast([96, EXP, SLOT]), ALU.mult))
            TVN["SP"] = n[0]

            def copy_x(b, k, g):
                dve.wait_ge(s_xt, b + 1)
                dve.wait_ge(s_lg, b + 1)
                dve.tensor_copy(XT[:, k % 2, 1], pX[:, 1, :]).then_inc(s_xc[1], 1)

            def softmax(b, k, g):
                k2 = k % 2
                dve.wait_ge(s_ls, b + 3)
                dve.tensor_reduce(dm[:, k, 0:1], LS[:, k2], AX.X, ALU.max).then_inc(s_dm, 1)
                dve.wait_ge(s_dm, b * 3 + 1)
                dve.tensor_scalar(dm[:, k, 1:2], dm[:, k, 0:1], -1.0, None, ALU.mult).then_inc(s_dm, 1)
                dve.wait_ge(s_lt, b + 3)
                dve.tensor_reduce(cm[:, k, 0], pC[:], AX.X, ALU.max).then_inc(s_cm, 1)
                dve.wait_ge(s_cm, b * 4 + 5)
                dve.wait_ge(s_ce, b + 1)
                dve.tensor_tensor(C0[:, k2], pC[:], cm[:, k, 0, :, None].to_broadcast([P, IB, NS]),
                                  ALU.subtract).then_inc(s_cm, 1)

            def finish(b, k, g):
                k2 = k % 2
                dve.wait_ge(s_de, b + 3)
                dve.reciprocal(dm[:, k, 3:4], dm[:, k, 2:3]).then_inc(s_dm, 1)
                dve.wait_ge(s_dm, b * 3 + 3)
                dve.wait_ge(s_tn, b + 1)
                dve.tensor_scalar(DN[:, k2], DT[:, k2], dm[:, k, 3:4], None, ALU.mult).then_inc(s_dn, 1)
                dve.wait_ge(s_ce, b + 3)
                dve.tensor_reduce(cm[:, k, 1], C1[:, k2], AX.X, ALU.add).then_inc(s_cm, 1)
                dve.wait_ge(s_cm, b * 4 + 7)
                dve.reciprocal(cm[:, k, 2], cm[:, k, 1]).then_inc(s_cm, 1)
                dve.wait_ge(s_cm, b * 4 + 8)
                dve.tensor_tensor(C2[:, k2], C1[:, k2], cm[:, k, 2, :, None].to_broadcast([P, IB, NS]),
                                  ALU.mult).then_inc(s_cn, 1)

            def copy_dispatch(b, k, g):
                dve.wait_ge(s_tn, b + 3)
                dve.wait_ge(s_s, b + U - 1)
                dve.tensor_copy(DK[:, k % 2], pD[:]).then_inc(s_dk, 1)

            def normalise(b, k, g):
                dve.wait_ge(s_s, b + 1)
                for i in range(IB):
                    t = bass.ds(b * IB + i, 1)
                    dve.tensor_scalar(XN[:, k, i], H1[:, t, :].rearrange("p a n -> p (a n)"),
                                      stats[:, t, 0:1].rearrange("p a n -> p (a n)"),
                                      tok[:, 5, t], ALU.subtract, ALU.mult).then_inc(s_xn, 1)

            dve.sem_inc(s_dk, 1)
            dve.sem_inc(s_dn, 2)
            dve.sem_inc(s_cn, 2)
            dve.sem_inc(s_cm, 4)
            dve.sem_inc(s_xc[1], 1)
            batches(dve, U, [(0, normalise), (2, finish), (3, copy_dispatch), (1, softmax), (0, copy_x)])

        @block.scalar
        def _(act):
            act.wait_ge(s_sp, TVN["var"])
            act.activation(tok[:, 2], tok[:, 0], ACT.Sqrt).then_inc(s_rt, 1)
            act.activation(tok[:, 3], tok[:, 1], ACT.Sqrt).then_inc(s_rt, 1)
            act.wait_ge(s_sp, TVN["sq"])
            act.activation(nrm[:, 1], nrm[:, 0], ACT.Sqrt).then_inc(s_rt, 1)

            def copy_x(b, k, g):
                act.wait_ge(s_xt, b + 1)
                act.wait_ge(s_lg, b + 1)
                act.activation(XT[:, k % 2, 0], pX[:, 0, :], ACT.Copy).then_inc(s_xc[0], 1)

            def copy_logits(b, k, g):
                act.wait_ge(s_lg, b + 3)
                act.wait_ge(s_lt, b + 1)
                act.activation(LS[:, k % 2], pL[:, k % 2], ACT.Copy).then_inc(s_ls, 1)

            def exps(b, k, g):
                act.wait_ge(s_dm, b * 3 + 2)
                act.wait_ge(s_dn, b + 1)
                act.activation(DT[:, k % 2], LS[:, k % 2], ACT.Exp, bias=dm[:, k, 1:2],
                               accum_out=dm[:, k, 2:3]).then_inc(s_de, 1)
                act.wait_ge(s_cm, b * 4 + 6)
                act.wait_ge(s_cn, b + 1)
                act.activation(C1[:, k % 2], C0[:, k % 2], ACT.Exp).then_inc(s_ce, 1)

            def copy_combine(b, k, g):
                act.wait_ge(s_tn, b + 3)
                act.activation(CTA[:, bass.ds(b * P, P)], pT[:], ACT.Copy).then_inc(s_cc, 1)

            def copy_slots(b, k, g):
                act.wait_ge(s_s, b + (U + 1))
                act.activation(XTL[:, :, bass.ds(b, 1), :],
                               pS[:].rearrange("p c (a n) -> p c a n", a=1), ACT.Copy).then_inc(s_sc, 1)

            act.sem_inc(s_ce, 2)
            act.sem_inc(s_de, 2)
            act.sem_inc(s_ls, 2)
            act.sem_inc(s_xc[0], 1)
            act.sem_inc(s_sc, 1)
            act.sem_inc(s_cc, 1)
            batches(act, U, [(4, copy_slots), (3, copy_combine), (1, copy_logits), (0, copy_x), (1, exps)])

        @block.tensor
        def _(pe):
            def turn_x(b, k, g):
                pe.wait_ge(s_xn, b * IB + IB)
                for half in range(2):
                    pe.wait_ge(s_xc[half], b + 1)
                for c in range(KC):
                    for i in range(IB):
                        mm = pe.transpose(pX[:, c, i * P:(i + 1) * P], XN[:, k, i, c * 96:(c + 1) * 96], ident[:])
                mm.then_inc(s_xt, 1)

            def logits(b, k, g):
                for half in range(2):
                    pe.wait_ge(s_xc[half], b + 2)
                pe.wait_ge(s_ls, b + 1)
                for c in range(KC):
                    mm = pe.matmul(pL[:, k % 2], SP[:, c, :], XT[:, k % 2, c, :], start=(c == 0), stop=(c == KC - 1))
                mm.then_inc(s_lg, 1)

            def turn_logits(b, k, g):
                pe.wait_ge(s_ls, b + 3)
                pe.wait_ge(s_cm, b * 4 + 2)
                pe.sem_inc(s_go, 1)
                for i in range(IB):
                    mm = pe.transpose(pC[:, i, :], LS[:, k % 2, i * P:(i + 1) * P], ident[0:NS, 0:NS])
                mm.then_inc(s_lt, 1)

            def sum_slots(b, k, g):
                pe.wait_ge(s_dk, b + 2)
                pe.wait_ge(s_sc, b + 1)
                for c in range(KC):
                    for i in range(IB):
                        mm = pe.matmul(pS[:, c, :], XN[:, k, i, c * 96:(c + 1) * 96], DK[:, k % 2, i, :],
                                       start=(i == 0), stop=(i == IB - 1), skip_group_check=True)
                mm.then_inc(s_s, 1)

            def turn_both(b, k, g):
                pe.wait_ge(s_dn, b + 3)
                pe.wait_ge(s_cn, b + 3)
                pe.wait_ge(s_dk, b + 1)
                pe.wait_ge(s_cc, b + 1)
                pe.sem_inc(s_go, 1)
                for i in range(IB):
                    pe.transpose(pD[:, i, :], DN[:, k % 2, i * P:(i + 1) * P], ident[0:NS, 0:NS])
                mm = pe.transpose(pT[:], C2[:, k % 2].rearrange("p i n -> p (i n)"), ident[:])
                mm.then_inc(s_tn, 1)

            pe.sem_inc(s_s, U)
            pe.sem_inc(s_lg, 2)
            pe.sem_inc(s_lt, 2)
            pe.sem_inc(s_tn, 2)
            pe.wait_ge(s_sp, TVN["SP"])
            batches(pe, U, [(3, turn_both), (1, logits), (0, turn_x), (1, turn_logits), (3, sum_slots)])


def mix_block(nc, dram, keep):
    H1, CTA, XTL = keep["H1"], keep["CTA"], keep["XTL"]
    with ExitStack() as ctx:
        def sb(name, shape, dt=F32):
            return ctx.enter_context(nc.sbuf_tensor(name, shape, dt))

        def sem(name):
            return ctx.enter_context(nc.semaphore(name))

        Wd, Wu, bd, bu = (keep[k] for k in ("Wd", "Wu", "bd", "bu"))
        ones = sb("onesr", [1, B * SLOT])
        HG = sb("HG", [HF, EXP, B * SLOT])
        YS = sb("YS", [B * SLOT, EXP, D])
        YB = sb("YB", [P, B, D])
        OUT = sb("OUT", [P, 2, IB, D])
        pH = ctx.enter_context(nc.psum_tensor("pH", [P, 8, 512], F32))
        s_on, s_h, s_g, s_y, s_yc, s_yd, s_yb = (sem(n) for n in (
            "ones_set", "hidden_ready", "gelu_done", "slot_out", "slot_out_copied",
            "slot_out_stored", "slot_out_loaded"))
        s_m, s_o = sem("mixed"), sem("outputs_ready")
        s_od = [sem("outputs_written_even"), sem("outputs_written_odd")]
        block = ctx.enter_context(nc.Block())

        @block.sync
        def _(sp):
            sp.wait_ge(s_yc, EXP // 2)
            sp.dma_start(dram["yD"].rearrange("e p b d -> (p b) e d"), YS[:]).then_inc(s_yd, 16)
            sp.wait_ge(s_yd, 16)
            for i in range(IB):
                sp.dma_start(YB[i * NS:(i + 1) * NS], dram["yD"].rearrange("e p b d -> (e p) b d")
                             ).then_inc(s_yb, 16)
            for k in range(2):
                sp.sem_inc(s_od[k], 16)
            with sp.Fori(0, B // 2) as bp:
                for k in range(2):
                    sp.wait_ge(s_o, bp * 2 + (k + 1))
                    sp.dma_start(dram["out"].rearrange("b (i p) d -> b p i d", p=P)[bp * 2 + k],
                                 OUT[:, k]).then_inc(s_od[k], 16)
            for k in range(2):
                sp.wait_ge(s_od[k], 16 + 16 * B // 2)

        @block.scalar
        def _(act):
            act.wait_ge(s_h, 1)
            for e in range(EXP):
                ins = act.activation(HG[:, e, :], pH[0:HF, 0, e * 64:(e + 1) * 64], ACT.Gelu, bias=bd[:, e:e + 1])
            ins.then_inc(s_g, 1)

        @block.vector
        def _(dve):
            dve.memset(ones[:], 1.0).then_inc(s_on, 1)
            for e in range(0, EXP, 2):
                dve.wait_ge(s_y, e // 2 + 1)
                dve.tensor_copy(YS[:, e:e + 2, :], pH[0:B * SLOT, 1 + e // 2, 0:2 * D].rearrange(
                    "p (e d) -> p e d", e=2)).then_inc(s_yc, 1)
            with dve.Fori(0, B // 2) as bp:
                for k in range(2):
                    dve.wait_ge(s_m, bp * 2 + (k + 1))
                    dve.wait_ge(s_od[k], (bp + 1) * 16)
                    dve.tensor_tensor(OUT[:, k], pH[:, 4 * k:4 * k + 4, 0:D],
                                      H1[:, bass.ds(bp * (2 * IB) + k * IB, IB), :], ALU.add).then_inc(s_o, 1)

        @block.tensor
        def _(pe):
            pe.wait_ge(s_on, 1)
            for e in range(EXP):
                for c in range(KC):
                    mm = pe.matmul(pH[0:HF, 0, e * 64:(e + 1) * 64], Wd[:, c, e, :],
                                   XTL[:, c, :, e * SLOT:(e + 1) * SLOT].rearrange("k b p -> k p b"), start=(c == 0), stop=(c == KC - 1),
                                   skip_group_check=True)
            mm.then_inc(s_h, 1)
            pe.wait_ge(s_g, 1)
            for e in range(EXP):
                out = pH[0:B * SLOT, 1 + e // 2, (e % 2) * D:(e % 2 + 1) * D]
                pe.matmul(out, HG[:, e, :], Wu[:, e, :], start=True, stop=False, skip_group_check=True)
                mm = pe.matmul(out, ones[0:1, :], bu[0:1, e, :], start=False, stop=True, skip_group_check=True)
                if e % 2:
                    mm.then_inc(s_y, 1)
            pe.wait_ge(s_yb, 16 * IB)
            for b in range(B):
                if b >= 2:
                    pe.wait_ge(s_o, b - 1)
                for i in range(IB):
                    mm = pe.matmul(pH[:, 4 * (b % 2) + i, 0:D], CTA[i * NS:(i + 1) * NS, b * P:(b + 1) * P],
                                   YB[i * NS:(i + 1) * NS, b, :], start=True, stop=True)
                mm.then_inc(s_m, 1)


def build(nc, dram):
    with ExitStack() as outer:
        def sb(name, shape, dt=F32):
            return outer.enter_context(nc.sbuf_tensor(name, shape, dt))

        keep = {"ident": sb("ident", [P, P])}
        with ExitStack() as ctx:
            keep["FX"] = ctx.enter_context(nc.sbuf_tensor("FX", [KF, T], BF16))
            keep["GS"] = ctx.enter_context(nc.sbuf_tensor("GS", [KF, GN], BF16))
            embed_block(nc, dram, keep)
            key_tables_block(nc, dram, keep)
            attention_block(nc, dram, keep)
        sums_block(nc, dram)
        keep["H1"] = sb("H1", [P, NT, D])
        keep["stats"] = sb("stats", [P, NT, 2])
        residual_block(nc, dram, keep)
        keep["CTA"] = sb("CTA", [P, B * P])
        keep["XTL"] = sb("XTL", [96, KC, B, NS])
        keep["Wd"], keep["Wu"] = sb("Wd", [96, KC, EXP, HF]), sb("Wu", [HF, EXP, D])
        keep["bd"], keep["bu"] = sb("bd", [HF, EXP]), sb("bu", [1, EXP, D])
        experts_block(nc, dram, keep)
        mix_block(nc, dram, keep)


def kernel(x, L0_tok_quantum_params, L0_tok_post_w, L0_tok_post_b, L0_attn_Wq, L0_attn_bq, L0_attn_Wk,
           L0_attn_bk, L0_attn_Wv, L0_attn_bv, L0_attn_rel_table, L0_attn_Wpk, L0_attn_bpk, L0_attn_Wpq,
           L0_attn_bpq, L0_attn_Wo, L0_attn_bo, L0_ffn_slot_params, L0_ffn_scale, L0_ffn_W_down,
           L0_ffn_b_down, L0_ffn_W_up, L0_ffn_b_up):
    import concourse.bacc as bacc
    from concourse.bass_utils import run_bass_kernel_spmd

    f4 = np.float32
    one = np.ones((1, 1), f4)
    rel = np.asarray(L0_attn_rel_table).T
    post_w, post_b = np.asarray(L0_tok_post_w), np.asarray(L0_tok_post_b)
    arrays = {
        "ids": np.asarray(x).reshape(NT, P).T,
        "qparams": np.asarray(L0_tok_quantum_params).reshape(-1, NA),
        "Wq": L0_attn_Wq, "Wk": L0_attn_Wk, "Wv": L0_attn_Wv, "Wpk": L0_attn_Wpk, "Wpq": L0_attn_Wpq,
        "Wo": L0_attn_Wo,
        "post": np.concatenate([post_w, post_b[:, None], np.zeros((D, 1), f4)], axis=1),
        "post_rows": np.concatenate([post_w.T, post_b[None], np.asarray(L0_attn_bo)[None]]),
        "rel_back": rel[:, ::-1], "rel_fore": rel,
        "rows": np.stack([np.asarray(a) for a in (L0_attn_bq, L0_attn_bk, L0_attn_bv, L0_attn_bpk,
                                                  L0_attn_bpq)])[None],
        "slots": np.asarray(L0_ffn_slot_params).reshape(D, NS),
        "scale": np.asarray(L0_ffn_scale).reshape(1, 1),
        "Wd": L0_ffn_W_down, "bd": L0_ffn_b_down, "Wu": L0_ffn_W_up, "bu": L0_ffn_b_up,
        "ident": np.eye(P, dtype=f4),
        "centre": np.eye(D, dtype=f4) - f4(1 / D),
        "parity": (np.arange(P)[:, None] % 2 == np.arange(2)[None]).astype(f4),
        "hmask": (np.arange(96)[:, None] // DH == np.arange(HC)[None]).astype(f4),
        "e7": np.eye(NF, dtype=f4)[7:8],
    }
    arrays = {k: np.ascontiguousarray(v) for k, v in arrays.items()}
    nc = bacc.Bacc("TRN2", target_bir_lowering=False, num_devices=1)
    dram = {k: nc.dram_tensor(f"{k}_in", a.shape, mybir.dt.from_np(a.dtype), kind="ExternalInput").ap()
            for k, a in arrays.items()}
    dram["out"] = nc.dram_tensor("out_dram", (B, S, D), F32, kind="ExternalOutput").ap()
    scratch = {
        "tabD": ((H + 1) * NF, 3, 2, TAB, BF16),
        "evT": (NF, T, F32),
        "gmD": (NF, NF, F32),
        "gD": (3, IB, H, NF, 2, B, P, BF16),
        "otD": (H, 2 * DH, B, S, F32),
        "overD": (H * B, S, F32),
        "yD": (EXP, SLOT, B, D, F32),
    }
    for k, (*shape, dt) in scratch.items():
        dram[k] = nc.dram_tensor(f"{k}_scratch", tuple(shape), dt).ap()
    build(nc, dram)
    r = run_bass_kernel_spmd(nc, [{f"{k}_in": a for k, a in arrays.items()}], core_ids=[0])
    return r.results[0]["out_dram"]
```

```python
import math
from contextlib import ExitStack

import numpy as np
import concourse.bass as bass
from concourse import mybir

ALU = mybir.AluOpType
ACT = mybir.ActivationFunctionType
AX = mybir.AxisListType
F32 = mybir.dt.float32
BF16 = mybir.dt.bfloat16
I32 = mybir.dt.int32

B, S, D = 16, 512, 192
H, DH = 12, 16
P = 128
IB = S // P
NT = B * IB
T = B * S
KC = D // 96
HC = H // KC
NQ, NA = 6, 36
NF = 8
REL = 127
NR = 2 * REL + 1
NPR = 6
KF = 2 * NPR * NF
TAB = 516
SCALE = 1.0 / math.sqrt(3.0 * DH)
EXP, SLOT = 8, 4
NS = EXP * SLOT
HF = D // 8
GN = 2 * H * 2 * NF + D
EPS_LN, EPS_L2 = 1e-5, 1e-6
HI, MID, LO = range(3)

TABLE_PARTS = (0, 0, 0, 1, 1, 2)
TOKEN_PARTS = (0, 1, 2, 0, 1, 0)

XQ_PITCH = 5 * P
XQ_LEN = 2 * P + B * XQ_PITCH


def beside(ib):
    return [jb for jb in (ib - 1, ib, ib + 1) if 0 <= jb < IB]


def circuit_plan(n=NQ):
    steps, memo = [], {}

    def emit(op, a, b):
        key = (op, min(a, b), max(a, b)) if op != "subtract" else (op, a, b)
        if key not in memo:
            memo[key] = len(steps)
            steps.append((op, a, b))
        return ("t", memo[key])

    def times(a, b):
        if a is None or b is None:
            return b if a is None else a
        return emit("mult", a, b)

    def total(terms):
        plus = [t for s, t in terms if s > 0]
        minus = [t for s, t in terms if s < 0]
        sign = 1
        if not plus:
            plus, minus, sign = minus, plus, -1
        while len(plus) > 1:
            plus = plus[2:] + [emit("add", plus[0], plus[1])]
        while len(minus) > 1:
            minus = minus[2:] + [emit("add", minus[0], minus[1])]
        return (sign, emit("subtract", plus[0], minus[0]) if minus else plus[0])

    def site(ops):
        x = z = k = 0
        for a in ops:
            if a == "X":
                k += 2 * z
                x ^= 1
            else:
                z ^= 1
        return x, z, (k - (x & z)) % 4

    def chain(sites, menu):
        last, out = max(sites), []
        for wrap in (0, 1) if last == n - 1 else (0,):
            for z0 in (0, 1) if 0 in sites else (0,):
                cur = {(par, 0): (0, 1, None) for par in (0, 1)}
                for j in range(n):
                    new = {}
                    for (pold, xo), (ko, so, no) in cur.items():
                        opts = [(0, 0, None, 1, 0)]
                        if j in sites:
                            opts = [(x, z, *v) for (x, z), v in menu.items() if j > 0 or z == z0]
                        for x, z, c, s, k in opts:
                            if j == n - 1 and last == n - 1 and x != wrap:
                                continue
                            par = pold ^ z if j > 0 else pold
                            ops = ["X"] * (j == 1 and xo) + ["Z"] * (j >= 1 and z0) + ["X"] * (j > 1 and xo)
                            ops += ["X"] * x + ["Z"] * (z and j > 0) + ["Z"] * par + ["X"] * (wrap and j <= 1)
                            lx, lz, ph = site(ops)
                            letter = {(0, 0): None, (1, 0): "x", (0, 1): "z", (1, 1): "y"}[lx, lz]
                            tot = (ph + k + ko + (so < 0) * 2 + (s < 0) * 2) % 4
                            new.setdefault((par, x, c), []).append((tot, no, letter))
                    merged = {}
                    for (par, x, c), found in new.items():
                        kap = found[0][0] % 2
                        terms = [(1 if tot == kap else -1, times(no, ("b", lt, j) if lt else None))
                                 for tot, no, lt in found]
                        s1, node = terms[0] if len(terms) == 1 else total(terms)
                        node = times(node, ("w", c, j) if c else None)
                        merged.setdefault((par, x), []).append((kap, s1, node))
                    cur = {}
                    for key, found in merged.items():
                        s1, node = found[0][1:] if len(found) == 1 else total([f[1:] for f in found])
                        cur[key] = (found[0][0], s1, node)
                    if j >= last:
                        cur = {k: v for k, v in cur.items() if k[0] == 0}
                out += [(s1, node) for _, s1, node in cur.values()]
        return total(out)

    zs = {(0, 1): ("c", 1, 0), (1, 0): ("s", -1, 0)}
    xs = {(1, 0): ("al", 1, 0), (0, 1): ("be", 1, 0), (1, 1): ("ga", -1, 1)}
    ez = [chain(range(1, n), zs)] + [chain(range(q + 1), zs) for q in range(1, n)]
    ex = [chain((q, q + 1), xs) for q in range(n - 1)] + [chain((0, 1, n - 1), xs)]
    level = []
    for _, a, b in steps:
        level.append(1 + max([level[x[1]] for x in (a, b) if x[0] == "t"], default=-1))
    levels = [[i for i in range(len(steps)) if level[i] == v] for v in range(max(level) + 1)]
    ends = {e[1][1] for e in ez + ex}
    until = list(level)
    for i, (_, a, b) in enumerate(steps):
        for x in (a, b):
            if x[0] == "t":
                until[x[1]] = max(until[x[1]], level[i])
    for e in ends:
        until[e] = len(levels) + 1
    place, free, width = {}, [], 0
    for v, ids in enumerate(levels):
        free += sorted(place[i] for i in place if until[i] == v - 1 and i not in ends)
        for i in ids:
            if free:
                place[i] = free.pop(0)
            else:
                place[i], width = width, width + 1
    return steps, levels, place, width, ez, ex


def embed_block(nc, dram, keep):
    steps, levels, place, width, ez, ex = circuit_plan()
    AQ = 4
    EB, EQ = 4, 2
    with ExitStack() as ctx:
        def sb(name, shape, dt=F32):
            return ctx.enter_context(nc.sbuf_tensor(name, shape, dt))

        def ps(name, shape, dt=F32):
            return ctx.enter_context(nc.psum_tensor(name, shape, dt))

        def sem(name):
            return ctx.enter_context(nc.semaphore(name))

        ident, FX, GS = keep["ident"], keep["FX"], keep["GS"]
        ids = sb("ids", [P, NT], I32)
        angle = sb("angle", [P, NT, NA])
        turns = sb("turns", [P, NT, NA])
        sine = sb("sine", [P, NT, NA])
        cosine = sb("cosine", [P, NT, NA])
        bloch = sb("bloch", [P, 2, NQ, NT])
        tilt = sb("tilt", [P, 2, NQ, NT])
        work = sb("work", [P, width, NT])
        edge = sb("edge", [P, 3, NQ, NT])
        E = sb("E", [P, NT, NF])
        EU = sb("EU", [P, 2, NT, NQ + 1])
        var = sb("var", [P, 6, NT])
        Ft = sb("Ft", [P, NT, NF])
        Fr = sb("Fr", [P, 2, NT, NF])
        Fp = sb("Fp", [P, 3, NT, NF], BF16)
        parity = sb("parity", [P, 2])
        FW = sb("FW", [P, NT, 2, NPR, NF], BF16)
        identb = sb("identb", [P, P], BF16)
        ET = sb("ET", [NF, EB, S])
        GM = sb("GM", [NF, NF])
        GMB = sb("GMB", [P, NF, NF])
        Wq, Wk, Wv, Wpk, Wpq = (sb(f"W{k}", [96, KC, D]) for k in ("q", "k", "v", "pk", "pq"))
        cen = sb("cen", [96, KC, D])
        post = sb("post", [96, KC, NF])
        relr = sb("relr", [96, KC, NR])
        relf = sb("relf", [96, KC, NR])
        rows = sb("rows", [1, 5, D])
        ones = sb("ones", [1, 256])
        e7 = sb("e7", [1, NF])
        hmask = sb("hmask", [96, HC])
        CT = sb("CT", [96, KC, NF])
        WT = sb("WT", [96, 2, KC, NF])
        RT = sb("RT", [96, 2, KC, NR])
        WB = sb("WB", [96, 2, KC, HC, NF])
        K3 = sb("K3", [96, KC, 3, NF])
        KB = sb("KB", [96, KC, HC, 3, NF])
        LQ = sb("LQ", [96, KC, 2, NF])
        TB = sb("TB", [48, KC, 2, TAB])
        TR = sb("TR", [48, 2, KC, 2, TAB])
        TP_ = sb("TP", [48, 3, KC, 2, TAB], BF16)
        GW = sb("GW", [NF, GN])
        GR = sb("GR", [NF, 2, GN])
        GP = sb("GP", [NF, 3, GN], BF16)
        pbank = ps("pbank", [P, 8, 512])

        s_ids, s_w = sem("ids_loaded"), sem("weights_loaded")
        s_par = [sem(f"angles_gathered{k}") for k in range(AQ)]
        s_red, s_sin, s_lvl = sem("angles_reduced"), sem("sines_ready"), [
            sem("circuit_steps_by_vector"), sem("circuit_steps_by_gpsimd")]
        s_cir = sem("circuit_done")
        s_tab, s_tv = sem("tables_on_pe"), sem("tables_on_dve")
        s_et, s_ete = sem("evT_ready"), sem("evT_copied")
        s_etd = [sem(f"evT_stored{k}") for k in range(EB // EQ)]
        s_gm, s_v, s_sq = sem("gram_moved"), sem("variance_steps"), sem("root_ready")
        s_fw, s_fx = sem("features_split"), sem("featuresT_ready")
        s_fe = [sem("featuresT_copied_by_scalar"), sem("featuresT_copied_by_vector")]
        s_gs, s_td = sem("g_weights_stacked"), sem("tables_stored")

        block = ctx.enter_context(nc.Block())
        NW = 14
        FIRST = 4

        def pool_share(ids_):
            return round(len(ids_) * 0.32) if len(ids_) >= 6 else 0

        def circuit_step(engine, i):
            op, a, b = steps[i]
            return engine.tensor_tensor(work[:, place[i], :], operand(a), operand(b),
                                        {"mult": ALU.mult, "add": ALU.add, "subtract": ALU.subtract}[op])

        flat = "p t a -> p (t a)"
        quarters = [[x[:, k * (NT // AQ):(k + 1) * (NT // AQ)].rearrange(flat)
                     for x in (angle, turns, sine, cosine)] for k in range(AQ)]
        TWO_PI = 2 * np.pi
        C1 = 6.28125
        C2 = float(TWO_PI - C1)
        MAGIC = 1.5 * 2.0 ** 23
        EDGE = 3.1415925

        def gate(arr, layer, kind):
            return arr[:].rearrange("p t (l q g) -> p l g q t", l=3, q=NQ)[:, layer, kind]

        def operand(x):
            if x[0] == "t":
                return work[:, place[x[1]], :]
            kind, name, q = x
            if kind == "b":
                return gate(cosine, 0, 0)[:, q] if name == "z" else bloch[:, "xy".index(name), q, :]
            if name in ("al", "be"):
                return tilt[:, ("al", "be").index(name), q, :]
            return {"c": gate(cosine, 1, 0), "s": gate(sine, 1, 0), "ga": gate(sine, 1, 1)}[name][:, q]

        @block.gpsimd
        def _(pool):
            pool.wait_ge(s_ids, 16)
            for t in range(NT):
                pool.indirect_dma_start(
                    out=angle[:, t, :], out_offset=None, in_=dram["qparams"],
                    in_offset=bass.IndirectOffsetOnAxis(ap=ids[:, t:t + 1], axis=0)
                ).then_inc(s_par[t // (NT // AQ)], 16)
            pool.wait_ge(s_sin, 2 * AQ)
            by_vector, by_pool = FIRST, 0
            for ids_ in levels:
                n = pool_share(ids_)
                if n:
                    pool.wait_ge(s_lvl[0], by_vector)
                    if by_pool:
                        pool.wait_ge(s_lvl[1], by_pool)
                for i in ids_[len(ids_) - n:]:
                    circuit_step(pool, i).then_inc(s_lvl[1], 1)
                by_vector, by_pool = by_vector + len(ids_) - n, by_pool + n

        TV = {}

        @block.vector
        def _(dve):
            done = [0]

            def step(ins, name=None):
                ins.then_inc(s_tv, 1)
                done[0] += 1
                if name:
                    TV[name] = done[0]
                dve.wait_ge(s_tv, done[0])

            dve.wait_ge(s_w, 16 * NW)
            step(dve.memset(ones[:], 1.0), "ones")
            step(dve.tensor_copy(identb[:], ident[:]), "identb")
            dve.wait_ge(s_tab, 1)
            step(dve.tensor_copy(CT[:], pbank[0:96, 0, 0:KC * NF].rearrange("p (c f) -> p c f", c=KC)), "CT")
            dve.wait_ge(s_tab, 2)
            step(dve.tensor_scalar(GM[:], pbank[0:NF, 1, 480:488], 1.0 / D, None, ALU.mult), "GM")
            step(dve.tensor_copy(WT[:], pbank[0:96, 2, 0:2 * KC * NF].rearrange(
                "p (k c f) -> p k c f", k=2, c=KC)))
            for k in range(2):
                for m in range(KC):
                    step(dve.tensor_copy(RT[:, k, m, :], pbank[0:96, 3 + 2 * k + m, 0:NR]))
            for k in range(2):
                for m in range(KC):
                    step(dve.tensor_tensor(
                        WB[:, k, m], WT[:, k, m, None, :].to_broadcast([96, HC, NF]),
                        hmask[:, :, None].to_broadcast([96, HC, NF]), ALU.mult))
            for m in range(KC):
                for t in range(3):
                    step(dve.tensor_copy(K3[:, m, t, :], WT[:, 1, m, :]))
                for t, r in ((HI, 0), (LO, NR - 1)):
                    step(dve.tensor_tensor(K3[:, m, t, 7:8], K3[:, m, t, 7:8], RT[:, 0, m, r:r + 1], ALU.add))
                for t in range(3):
                    step(dve.tensor_tensor(
                        KB[:, m, :, t, :], K3[:, m, t, None, :].to_broadcast([96, HC, NF]),
                        hmask[:, :, None].to_broadcast([96, HC, NF]), ALU.mult))
                step(dve.memset(LQ[:, m], 0.0))
                for i, r in ((0, NR - 1), (1, 0)):
                    step(dve.tensor_copy(LQ[:, m, i, 7:8], RT[:, 1, m, r:r + 1]))
            TV["blocks"] = done[0]
            dve.wait_ge(s_tab, 3)
            for k in range(2):
                for m in range(KC):
                    src = pbank[0:48, 3 + 2 * k + m, 0:NR]
                    step(dve.tensor_copy(TB[:, m, k, 130:130 + NR], src))
                    step(dve.tensor_copy(TB[:, m, k, 0:130], src[:, 0:1].to_broadcast([48, 130])))
                    step(dve.tensor_copy(TB[:, m, k, 385:TAB], src[:, NR - 1:NR].to_broadcast([48, TAB - 385])))
            for k, t0 in enumerate((MID, HI)):
                step(dve.tensor_copy(GW[:, k * 192:(k + 1) * 192].rearrange("p (h f t) -> p h f t", h=H, f=NF),
                                     pbank[0:NF, 0, 0:288].rearrange("p (h t f) -> p h f t", h=H, t=3)[
                                         :, :, :, t0:t0 + 2]))
            step(dve.tensor_copy(GW[:, 384:576], pbank[0:NF, 1, 0:D]))
            for src, rest, parts, name in ((TB[:], TR, TP_, "tables"), (GW[:], GR, GP, "gparts")):
                step(dve.tensor_copy(parts[:, 0], src))
                step(dve.tensor_tensor(rest[:, 0], src, parts[:, 0], ALU.subtract))
                step(dve.tensor_copy(parts[:, 1], rest[:, 0]))
                step(dve.tensor_tensor(rest[:, 1], rest[:, 0], parts[:, 1], ALU.subtract))
                step(dve.tensor_copy(parts[:, 2], rest[:, 1]), name)

            n = [0]

            def red(ins):
                ins.then_inc(s_red, 1)
                n[0] += 1
                dve.wait_ge(s_red, n[0])

            for q, (ang, trn, _, _) in enumerate(quarters):
                dve.wait_ge(s_par[q], 16 * NT // AQ)
                red(dve.tensor_scalar(trn, ang, float(1 / TWO_PI), MAGIC, ALU.mult, ALU.add))
                red(dve.tensor_scalar(trn, trn, MAGIC, None, ALU.subtract))
                red(dve.scalar_tensor_tensor(out=ang, in0=trn, scalar=-C1, in1=ang, op0=ALU.mult, op1=ALU.add))
                red(dve.scalar_tensor_tensor(out=ang, in0=trn, scalar=-C2, in1=ang, op0=ALU.mult, op1=ALU.add))
                red(dve.tensor_scalar(ang, ang, EDGE, -EDGE, ALU.min, ALU.max))
                red(dve.tensor_scalar(trn, ang, float(np.pi / 2), float(-TWO_PI), ALU.is_gt, ALU.mult))
                red(dve.scalar_tensor_tensor(out=trn, in0=ang, scalar=float(np.pi / 2), in1=trn,
                                             op0=ALU.add, op1=ALU.add))
                red(dve.tensor_scalar(trn, trn, EDGE, -EDGE, ALU.min, ALU.max))
            dve.wait_ge(s_sin, 2 * AQ)
            pre = [0]

            def lvl(ins):
                ins.then_inc(s_lvl[0], 1)
                pre[0] += 1

            lvl(dve.tensor_tensor(bloch[:, 0], gate(sine, 0, 0), gate(cosine, 0, 1), ALU.mult))
            lvl(dve.tensor_tensor(bloch[:, 1], gate(sine, 0, 0), gate(sine, 0, 1), ALU.mult))
            lvl(dve.tensor_tensor(tilt[:, 0], gate(cosine, 1, 1), gate(cosine, 1, 0), ALU.mult))
            lvl(dve.tensor_tensor(tilt[:, 1], gate(cosine, 1, 1), gate(sine, 1, 0), ALU.mult))
            assert pre[0] == FIRST
            by_pool = 0
            for ids_ in levels:
                dve.wait_ge(s_lvl[0], pre[0])
                if by_pool:
                    dve.wait_ge(s_lvl[1], by_pool)
                n = pool_share(ids_)
                for i in ids_[:len(ids_) - n]:
                    lvl(circuit_step(dve, i))
                by_pool += n
            dve.wait_ge(s_lvl[0], pre[0])
            dve.wait_ge(s_lvl[1], by_pool)
            for q in range(NQ):
                lvl(dve.tensor_tensor(edge[:, 0, q], gate(cosine, 2, 0)[:, q], operand(ez[q][1]), ALU.mult))
                lvl(dve.tensor_tensor(edge[:, 1, q], gate(sine, 2, 0)[:, q], operand(ex[q][1]), ALU.mult))
            lvl(dve.memset(E[:], 1.0))
            dve.wait_ge(s_lvl[0], pre[0])
            for q in range(NQ):
                assert ez[q][0] == 1 and ex[q][0] == 1
                ins = dve.tensor_tensor(E[:, :, q], edge[:, 0, q], edge[:, 1, q], ALU.subtract)
            ins.then_inc(s_cir, 1)

            dve.wait_ge(s_cir, 1)
            dve.wait_ge(s_gm, 32)
            vn = [0]

            def vs(ins):
                ins.then_inc(s_v, 1)
                vn[0] += 1
                dve.wait_ge(s_v, vn[0])

            F1 = NQ + 1
            for g in range(F1):
                vs(dve.tensor_tensor(EU[:, min(g, 1)], E[:, :, g:g + 1].to_broadcast([P, NT, F1]),
                                     GMB[:, g, None, 0:F1].to_broadcast([P, NT, F1]), ALU.mult))
                if g:
                    vs(dve.tensor_tensor(EU[:, 0], EU[:, 0], EU[:, 1], ALU.add))
            vs(dve.tensor_tensor(EU[:, 0], EU[:, 0], E[:, :, 0:F1], ALU.mult))
            vs(dve.tensor_reduce(var[:, 0], EU[:, 0], AX.X, ALU.add))
            vs(dve.tensor_scalar(var[:, 1], var[:, 0], 0.0, EPS_LN, ALU.max, ALU.add))
            assert vn[0] == 2 * NQ + 4
            dve.wait_ge(s_sq, 1)
            vs(dve.reciprocal(var[:, 3], var[:, 2]))
            vs(dve.tensor_tensor(var[:, 4], var[:, 3], var[:, 3], ALU.mult))
            vs(dve.tensor_tensor(var[:, 4], var[:, 4], var[:, 1], ALU.mult))
            vs(dve.tensor_scalar(var[:, 4], var[:, 4], -0.5, 1.5, ALU.mult, ALU.add))
            vs(dve.tensor_tensor(var[:, 5], var[:, 3], var[:, 4], ALU.mult))
            vs(dve.memset(Ft[:, :, 7:8], 1.0))
            vs(dve.tensor_tensor(Ft[:, :, 0:7], E[:, :, 0:7],
                                 var[:, 5, :, None].to_broadcast([P, NT, 7]), ALU.mult))
            vs(dve.tensor_copy(Fp[:, 0], Ft[:]))
            vs(dve.tensor_tensor(Fr[:, 0], Ft[:], Fp[:, 0], ALU.subtract))
            vs(dve.tensor_copy(Fp[:, 1], Fr[:, 0]))
            vs(dve.tensor_tensor(Fr[:, 1], Fr[:, 0], Fp[:, 1], ALU.subtract))
            vs(dve.tensor_copy(Fp[:, 2], Fr[:, 1]))
            for half in range(2):
                t = slice(half * NT // 2, (half + 1) * NT // 2)
                for u in range(2):
                    for k, part in enumerate(TOKEN_PARTS):
                        ins = dve.tensor_scalar(FW[:, t, u, k, :], Fp[:, part, t], parity[:, u:u + 1], None, ALU.mult)
                ins.then_inc(s_fw, 1)
            for c in range(1, NT // 8, 2):
                dve.wait_ge(s_fx, c + 1)
                dve.tensor_copy(FX[:, c * 1024:(c + 1) * 1024],
                                pbank[0:KF, 2 + c % 2, :].bitcast(BF16)).then_inc(s_fe[1], 1)

        @block.sync
        def _(sp):
            sp.dma_start(ids[:], dram["ids"]).then_inc(s_ids, 16)
            for t, name in ((Wq, "Wq"), (Wk, "Wk"), (Wv, "Wv"), (Wpk, "Wpk"), (Wpq, "Wpq")):
                sp.dma_start(t[:], dram[name].rearrange("(c k) n -> k c n", c=KC)).then_inc(s_w, 16)
            sp.dma_start(cen[:], dram["centre"].rearrange("(c k) n -> k c n", c=KC)).then_inc(s_w, 16)
            sp.dma_start(post[:], dram["post"].rearrange("(c k) n -> k c n", c=KC)).then_inc(s_w, 16)
            sp.dma_start(relr[:], dram["rel_back"].rearrange("(c k) n -> k c n", c=KC)).then_inc(s_w, 16)
            sp.dma_start(relf[:], dram["rel_fore"].rearrange("(c k) n -> k c n", c=KC)).then_inc(s_w, 16)
            sp.dma_start(rows[:], dram["rows"]).then_inc(s_w, 16)
            sp.dma_start(ident[:], dram["ident"]).then_inc(s_w, 16)
            sp.dma_start(parity[:], dram["parity"]).then_inc(s_w, 16)
            sp.dma_start(hmask[:], dram["hmask"]).then_inc(s_w, 16)
            sp.dma_start(e7[:], dram["e7"]).then_inc(s_w, 16)
            sp.wait_ge(s_tv, TV["GM"])
            sp.dma_start(dram["gmD"], GM[:]).then_inc(s_gm, 16)
            sp.wait_ge(s_gm, 16)
            sp.dma_start(GMB[:].rearrange("p f g -> p (f g)"), dram["gmD"].rearrange("(a f) g -> a (f g)", a=1
                         ).to_broadcast([P, NF * NF])).then_inc(s_gm, 16)
            sp.wait_ge(s_tv, TV["tables"])
            for m in range(KC):
                sp.dma_start(dram["tabD"][m * 48:(m + 1) * 48], TP_[:, :, m]).then_inc(s_td, 16)
            sp.dma_start(dram["tabD"][96:104], TP_[40:48, :, KC - 1]).then_inc(s_td, 16)
            sp.wait_ge(s_tv, TV["gparts"])
            for u in range(2):
                for k, part in enumerate(TABLE_PARTS):
                    r0 = (u * NPR + k) * NF
                    sp.dma_start(GS[r0:r0 + NF, :], GP[:, part, :]).then_inc(s_gs, 16)
            for n in range(B // EQ):
                sp.wait_ge(s_ete, (n + 1) * EQ)
                q = n % (EB // EQ)
                sp.dma_start(dram["evT"][:, n * EQ * S:(n + 1) * EQ * S],
                             ET[:, q * EQ:(q + 1) * EQ].rearrange("f b n -> f (b n)")).then_inc(s_etd[q], 16)
            for q in range(EB // EQ):
                sp.wait_ge(s_etd[q], 16 * B // EB)
            sp.wait_ge(s_td, 16 * (KC + 1))
            sp.wait_ge(s_gs, 16 * 2 * NPR)

        @block.scalar
        def _(act):
            for q, (ang, trn, sn, cs) in enumerate(quarters):
                act.wait_ge(s_red, 8 * (q + 1))
                act.activation(sn, ang, ACT.Sin).then_inc(s_sin, 1)
                act.activation(cs, trn, ACT.Sin).then_inc(s_sin, 1)
            for b in range(B):
                if b == 7:
                    act.wait_ge(s_v, 2 * NQ + 4)
                    act.activation(var[:, 2], var[:, 1], ACT.Sqrt).then_inc(s_sq, 1)
                act.wait_ge(s_et, b + 1)
                if b >= EB and b % EQ == 0:
                    act.wait_ge(s_etd[b % EB // EQ], 16 * (b // EB))
                act.activation(ET[:, b % EB, :], pbank[0:NF, 4 + b % 2, :], ACT.Copy).then_inc(s_ete, 1)
            for c in range(0, NT // 8, 2):
                act.wait_ge(s_fx, c + 1)
                act.activation(FX[:, c * 1024:(c + 1) * 1024],
                               pbank[0:KF, 2 + c % 2, :].bitcast(BF16), ACT.Copy).then_inc(s_fe[0], 1)

        @block.tensor
        def _(pe):
            pe.wait_ge(s_tv, TV["ones"])
            for m in range(KC):
                for c in range(KC):
                    mm = pe.matmul(pbank[0:96, 0, m * NF:(m + 1) * NF], cen[:, c, m * 96:(m + 1) * 96],
                                   post[:, c, :], start=(c == 0), stop=(c == KC - 1), skip_group_check=True)
            mm.then_inc(s_tab, 1)
            pe.wait_ge(s_tv, TV["CT"])
            for c in range(KC):
                pe.matmul(pbank[0:NF, 1, 480:488], CT[:, c, :], CT[:, c, :], start=(c == 0),
                          stop=(c == KC - 1), skip_group_check=True)
            for k, w in enumerate((Wq, Wk)):
                for m in range(KC):
                    out = pbank[0:96, 2, (k * KC + m) * NF:(k * KC + m + 1) * NF]
                    for c in range(KC):
                        pe.matmul(out, w[:, c, m * 96:(m + 1) * 96], CT[:, c, :], start=(c == 0),
                                  stop=False, skip_group_check=True)
                    pe.matmul(out, rows[0:1, k, m * 96:(m + 1) * 96], e7[0:1, :], start=False, stop=True,
                              skip_group_check=True)
            for k, (w, rel) in enumerate(((Wpk, relr), (Wpq, relf))):
                for m in range(KC):
                    out = pbank[0:96, 3 + 2 * k + m, 0:NR]
                    for c in range(KC):
                        pe.matmul(out, w[:, c, m * 96:(m + 1) * 96], rel[:, c, :], start=(c == 0),
                                  stop=False, skip_group_check=True)
                    mm = pe.matmul(out, rows[0:1, 3 + k, m * 96:(m + 1) * 96], ones[0:1, 0:NR], start=False,
                                   stop=True, skip_group_check=True)
            mm.then_inc(s_tab, 1)
            pe.wait_ge(s_tv, TV["blocks"])
            for k in range(2):
                for m in range(KC):
                    pe.matmul(pbank[0:48, 3 + 2 * k + m, 0:NR], WB[:, k, m].rearrange("p h f -> p (h f)"),
                              RT[:, k, m, :], start=True, stop=True, skip_group_check=True)
            for m in range(KC):
                for t in range(3):
                    out = pbank[0:NF, 0, 0:288].rearrange("p (h t f) -> p h t f", h=H, t=3)[
                        :, m * HC:(m + 1) * HC, t, :]
                    pe.matmul(out, WT[:, 0, m, :], KB[:, m, :, t, :], start=True, stop=(t == MID),
                              skip_group_check=True)
                    if t != MID:
                        pe.matmul(out, LQ[:, m, 0 if t == HI else 1, :], WB[:, 1, m], start=False, stop=True,
                                  skip_group_check=True)
            for c in range(KC):
                pe.matmul(pbank[0:NF, 1, 0:D], CT[:, c, :], Wv[:, c, :], start=(c == 0), stop=False,
                          skip_group_check=True)
            pe.matmul(pbank[0:NF, 1, 0:D], e7[0:1, :], rows[0:1, 2, :], start=False, stop=True,
                      skip_group_check=True).then_inc(s_tab, 1)

            pe.wait_ge(s_cir, 1)
            pe.wait_ge(s_tv, TV["gparts"])
            for b in range(B):
                if b >= 2:
                    pe.wait_ge(s_ete, b - 1)
                for k in range(IB):
                    mm = pe.transpose(pbank[0:NF, 4 + b % 2, k * P:(k + 1) * P], E[:, b * IB + k, :], ident[:])
                mm.then_inc(s_et, 1)
            for c in range(NT // 8):
                if c % (NT // 16) == 0:
                    pe.wait_ge(s_fw, c // (NT // 16) + 1)
                if c >= 2:
                    pe.wait_ge(s_fe[c % 2], c // 2)
                for k in range(8):
                    mm = pe.transpose(pbank[0:KF, 2 + c % 2, :].bitcast(BF16)[:, k * P:(k + 1) * P],
                                      FW[:, c * 8 + k].rearrange("p u k f -> p (u k f)"), identb[:])
                mm.then_inc(s_fx, 1)


def batches(engine, unroll, stages, count=B):
    lag = max(lag for lag, _ in stages)
    lead = -(-lag // unroll) * unroll

    def rounds(first, last, base):
        for r in range(first, last):
            for late, stage in stages:
                c = r - late
                if base is None and not 0 <= c < count:
                    continue
                if base is None:
                    stage(c, c % unroll, c // unroll)
                else:
                    stage(base * unroll + c, c % unroll, base + c // unroll)

    rounds(0, lead, None)
    with engine.Fori(0, (count - lead) // unroll) as base:
        rounds(lead, lead + unroll, base)
    rounds(count, count + lag, None)


def load_tables(sp, dram, keep, h):
    for u in range(2):
        for part, k0, n in ((0, 0, 3), (1, 3, 2), (2, 5, 1)):
            for k in range(k0, k0 + n):
                r0 = (u * NPR + k) * NF
                sp.dma_start(keep["TT"][r0:r0 + NF], dram["tabD"][bass.ds(h * NF, NF), part, :, 1 - u:513 - u]
                             ).then_inc(keep["s_tt"], 16)


def key_tables_block(nc, dram, keep):
    GB = 2
    UNITS = 2 * B // GB
    U = 4
    with ExitStack() as ctx:
        gps = ctx.enter_context(nc.psum_tensor("gps", [96, U, IB, GB * P], F32))
        parts = ctx.enter_context(nc.sbuf_tensor("gparts", [96, U, 3, IB, GB * P], BF16))
        rest = ctx.enter_context(nc.sbuf_tensor("grest", [96, U, IB, GB * P], F32))
        FX, GS = keep["FX"], keep["GS"]
        s_mm, s_hi, s_rest, s_mid = (ctx.enter_context(nc.semaphore(n)) for n in (
            "g_ready", "g_high", "g_rest", "g_middle"))
        s_low = [ctx.enter_context(nc.semaphore(n)) for n in ("g_low_by_vector", "g_low_by_gpsimd")]
        s_st = [ctx.enter_context(nc.semaphore(f"g_stored{k}")) for k in range(U)]
        s_go = ctx.enter_context(nc.semaphore("stores_begun"))
        block = ctx.enter_context(nc.Block())
        FOR_POOL = IB // 2

        @block.tensor
        def _(pe):
            def product(u, k, g):
                pe.wait_ge(s_rest, u + 1)
                for i in range(IB):
                    at = (0 if i < IB // 2 else 192) + 96 * (k % 2)
                    mm = pe.matmul(gps[:, k, i], GS[0:KF, at:at + 96],
                                   FX[0:KF, :].rearrange("k (b i p) -> k b i p", b=B, i=IB)[
                                       :, bass.ds(g * (U // 2 * GB) + k // 2 * GB, GB), i, :], start=True, stop=True)
                mm.then_inc(s_mm, 1)

            batches(pe, U, [(0, product)], UNITS)

        @block.scalar
        def _(act):
            def high(u, k, g):
                act.wait_ge(s_mm, u + 1)
                act.wait_ge(s_st[k], g * 48 + 48)
                act.activation(parts[:, k, 0], gps[:, k], ACT.Copy).then_inc(s_hi, 1)

            def middle(u, k, g):
                act.wait_ge(s_rest, u + (U + 1))
                act.activation(parts[:, k, 1], rest[:, k], ACT.Copy).then_inc(s_mid, 1)

            batches(act, U, [(0, high), (1, middle)], UNITS)

        @block.vector
        def _(dve):
            def subtract_high(u, k, g):
                dve.wait_ge(s_hi, u + 1)
                dve.wait_ge(s_low[1], u + 1)
                dve.tensor_tensor(rest[:, k], gps[:, k], parts[:, k, 0], ALU.subtract).then_inc(s_rest, 1)

            def low(u, k, g):
                dve.wait_ge(s_mid, u + 1)
                dve.tensor_tensor(parts[:, k, 2, FOR_POOL:], rest[:, k, FOR_POOL:], parts[:, k, 1, FOR_POOL:],
                                  ALU.subtract).then_inc(s_low[0], 1)

            dve.sem_inc(s_rest, U)
            batches(dve, U, [(0, subtract_high), (1, low)], UNITS)

        @block.gpsimd
        def _(pool):
            def low(u, k, g):
                pool.wait_ge(s_mid, u + 1)
                pool.tensor_tensor(parts[:, k, 2, 0:FOR_POOL], rest[:, k, 0:FOR_POOL], parts[:, k, 1, 0:FOR_POOL],
                                   ALU.subtract).then_inc(s_low[1], 1)

            pool.sem_inc(s_low[1], U)
            batches(pool, U, [(0, low)], UNITS)

        @block.sync
        def _(sp):
            def store(u, k, g):
                rows = dram["gD"].rearrange("s i h c t b p -> (h c t) s i (b p)")[(k % 2) * 96:(k % 2 + 1) * 96]
                for part in range(3):
                    if part < 2:
                        sp.wait_ge((s_hi, s_mid)[part], u + 1)
                    else:
                        sp.wait_ge(s_low[0], u + 1)
                        sp.sem_inc(s_go, 1)
                        sp.wait_ge(s_low[1], u + (U + 1))
                    sp.sem_inc(s_go, 1)
                    sp.dma_start(rows[:, part, :, bass.ds(g * (U // 2 * GB * P) + k // 2 * GB * P, GB * P)],
                                 parts[:, k, part]).then_inc(s_st[k], 16)

            load_tables(sp, dram, keep, 0)
            for k in range(U):
                sp.sem_inc(s_st[k], 48)
            batches(sp, U, [(0, store)], UNITS)
            sp.wait_ge(keep["s_tt"], 16 * 2 * NPR)
            for k in range(U):
                sp.wait_ge(s_st[k], 48 + 48 * UNITS // U)


def attention_block(nc, dram, keep):
    UB = B
    UH = IB * UB
    SB, XR, TB_, PR, OB = 3, 4, 2, 8, 2
    CH = [4 * len(beside(ib)) for ib in range(IB)]
    CHH = 1 + sum(CH)
    AHEAD = CH[0]
    VALUES = 5
    with ExitStack() as ctx:
        def sb(name, shape, dt=F32):
            return ctx.enter_context(nc.sbuf_tensor(name, shape, dt))

        ident, FX = keep["ident"], keep["FX"]
        WV = keep["GS"][0:KF, 384:576]
        TT, s_tt = keep["TT"], keep["s_tt"]
        gB = sb("gB", [KF, 2, 2, B * P], BF16)
        XP = sb("XP", [P, 2, 3, B, P])
        XQ = sb("XQ", [P, 2, XQ_LEN])
        Vh = sb("Vh", [P, NT, 2 * DH])
        X = sb("X", [P, XR, S])
        mx = sb("mx", [P, XR])
        PT = sb("PT", [P, PR, S])
        OT = sb("OT", [P, OB, P])
        sums, over, over_rest = (sb(n, [P, B * S // P]) for n in ("sums", "over", "over_rest"))
        over_parts = sb("over_parts", [P, 3, B * S // P], BF16)
        SC = ctx.enter_context(nc.psum_tensor("SC", [P, SB, S], F32))
        TU = ctx.enter_context(nc.psum_tensor("TU", [P, TB_, S], F32))
        BI = ctx.enter_context(nc.psum_tensor("BI", [P, 2, S], F32))
        OV = ctx.enter_context(nc.psum_tensor("OV", [P, S], F32))

        def sem(name):
            return ctx.enter_context(nc.semaphore(name))

        s_z = sem("zeros_ready")
        s_g = [sem("g_loaded_even"), sem("g_loaded_odd")]
        s_bias = [sem("key_bias_ready"), sem("query_bias_ready")]
        s_biased = [sem("key_bias_copied"), sem("query_bias_copied")]
        s_sc = sem("scores_ready")
        s_sum = sem("scores_summed")
        s_sh = sem("scores_shifted")
        s_tu = sem("scores_turned")
        s_ex = sem("exps_ready")
        s_pv = sem("values_summed")
        s_ov = sem("outputs_copied")
        s_go = sem("sums_begun")
        s_sm, s_inv, s_os = sem("softmax_sums_loaded"), sem("softmax_sums_inverted"), sem("inverses_stored")
        s_od = [sem(f"outputs_stored{i}") for i in range(OB)]

        block = ctx.enter_context(nc.Block())

        def bank(s):
            return s % SB if s < UH - 1 else 1

        def bank_free(s):
            before = next(v for v in range(s - 1, -UH, -1) if bank(v % UH) == bank(s))
            return max(before + 1 + SB, 1)

        def chunks(ib):
            return [(jb - ib + 1, jb, jq) for jb in beside(ib) for jq in range(4)]

        def chunk_base(ib):
            return 1 + sum(CH[1:ib]) if ib else 1 + sum(CH[1:])

        TURN, OUT = 3, 9
        LEAD = OUT + 4
        STEPS = UH + LEAD

        def heads(engine, step):
            for s in range(LEAD):
                step([(0, s)])
            with engine.Fori(0, H - 1) as h:
                for s in range(LEAD, STEPS):
                    step([(h, s)] if s < UH else [(h, s), (h + 1, s - UH)])
            for s in range(LEAD, STEPS):
                step([(H - 1, s)])

        def chunk_at(s):
            if s >= UH:
                return None
            ib = s // UB
            nxt = (ib + 1) % IB
            c = s % UB
            if c >= CH[nxt]:
                return None
            return nxt, c, chunk_base(nxt) + c - (1 if nxt == 1 and c < VALUES else 0)

        @block.sync
        def _(sp):
            def load_g(h, ib):
                for u in range(2):
                    for part, k0, n in ((0, 0, 3), (1, 3, 2), (2, 5, 1)):
                        r0 = (u * NPR + k0) * NF
                        sp.dma_start(gB[r0:r0 + n * NF, ib % 2].rearrange("r t n -> r (t n)"),
                                     dram["gD"][part, ib, h].rearrange("(a c) t b p -> a c (t b p)", a=1
                                     ).to_broadcast([n, NF, 2 * B * P])).then_inc(s_g[ib % 2], 16)

            def store(h, q):
                sp.wait_ge(s_ov, h * (UH // 4) + (q + 1 + OB))
                ib, b0 = q // 4, 4 * (q % 4)
                sp.dma_start(dram["otD"].rearrange("h r b n -> h b r n")[h, b0:b0 + 4, :, ib * P:(ib + 1) * P],
                             OT[:, q % OB, :]).then_inc(s_od[q % OB], 16)

            def head(h, last):
                for ib in range(IB):
                    if ib == 2:
                        for k in range(2):
                            sp.wait_ge(s_bias[k], h * CHH + (AHEAD + chunk_base(3) + CH[3]))
                        load_tables(sp, dram, keep, h + 1)
                    for q in range(4 * ib, 4 * ib + 4):
                        store(h, q)
                    if ib < 2 or not last:
                        sp.wait_ge(s_sc, h * UH + (ib + 1) * UB)
                        load_g(h + (ib + 2) // IB, (ib + 2) % IB)
                for i in range(OB):
                    sp.wait_ge(s_od[i], h * (16 * (UH // 4 // OB)) + 16 * (1 + UH // 4 // OB))
                sp.sem_inc(s_go, 1)
                sp.dma_start(sums[:], dram["otD"].rearrange("h r b n -> h r (b n)")[h, DH, :].rearrange(
                    "(p c) -> p c", p=P)).then_inc(s_sm, 16)
                sp.wait_ge(s_inv, h * 5 + 5)
                sp.sem_inc(s_go, 1)
                sp.dma_start(dram["overD"].rearrange("s h (p c) -> h p s c", p=P)[h], over_parts[:]
                             ).then_inc(s_os, 16)

            for i in range(OB):
                sp.sem_inc(s_od[i], 16)
            sp.sem_inc(s_os, 16)
            load_g(0, 0)
            load_g(0, 1)
            with sp.Fori(0, H - 1) as h:
                head(h, False)
            head(H - 1, True)
            sp.wait_ge(s_os, 16 + 16 * H)

        @block.gpsimd
        def _(pool):
            for k in range(2):
                pool.memset(XQ[:, k, 0:2 * P], 0.0).then_inc(s_z, 1)
                pool.memset(XQ[:, k, 2 * P:].rearrange("p (b n) -> p b n", b=B)[:, :, 3 * P:], 0.0).then_inc(s_z, 1)
            pool.memset(Vh[:, :, DH:], 1.0).then_inc(s_z, 1)
            with pool.Fori(0, H) as h:
                for s in range(UH):
                    pool.wait_ge(s_sum, h * UH + (s + 1 + SB))
                    pool.tensor_tensor(X[:, s % XR, :], X[:, s % XR, :],
                                       mx[:, s % XR:s % XR + 1].to_broadcast([P, S]),
                                       ALU.subtract).then_inc(s_sh, 1)

        def bias_out(kind, ib, c):
            rel, jb, jq = chunks(ib)[c]
            if kind == 0:
                return XP[:, ib % 2, rel, :, jq * 32:(jq + 1) * 32]
            o = 2 * P + rel * P + jq * 32
            return XQ[:, ib % 2, 2 * P:].rearrange("p (b n) -> p b n", b=B)[:, :, o - 2 * P:o - 2 * P + 32]

        @block.scalar
        def _(act):
            act.sem_inc(s_biased[0], 1)
            act.sem_inc(s_ex, TB_)
            act.sem_inc(s_ov, OB)

            def copy_bias(count, ib, c):
                act.wait_ge(s_bias[0], count + 1)
                act.activation(bias_out(0, ib, c), BI[:, 0, :].rearrange("p (b n) -> p b n", b=B),
                               ACT.Copy).then_inc(s_biased[0], 1)

            def step(at):
                for h, s in at:
                    if s == VALUES:
                        act.wait_ge(s_bias[0], h * CHH + (AHEAD + VALUES + 1))
                        act.wait_ge(s_pv, h * (UH // 4) + PR // 4)
                        act.activation(Vh[:, 0:NT // 2, 0:DH], BI[:, 0, :].rearrange("p (t d) -> p t d", d=DH),
                                       ACT.Copy).then_inc(s_biased[0], 1)
                    if chunk_at(s):
                        ib, c, n = chunk_at(s)
                        copy_bias(h * CHH + (AHEAD + n), ib, c)
                for h, s in at:
                    u = s - TURN
                    if 0 <= u < UH:
                        act.wait_ge(s_tu, h * UH + (u + 1 + XR))
                        act.wait_ge(s_pv, h * (UH // 4) + (u // 4 + 1))
                        act.activation(PT[:, u % PR, :], TU[:, u % TB_, :], ACT.Exp, scale=SCALE).then_inc(s_ex, 1)
                    if s >= OUT and (s - OUT) % 4 == 0 and (s - OUT) // 4 < UH // 4:
                        q = (s - OUT) // 4
                        act.wait_ge(s_pv, h * (UH // 4) + (q + 1 + PR // 4))
                        act.wait_ge(s_od[q % OB], (h * (UH // 4 // OB) + (q // OB + 1)) * 16)
                        act.activation(OT[:, q % OB, :], OV[:, 0:P], ACT.Copy).then_inc(s_ov, 1)

            for c in range(AHEAD):
                copy_bias(c, 0, c)
            heads(act, step)

        @block.vector
        def _(dve):
            dve.sem_inc(s_biased[1], 1)
            dve.sem_inc(s_sum, SB)
            dve.wait_ge(s_z, 5)

            def copy_bias(count, ib, c):
                dve.wait_ge(s_bias[1], count + 1)
                dve.tensor_copy(bias_out(1, ib, c),
                                BI[:, 1, :].rearrange("p (b n) -> p b n", b=B)).then_inc(s_biased[1], 1)

            for c in range(AHEAD):
                copy_bias(c, 0, c)
            def step(at):
                for h, s in at:
                    if s == VALUES:
                        dve.wait_ge(s_bias[1], h * CHH + (AHEAD + VALUES + 1))
                        dve.wait_ge(s_pv, h * (UH // 4) + PR // 4)
                        dve.tensor_copy(Vh[:, NT // 2:, 0:DH],
                                        BI[:, 1, :].rearrange("p (t d) -> p t d", d=DH)).then_inc(s_biased[1], 1)
                    if s == STEPS - 1:
                        dve.wait_ge(s_sm, h * 16 + 16)
                        dve.wait_ge(s_os, h * 16 + 16)
                        dve.reciprocal(over[:], sums[:]).then_inc(s_inv, 1)
                        dve.wait_ge(s_inv, h * 5 + 1)
                        dve.tensor_copy(over_parts[:, 0], over[:]).then_inc(s_inv, 1)
                        dve.wait_ge(s_inv, h * 5 + 2)
                        dve.tensor_tensor(over_rest[:], over[:], over_parts[:, 0], ALU.subtract).then_inc(s_inv, 1)
                        dve.wait_ge(s_inv, h * 5 + 3)
                        dve.tensor_copy(over_parts[:, 1], over_rest[:]).then_inc(s_inv, 1)
                        dve.wait_ge(s_inv, h * 5 + 4)
                        dve.tensor_tensor(over_parts[:, 2], over_rest[:], over_parts[:, 1],
                                          ALU.subtract).then_inc(s_inv, 1)
                    if s >= UH:
                        continue
                    ib, b = s // UB, s % UB
                    if b == 0:
                        n = 0 if ib == 0 else chunk_base(ib) + CH[ib]
                        dve.wait_ge(s_biased[1], h * CHH + (AHEAD + n + 1))
                        dve.wait_ge(s_sum, h * UH + (s + SB))
                    dve.wait_ge(s_sc, h * UH + (s + 1))
                    dve.wait_ge(s_tu, h * UH + (s + 1))
                    dve.sem_inc(s_go, 1)
                    o = XQ_PITCH * b + 3 * P - P * ib
                    dve.tensor_tensor_reduce(X[:, s % XR, :], SC[:, bank(s), :], XQ[:, ib % 2, o:o + S],
                                             1.0, -3.0e38, ALU.add, ALU.max,
                                             mx[:, s % XR:s % XR + 1]).then_inc(s_sum, 1)
                    if chunk_at(s):
                        nib, c, n = chunk_at(s)
                        copy_bias(h * CHH + (AHEAD + n), nib, c)

            heads(dve, step)

        @block.tensor
        def _(pe):
            pe.sem_inc(s_tu, XR)
            pe.sem_inc(s_pv, PR // 4)

            def bias(kind, count, ib, c):
                rel, jb, jq = chunks(ib)[c]
                pe.wait_ge(s_biased[kind], count + 1)
                out = BI[:, kind, :].rearrange("p (b n) -> p b n", b=B)
                own, other = (jb, ib) if kind == 0 else (ib, jb)
                for g in range(16):
                    at = other * P + jq * 32 + 2 * g
                    w = 256 - (at - own * P)
                    mm = pe.matmul(out[:, :, 2 * g:2 * g + 2], TT[:, kind, w:w + P],
                                   FX[0:KF, :].rearrange("k (b n) -> k b n", b=B)[:, :, at:at + 2],
                                   start=(g == 0), stop=(g == 15), skip_group_check=True)
                mm.then_inc(s_bias[kind], 1)

            def values(h):
                for half in range(2):
                    pe.wait_ge(s_biased[half], h * CHH + (AHEAD + VALUES + 1))
                    for t in range(NT // 2):
                        tile = half * NT // 2 + t
                        mm = pe.matmul(BI[:, half, t * DH:(t + 1) * DH], FX[0:KF, tile * P:(tile + 1) * P],
                                       WV[:, bass.ds(h * DH, DH)], start=(t == 0), stop=(t == NT // 2 - 1),
                                       skip_group_check=True)
                    mm.then_inc(s_bias[half], 1)

            def score(h, s):
                ib, b = s // UB, s % UB
                if b == 0:
                    n = 0 if ib == 0 else chunk_base(ib) + CH[ib]
                    pe.wait_ge(s_biased[0], h * CHH + (AHEAD + n + 1))
                    pe.wait_ge(s_g[ib % 2], (h * (IB // 2) + (ib // 2 + 1)) * (16 * 2 * 3))
                pe.wait_ge(s_sum, h * UH + bank_free(s))
                near = beside(ib)
                for i, jb in enumerate(near):
                    pe.matmul(SC[:, bank(s), jb * P:(jb + 1) * P], XP[:, ib % 2, jb - ib + 1, b, :], ident[:],
                              start=(i == 0), stop=False, is_transpose=True, skip_group_check=True)
                runs = [(HI, 0, near[0]), (LO, near[-1] + 1, IB), (MID, near[0], near[-1] + 1)]
                for t, j0, j1 in runs:
                    if j0 < j1:
                        slot = t - (MID if ib < IB // 2 else HI)
                        mm = pe.matmul(SC[:, bank(s), j0 * P:j1 * P], gB[:, ib % 2, slot, b * P:(b + 1) * P],
                                       FX[0:KF, b * S + j0 * P:b * S + j1 * P], start=False, stop=(t == MID),
                                       skip_group_check=True)
                mm.then_inc(s_sc, 1)

            def turn(h, u):
                pe.wait_ge(s_sh, h * UH + (u + 1))
                pe.wait_ge(s_ex, h * UH + (u + 1))
                for jb in range(IB):
                    mm = pe.transpose(TU[:, u % TB_, jb * P:(jb + 1) * P], X[:, u % XR, jb * P:(jb + 1) * P],
                                      ident[:])
                mm.then_inc(s_tu, 1)

            def sum_values(h, q):
                if q == 0:
                    for half in range(2):
                        pe.wait_ge(s_biased[half], h * CHH + (AHEAD + VALUES + 2))
                pe.wait_ge(s_ex, h * UH + (4 * q + 4 + TB_))
                pe.wait_ge(s_ov, h * (UH // 4) + (q + OB))
                for jb in range(IB):
                    for k in range(4):
                        u = 4 * q + k
                        mm = pe.matmul(OV[32 * k:32 * (k + 1), 0:P], Vh[:, (u % UB) * IB + jb, :],
                                       PT[:, u % PR, jb * P:(jb + 1) * P], start=(jb == 0), stop=(jb == IB - 1),
                                       skip_group_check=True)
                mm.then_inc(s_pv, 1)

            pe.wait_ge(s_tt, 16 * 2 * NPR)
            for c in range(AHEAD):
                for kind in range(2):
                    bias(kind, c, 0, c)
            def step(at):
                for h, s in at:
                    if s < UH:
                        score(h, s)
                    if s == 3 * UB:
                        pe.wait_ge(s_tt, (h + 2) * (16 * 2 * NPR))
                    if s == VALUES:
                        values(h)
                    if chunk_at(s):
                        ib, c, n = chunk_at(s)
                        bias(0, h * CHH + (AHEAD + n), ib, c)
                for h, s in at:
                    if TURN <= s < UH + TURN:
                        turn(h, s - TURN)
                for h, s in at:
                    if chunk_at(s):
                        ib, c, n = chunk_at(s)
                        bias(1, h * CHH + (AHEAD + n), ib, c)
                for h, s in at:
                    q = (s - OUT + 1) // 4
                    if (s - OUT + 1) % 4 == 0 and 0 <= q < UH // 4:
                        sum_values(h, q)

            heads(pe, step)


def residual_block(nc, dram, keep):
    H1, stats = keep["H1"], keep["stats"]
    U = 4
    with ExitStack() as ctx:
        def sb(name, shape, dt=F32):
            return ctx.enter_context(nc.sbuf_tensor(name, shape, dt))

        def sem(name):
            return ctx.enter_context(nc.semaphore(name))

        Wo = sb("Wo", [96 + NF, KC, D])
        O = sb("O", [96, KC, U, S])
        RP = sb("RP", [3 * H, B * S], BF16)
        sel32, sel = sb("sel32", [3 * H, KC, 96]), sb("sel", [3 * H, KC, 96], BF16)
        ON = sb("ON", [96 + NF, KC, U, S])
        bn, agg = sb("bn", [P, U, IB, 6]), sb("agg", [P, U, IB, 2])
        ph = ctx.enter_context(nc.psum_tensor("ph", [P, 2, 2, 512], F32))
        s_w, s_h = sem("out_weights"), sem("h1_ready")
        s_yz = sem("slot_outputs_zeroed")
        pR = ctx.enter_context(nc.psum_tensor("pR", [96, 2, KC, S], F32))
        s_on, s_sel, s_r = sem("heads_scaled"), sem("selection_ready"), sem("inverses_spread")
        s_wr = sem("inverses_loaded")
        s_in = [sem(f"heads_loaded{k}") for k in range(U // 2)]
        s_hc, s_bn, s_ag, s_st = sem("h1_copied"), sem("bn_ready"), sem("bn_done"), sem("stats_kept")
        s_go = sem("aggregates_begun")
        block = ctx.enter_context(nc.Block())
        NL = 16 * (KC + 1)

        @block.sync
        def _(sp):
            sp.dma_start(Wo[0:96], dram["Wo"].rearrange("(c k) n -> k c n", c=KC)).then_inc(s_w, 16)
            sp.dma_start(Wo[96:96 + NF, 1, :], dram["post_rows"]).then_inc(s_w, 16)
            sp.dma_start(sel32[:], dram["sel"]).then_inc(s_wr, 16)
            sp.dma_start(RP[:], dram["overD"].rearrange("s h n -> (s h) n")).then_inc(s_wr, 16)

            def load(b, k, g):
                if k % 2:
                    return
                sp.wait_ge(s_h, b + 2)
                for c in range(KC):
                    sp.dma_start(O[:, c, k:k + 2], dram["otD"][c * HC:(c + 1) * HC, 0:DH, bass.ds(b, 2), :]
                                 ).then_inc(s_in[k // 2], 16)
                sp.dma_start(ON[96:96 + NF, 1, k:k + 2], dram["evT"].rearrange("f (b n) -> f b n", b=B)[
                    :, bass.ds(b, 2)]).then_inc(s_in[k // 2], 16)

            batches(sp, U, [(0, load)])

        @block.gpsimd
        def _(pool):
            pool.memset(keep["YB"][:], 0.0).then_inc(s_yz, 1)
            pool.wait_ge(s_yz, 1)

        @block.vector
        def _(dve):
            def scale(b, k, g):
                dve.wait_ge(s_in[k // 2], g * NL + NL)
                dve.wait_ge(s_h, b + 1)
                dve.wait_ge(s_r, b + 1)
                dve.tensor_tensor(ON[0:96, :, k], O[:, :, k], pR[:, k % 2], ALU.mult).then_inc(s_on, 1)

            def spread(b, k, g):
                dve.wait_ge(s_hc, b + 3)
                dve.wait_ge(s_ag, b * IB + IB)
                for i in range(IB):
                    dve.bn_stats(bn[:, k, i], H1[:, bass.ds(b * IB + i, 1), :].rearrange("p a n -> p (a n)")
                                 ).then_inc(s_bn, 1)

            def aggregate(b, k, g):
                dve.wait_ge(s_bn, b * IB + IB)
                dve.wait_ge(s_st, b + 1)
                dve.sem_inc(s_go, 1)
                for i in range(IB):
                    dve.bn_aggr(agg[:, k, i], bn[:, k, i]).then_inc(s_ag, 1)

            def store(b, k, g):
                dve.wait_ge(s_ag, b * IB + (U + 1) * IB)
                dve.tensor_copy(stats[:, bass.ds(b * IB, IB), :], agg[:, k]).then_inc(s_st, 1)

            dve.wait_ge(s_wr, 32)
            dve.tensor_copy(sel[:], sel32[:]).then_inc(s_sel, 1)
            dve.sem_inc(s_on, 2)
            dve.sem_inc(s_st, U)
            dve.sem_inc(s_ag, U * IB)
            batches(dve, U, [(0, scale), (3, store), (2, aggregate), (1, spread)])

        @block.scalar
        def _(act):
            def copy(b, k, g):
                act.wait_ge(s_h, b + (U + 1))
                act.activation(H1[:, bass.ds(b * IB, IB), :].rearrange("p (a i) n -> p a i n", a=2),
                               ph[:, k % 2, :, 0:2 * D].rearrange("p a (i n) -> p a i n", i=2),
                               ACT.Copy).then_inc(s_hc, 1)

            act.sem_inc(s_hc, 2)
            batches(act, U, [(0, copy)])

        @block.tensor
        def _(pe):
            def project(b, k, g):
                pe.wait_ge(s_on, b + 3)
                pe.wait_ge(s_hc, b + 1)
                for i in range(IB):
                    out = ph[:, k % 2, i // 2, (i % 2) * D:(i % 2 + 1) * D]
                    pe.matmul(out, ON[0:96, 0, k, i * P:(i + 1) * P], Wo[0:96, 0, :], start=True, stop=False,
                              skip_group_check=True)
                    mm = pe.matmul(out, ON[:, 1, k, i * P:(i + 1) * P], Wo[:, 1, :], start=False, stop=True,
                                   skip_group_check=True)
                mm.then_inc(s_h, 1)

            def spread_inverses(b, k, g):
                pe.wait_ge(s_on, b + 1)
                for c in range(KC):
                    mm = pe.matmul(pR[:, k % 2, c], sel[:, c, :], RP[:, bass.ds(b * S, S)], start=True, stop=True)
                mm.then_inc(s_r, 1)

            pe.sem_inc(s_h, U)
            pe.wait_ge(s_w, 32)
            pe.wait_ge(s_sel, 1)
            batches(pe, U, [(0, spread_inverses), (1, project)])


def experts_block(nc, dram, keep):
    H1, stats, CTA, ident, XTL = keep["H1"], keep["stats"], keep["CTA"], keep["ident"], keep["XTL"]
    U = 4
    with ExitStack() as ctx:
        def sb(name, shape, dt=F32):
            return ctx.enter_context(nc.sbuf_tensor(name, shape, dt))

        def ps(name, shape):
            return ctx.enter_context(nc.psum_tensor(name, shape, F32))

        def sem(name):
            return ctx.enter_context(nc.semaphore(name))

        slot, sq, SP = sb("slot", [96, KC, NS]), sb("sq", [96, KC, NS]), sb("SP", [96, KC, NS])
        scale, nrm = sb("scale", [96, 1]), sb("nrm", [96, 5, KC, SLOT])
        tok = sb("tok", [P, 6, NT])
        XN = sb("XN", [P, U, IB, D])
        XT = sb("XT", [96, 2, KC, S])
        DT, DN = sb("DT", [NS, 2, S]), sb("DN", [NS, 2, S])
        dm = sb("dm", [NS, U, 4])
        DK = sb("DK", [P, 2, IB, NS])
        C0, C1, C2 = (sb(f"C{i}", [P, 2, IB, NS]) for i in range(3))
        cm = sb("cm", [P, U, 3, IB])
        pX = ps("pX", [96, KC, S])
        pL = ps("pL", [NS, 2, S])
        pC = ps("pC", [P, IB, NS])
        LS = sb("LS", [NS, 2, S])
        pD = ps("pD", [P, IB, NS])
        pT = ps("pT", [P, P])
        pS = ps("pS", [96, KC, NS])
        Wd, Wu, bd = (keep[k] for k in ("Wd", "Wu", "bd"))
        s_gp = sem("scalings_begun")
        s_ew = sem("expert_weights")
        s_dr, s_cs, s_cr = sem("dispatch_inverted"), sem("combine_summed"), sem("combine_inverted")
        s_w, s_sp, s_rt = sem("slots_loaded"), sem("slot_steps"), sem("roots")
        s_xn, s_xt = sem("x_normed"), sem("x_turned")
        s_xc = [sem("x_copied_by_scalar"), sem("x_copied_by_vector")]
        s_ls, s_lt = sem("logits_copied"), sem("logits_turned")
        s_lg, s_dm, s_cm = sem("logits"), sem("dispatch_steps"), sem("combine_steps")
        s_de, s_ce = sem("dispatch_exp"), sem("combine_exp")
        s_dn, s_cn = sem("dispatch_scaled"), sem("combine_scaled")
        s_tn, s_dk, s_cc = sem("both_turned"), sem("dispatch_copied"), sem("combine_copied")
        s_go = sem("turns_begun")
        s_s, s_sc = sem("slots_summed"), sem("slots_copied")
        block = ctx.enter_context(nc.Block())

        @block.sync
        def _(sp):
            sp.dma_start(slot[:], dram["slots"].rearrange("(c k) n -> k c n", c=KC)).then_inc(s_w, 16)
            sp.dma_start(scale[:], dram["scale"].to_broadcast([96, 1])).then_inc(s_w, 16)
            for c in range(KC):
                sp.dma_start(Wd[:, c], dram["Wd"].rearrange("e (c k) h -> c k e h", c=KC)[c]).then_inc(s_ew, 16)
            sp.dma_start(Wu[0:HF], dram["Wu"].rearrange("e h d -> h e d")).then_inc(s_ew, 16)
            with nc.allow_non_contiguous_dma(reason="192 biases"):
                sp.dma_start(bd[:], dram["bd"].rearrange("e h -> h e")).then_inc(s_ew, 16)
            sp.dma_start(Wu[HF:HF + 1], dram["bu"].rearrange("(a e) d -> a e d", a=1)).then_inc(s_ew, 16)
            sp.wait_ge(s_ew, 16 * (KC + 3))

        TVN = {}

        @block.vector
        def _(dve):
            n = [0]

            def st(ins):
                ins.then_inc(s_sp, 1)
                n[0] += 1
                dve.wait_ge(s_sp, n[0])

            st(dve.tensor_scalar(tok[:, 0], stats[:, :, 1], float(D), None, ALU.mult))
            st(dve.tensor_scalar(tok[:, 1], stats[:, :, 1], EPS_LN, None, ALU.add))
            TVN["var"] = n[0]
            dve.wait_ge(s_rt, 2)
            st(dve.tensor_scalar(tok[:, 4], tok[:, 3], EPS_L2, None, ALU.mult))
            st(dve.tensor_tensor(tok[:, 4], tok[:, 4], tok[:, 2], ALU.add))
            st(dve.reciprocal(tok[:, 5], tok[:, 4]))
            dve.wait_ge(s_w, 32)
            st(dve.tensor_tensor(sq[:], slot[:], slot[:], ALU.mult))
            st(dve.tensor_reduce(nrm[:, 0], sq[:].rearrange("k c (e s) -> k c s e", e=EXP), AX.X, ALU.add))
            TVN["sq"] = n[0]
            dve.wait_ge(s_rt, 3)
            st(dve.tensor_scalar(nrm[:, 2], nrm[:, 1], EPS_L2, None, ALU.add))
            st(dve.reciprocal(nrm[:, 3], nrm[:, 2]))
            st(dve.tensor_scalar(nrm[:, 4], nrm[:, 3], scale[:, 0:1], None, ALU.mult))
            for c in range(KC):
                st(dve.tensor_tensor(SP[:, c].rearrange("k (e s) -> k e s", e=EXP),
                                     slot[:, c].rearrange("k (e s) -> k e s", e=EXP),
                                     nrm[:, 4, c, None, :].to_broadcast([96, EXP, SLOT]), ALU.mult))
            TVN["SP"] = n[0]

            def copy_x(b, k, g):
                dve.wait_ge(s_xt, b + 1)
                dve.wait_ge(s_lg, b + 1)
                dve.tensor_copy(XT[:, k % 2, 1], pX[:, 1, :]).then_inc(s_xc[1], 1)

            def softmax(b, k, g):
                k2 = k % 2
                dve.wait_ge(s_ls, b + 3)
                dve.tensor_reduce(dm[:, k, 0:1], LS[:, k2], AX.X, ALU.max).then_inc(s_dm, 1)
                dve.wait_ge(s_dm, b * 2 + 1)
                dve.tensor_scalar(dm[:, k, 1:2], dm[:, k, 0:1], -1.0, None, ALU.mult).then_inc(s_dm, 1)
                dve.wait_ge(s_lt, b + 3)
                dve.tensor_reduce(cm[:, k, 0], pC[:], AX.X, ALU.max).then_inc(s_cm, 1)
                dve.wait_ge(s_cm, b * 2 + 3)
                dve.wait_ge(s_ce, b + 1)
                dve.tensor_tensor(C0[:, k2], pC[:], cm[:, k, 0, :, None].to_broadcast([P, IB, NS]),
                                  ALU.subtract).then_inc(s_cm, 1)

            def invert(b, k, g):
                dve.wait_ge(s_de, b + 3)
                dve.reciprocal(dm[:, k, 3:4], dm[:, k, 2:3]).then_inc(s_dr, 1)
                dve.wait_ge(s_ce, b + 3)
                dve.tensor_reduce(cm[:, k, 1], C1[:, k % 2], AX.X, ALU.add).then_inc(s_cs, 1)
                dve.wait_ge(s_cs, b + 1)
                dve.reciprocal(cm[:, k, 2], cm[:, k, 1]).then_inc(s_cr, 1)

            def copy_dispatch(b, k, g):
                dve.wait_ge(s_tn, b + 3)
                dve.wait_ge(s_s, b + U - 1)
                dve.tensor_copy(DK[:, k % 2], pD[:]).then_inc(s_dk, 1)

            def normalise(b, k, g):
                dve.wait_ge(s_s, b + 1)
                for i in range(IB):
                    t = bass.ds(b * IB + i, 1)
                    dve.tensor_scalar(XN[:, k, i], H1[:, t, :].rearrange("p a n -> p (a n)"),
                                      stats[:, t, 0:1].rearrange("p a n -> p (a n)"),
                                      tok[:, 5, t], ALU.subtract, ALU.mult).then_inc(s_xn, 1)

            dve.sem_inc(s_dk, 1)
            dve.sem_inc(s_cm, 2)
            dve.sem_inc(s_xc[1], 1)
            batches(dve, U, [(0, normalise), (2, invert), (3, copy_dispatch), (1, softmax), (0, copy_x)])

        @block.gpsimd
        def _(pool):
            def scale_both(b, k, g):
                k2 = k % 2
                pool.wait_ge(s_dr, b + 1)
                pool.wait_ge(s_tn, b + 1)
                pool.sem_inc(s_gp, 1)
                pool.tensor_scalar(DN[:, k2], DT[:, k2], dm[:, k, 3:4], None, ALU.mult).then_inc(s_dn, 1)
                pool.wait_ge(s_cr, b + 1)
                pool.tensor_tensor(C2[:, k2], C1[:, k2], cm[:, k, 2, :, None].to_broadcast([P, IB, NS]),
                                   ALU.mult).then_inc(s_cn, 1)

            pool.sem_inc(s_dn, 2)
            pool.sem_inc(s_cn, 2)
            batches(pool, U, [(2, scale_both)])

        @block.scalar
        def _(act):
            act.wait_ge(s_sp, TVN["var"])
            act.activation(tok[:, 2], tok[:, 0], ACT.Sqrt).then_inc(s_rt, 1)
            act.activation(tok[:, 3], tok[:, 1], ACT.Sqrt).then_inc(s_rt, 1)
            act.wait_ge(s_sp, TVN["sq"])
            act.activation(nrm[:, 1], nrm[:, 0], ACT.Sqrt).then_inc(s_rt, 1)

            def copy_x(b, k, g):
                act.wait_ge(s_xt, b + 1)
                act.wait_ge(s_lg, b + 1)
                act.activation(XT[:, k % 2, 0], pX[:, 0, :], ACT.Copy).then_inc(s_xc[0], 1)

            def copy_logits(b, k, g):
                act.wait_ge(s_lg, b + 3)
                act.wait_ge(s_lt, b + 1)
                act.activation(LS[:, k % 2], pL[:, k % 2], ACT.Copy).then_inc(s_ls, 1)

            def exps(b, k, g):
                act.wait_ge(s_dm, b * 2 + 2)
                act.wait_ge(s_dn, b + 1)
                act.activation(DT[:, k % 2], LS[:, k % 2], ACT.Exp, bias=dm[:, k, 1:2],
                               accum_out=dm[:, k, 2:3]).then_inc(s_de, 1)
                act.wait_ge(s_cm, b * 2 + 4)
                act.wait_ge(s_cn, b + 1)
                act.activation(C1[:, k % 2], C0[:, k % 2], ACT.Exp).then_inc(s_ce, 1)

            def copy_combine(b, k, g):
                act.wait_ge(s_tn, b + 3)
                act.activation(CTA[:, bass.ds(b * P, P)], pT[:], ACT.Copy).then_inc(s_cc, 1)

            def copy_slots(b, k, g):
                act.wait_ge(s_s, b + (U + 1))
                act.activation(XTL[:, :, bass.ds(b, 1), :],
                               pS[:].rearrange("p c (a n) -> p c a n", a=1), ACT.Copy).then_inc(s_sc, 1)

            act.sem_inc(s_ce, 2)
            act.sem_inc(s_de, 2)
            act.sem_inc(s_ls, 2)
            act.sem_inc(s_xc[0], 1)
            act.sem_inc(s_sc, 1)
            act.sem_inc(s_cc, 1)
            batches(act, U, [(4, copy_slots), (3, copy_combine), (1, copy_logits), (0, copy_x), (1, exps)])

        @block.tensor
        def _(pe):
            def turn_x(b, k, g):
                pe.wait_ge(s_xn, b * IB + IB)
                for half in range(2):
                    pe.wait_ge(s_xc[half], b + 1)
                for c in range(KC):
                    for i in range(IB):
                        mm = pe.transpose(pX[:, c, i * P:(i + 1) * P], XN[:, k, i, c * 96:(c + 1) * 96], ident[:])
                mm.then_inc(s_xt, 1)

            def logits(b, k, g):
                for half in range(2):
                    pe.wait_ge(s_xc[half], b + 2)
                pe.wait_ge(s_ls, b + 1)
                for c in range(KC):
                    mm = pe.matmul(pL[:, k % 2], SP[:, c, :], XT[:, k % 2, c, :], start=(c == 0), stop=(c == KC - 1))
                mm.then_inc(s_lg, 1)

            def turn_logits(b, k, g):
                pe.wait_ge(s_ls, b + 3)
                pe.wait_ge(s_cm, b * 2 + 2)
                pe.sem_inc(s_go, 1)
                for i in range(IB):
                    mm = pe.transpose(pC[:, i, :], LS[:, k % 2, i * P:(i + 1) * P], ident[0:NS, 0:NS])
                mm.then_inc(s_lt, 1)

            def sum_slots(b, k, g):
                pe.wait_ge(s_dk, b + 2)
                pe.wait_ge(s_sc, b + 1)
                for c in range(KC):
                    for i in range(IB):
                        mm = pe.matmul(pS[:, c, :], XN[:, k, i, c * 96:(c + 1) * 96], DK[:, k % 2, i, :],
                                       start=(i == 0), stop=(i == IB - 1), skip_group_check=True)
                mm.then_inc(s_s, 1)

            def turn_both(b, k, g):
                pe.wait_ge(s_dn, b + 3)
                pe.wait_ge(s_cn, b + 3)
                pe.wait_ge(s_dk, b + 1)
                pe.wait_ge(s_cc, b + 1)
                pe.sem_inc(s_go, 1)
                for i in range(IB):
                    pe.transpose(pD[:, i, :], DN[:, k % 2, i * P:(i + 1) * P], ident[0:NS, 0:NS])
                mm = pe.transpose(pT[:], C2[:, k % 2].rearrange("p i n -> p (i n)"), ident[:])
                mm.then_inc(s_tn, 1)

            pe.sem_inc(s_s, U)
            pe.sem_inc(s_lg, 2)
            pe.sem_inc(s_lt, 2)
            pe.sem_inc(s_tn, 2)
            pe.wait_ge(s_sp, TVN["SP"])
            batches(pe, U, [(3, turn_both), (1, logits), (0, turn_x), (1, turn_logits), (3, sum_slots)])


def mix_block(nc, dram, keep):
    H1, CTA, XTL = keep["H1"], keep["CTA"], keep["XTL"]
    U, YP = 4, 4
    with ExitStack() as ctx:
        def sb(name, shape, dt=F32):
            return ctx.enter_context(nc.sbuf_tensor(name, shape, dt))

        def sem(name):
            return ctx.enter_context(nc.semaphore(name))

        Wd, Wu, bd = (keep[k] for k in ("Wd", "Wu", "bd"))
        HG = sb("HG", [HF + 1, EXP, B * SLOT])
        YS = sb("YS", [B * SLOT, EXP, D])
        YB = keep["YB"]
        OUT = sb("OUT", [P, U, IB, D])
        pH = ctx.enter_context(nc.psum_tensor("pH", [P, 8, 512], F32))
        s_on, s_h, s_g, s_y, s_yc, s_yd = (sem(n) for n in (
            "ones_set", "hidden_ready", "gelu_done", "slot_out", "slot_out_copied",
            "slot_out_stored"))
        s_yb = [sem(f"slot_out_loaded{k}") for k in range(YP)]
        s_m, s_o = sem("mixed"), sem("outputs_ready")
        s_od = [sem(f"outputs_written{k}") for k in range(U)]
        block = ctx.enter_context(nc.Block())

        @block.sync
        def _(sp):
            sp.wait_ge(s_yc, EXP // 2)
            sp.dma_start(dram["yD"].rearrange("e p b d -> (p b) e d"), YS[:]).then_inc(s_yd, 16)
            sp.wait_ge(s_yd, 16)
            for part in range(YP):
                at = slice(part * B // YP, (part + 1) * B // YP)
                for i in range(IB):
                    sp.dma_start(YB[i * NS:(i + 1) * NS, i, at], dram["yD"].rearrange("e p b d -> (e p) b d")[:, at]
                                 ).then_inc(s_yb[part], 16)
            def store(b, k, g):
                sp.wait_ge(s_o, b + 1)
                sp.dma_start(dram["out"].rearrange("b (i p) d -> b p i d", p=P)[b], OUT[:, k]).then_inc(s_od[k], 16)

            for k in range(U):
                sp.sem_inc(s_od[k], 16)
            batches(sp, U, [(0, store)])
            for k in range(U):
                sp.wait_ge(s_od[k], 16 + 16 * B // U)

        @block.scalar
        def _(act):
            act.wait_ge(s_h, 1)
            act.wait_ge(s_on, 1)
            for e in range(EXP):
                ins = act.activation(HG[0:HF, e, :], pH[0:HF, 0, e * 64:(e + 1) * 64], ACT.Gelu, bias=bd[:, e:e + 1])
            ins.then_inc(s_g, 1)

        @block.vector
        def _(dve):
            dve.memset(HG[:], 1.0).then_inc(s_on, 1)
            for e in range(0, EXP, 2):
                dve.wait_ge(s_y, e // 2 + 1)
                dve.tensor_copy(YS[:, e:e + 2, :], pH[0:B * SLOT, 1 + e // 2, 0:2 * D].rearrange(
                    "p (e d) -> p e d", e=2)).then_inc(s_yc, 1)
            def add(b, k, g):
                dve.wait_ge(s_m, b + 1)
                dve.wait_ge(s_od[k], g * 16 + 16)
                dve.tensor_tensor(OUT[:, k].rearrange("p (a i) n -> p a i n", a=2),
                                  pH[:, 2 * k:2 * k + 2, 0:2 * D].rearrange("p a (i n) -> p a i n", i=2),
                                  H1[:, bass.ds(b * IB, IB), :].rearrange("p (a i) n -> p a i n", a=2),
                                  ALU.add).then_inc(s_o, 1)

            batches(dve, U, [(0, add)])

        @block.tensor
        def _(pe):
            for e in range(EXP):
                for c in range(KC):
                    mm = pe.matmul(pH[0:HF, 0, e * 64:(e + 1) * 64], Wd[:, c, e, :],
                                   XTL[:, c, :, e * SLOT:(e + 1) * SLOT].rearrange("k b p -> k p b"),
                                   start=(c == 0), stop=(c == KC - 1),
                                   skip_group_check=True)
            mm.then_inc(s_h, 1)
            pe.wait_ge(s_g, 1)
            for e in range(EXP):
                out = pH[0:B * SLOT, 1 + e // 2, (e % 2) * D:(e % 2 + 1) * D]
                mm = pe.matmul(out, HG[:, e, :], Wu[:, e, :], start=True, stop=True, skip_group_check=True)
                if e % 2:
                    mm.then_inc(s_y, 1)
            for b in range(B):
                if b % (B // YP) == 0:
                    pe.wait_ge(s_yb[b // (B // YP)], 16 * IB)
                if b >= U:
                    pe.wait_ge(s_o, b - U + 1)
                for i in range(IB):
                    mm = pe.matmul(pH[:, 2 * (b % U) + i // 2, (i % 2) * D:(i % 2 + 1) * D], CTA[:, b * P:(b + 1) * P],
                                   YB[:, i, b, :], start=True, stop=True, skip_group_check=True)
                mm.then_inc(s_m, 1)


def build(nc, dram):
    with ExitStack() as outer:
        def sb(name, shape, dt=F32):
            return outer.enter_context(nc.sbuf_tensor(name, shape, dt))

        keep = {"ident": sb("ident", [P, P])}
        with ExitStack() as ctx:
            keep["FX"] = ctx.enter_context(nc.sbuf_tensor("FX", [KF, T], BF16))
            keep["GS"] = ctx.enter_context(nc.sbuf_tensor("GS", [KF, GN], BF16))
            embed_block(nc, dram, keep)
            keep["TT"] = ctx.enter_context(nc.sbuf_tensor("TT", [KF, 2, 512], BF16))
            keep["s_tt"] = ctx.enter_context(nc.semaphore("tables_loaded"))
            key_tables_block(nc, dram, keep)
            attention_block(nc, dram, keep)
        keep["H1"] = sb("H1", [P, NT, D])
        keep["stats"] = sb("stats", [P, NT, 2])
        keep["YB"] = sb("YB", [P, IB, B, D])
        residual_block(nc, dram, keep)
        keep["CTA"] = sb("CTA", [P, B * P])
        keep["XTL"] = sb("XTL", [96, KC, B, NS])
        keep["Wd"], keep["Wu"] = sb("Wd", [96, KC, EXP, HF]), sb("Wu", [HF + 1, EXP, D])
        keep["bd"] = sb("bd", [HF, EXP])
        experts_block(nc, dram, keep)
        mix_block(nc, dram, keep)


def kernel(x, L0_tok_quantum_params, L0_tok_post_w, L0_tok_post_b, L0_attn_Wq, L0_attn_bq, L0_attn_Wk,
           L0_attn_bk, L0_attn_Wv, L0_attn_bv, L0_attn_rel_table, L0_attn_Wpk, L0_attn_bpk, L0_attn_Wpq,
           L0_attn_bpq, L0_attn_Wo, L0_attn_bo, L0_ffn_slot_params, L0_ffn_scale, L0_ffn_W_down,
           L0_ffn_b_down, L0_ffn_W_up, L0_ffn_b_up):
    import concourse.bacc as bacc
    from concourse.bass_utils import run_bass_kernel_spmd

    f4 = np.float32
    rel = np.asarray(L0_attn_rel_table).T
    post_w, post_b = np.asarray(L0_tok_post_w), np.asarray(L0_tok_post_b)
    arrays = {
        "ids": np.asarray(x).reshape(NT, P).T,
        "qparams": np.asarray(L0_tok_quantum_params).reshape(-1, NA),
        "Wq": L0_attn_Wq, "Wk": L0_attn_Wk, "Wv": L0_attn_Wv, "Wpk": L0_attn_Wpk, "Wpq": L0_attn_Wpq,
        "Wo": L0_attn_Wo,
        "post": np.concatenate([post_w, post_b[:, None], np.zeros((D, 1), f4)], axis=1),
        "post_rows": np.concatenate([post_w.T, post_b[None], np.asarray(L0_attn_bo)[None]]),
        "rel_back": rel[:, ::-1], "rel_fore": rel,
        "rows": np.stack([np.asarray(a) for a in (L0_attn_bq, L0_attn_bk, L0_attn_bv, L0_attn_bpk,
                                                  L0_attn_bpq)])[None],
        "slots": np.asarray(L0_ffn_slot_params).reshape(D, NS),
        "scale": np.asarray(L0_ffn_scale).reshape(1, 1),
        "Wd": L0_ffn_W_down, "bd": L0_ffn_b_down, "Wu": L0_ffn_W_up, "bu": L0_ffn_b_up,
        "ident": np.eye(P, dtype=f4),
        "centre": np.eye(D, dtype=f4) - f4(1 / D),
        "parity": (np.arange(P)[:, None] % 2 == np.arange(2)[None]).astype(f4),
        "hmask": (np.arange(96)[:, None] // DH == np.arange(HC)[None]).astype(f4),
        "e7": np.eye(NF, dtype=f4)[7:8],
        "sel": np.tile((np.arange(H)[:, None] == np.arange(D)[None] // DH).reshape(H, KC, 96), (3, 1, 1)).astype(f4),
    }
    arrays = {k: np.ascontiguousarray(v) for k, v in arrays.items()}
    nc = bacc.Bacc("TRN2", target_bir_lowering=False, num_devices=1)
    dram = {k: nc.dram_tensor(f"{k}_in", a.shape, mybir.dt.from_np(a.dtype), kind="ExternalInput").ap()
            for k, a in arrays.items()}
    dram["out"] = nc.dram_tensor("out_dram", (B, S, D), F32, kind="ExternalOutput").ap()
    scratch = {
        "tabD": ((H + 1) * NF, 3, 2, TAB, BF16),
        "evT": (NF, T, F32),
        "gmD": (NF, NF, F32),
        "gD": (3, IB, H, NF, 2, B, P, BF16),
        "otD": (H, 2 * DH, B, S, F32),
        "overD": (3, H, B * S, BF16),
        "yD": (EXP, SLOT, B, D, F32),
    }
    for k, (*shape, dt) in scratch.items():
        dram[k] = nc.dram_tensor(f"{k}_scratch", tuple(shape), dt).ap()
    build(nc, dram)
    r = run_bass_kernel_spmd(nc, [{f"{k}_in": a for k, a in arrays.items()}], core_ids=[0])
    return r.results[0]["out_dram"]
```
